# Optimizing a Trainium2 kernel written in Bass

```python
import numpy as np
import jax
import jax.numpy as jnp

def _softmax(x, axis=-1):
    return jax.nn.softmax(x, axis=axis)

def _gelu(x):
    return jax.nn.gelu(x, approximate=True)

def _silu(x):
    return jax.nn.silu(x)

def _sigmoid(x):
    return jax.nn.sigmoid(x)

def _layernorm(x, axis=-1, eps=1e-05):
    m = jnp.mean(x, axis=axis, keepdims=True)
    v = jnp.var(x, axis=axis, keepdims=True)
    return (x - m) / jnp.sqrt(v + eps)

def _scatter_add(tgt, idx, src, axis=0):
    return tgt.at[idx].add(src)

def _segment_sum(src, seg, n):
    return jax.ops.segment_sum(src, seg, n)
kernel_name = 'mk_conv_preact_d4_conv_nchw1024_r4_d78267'

def setup_inputs(seed: int=0):
    np.random.seed(seed)
    _w = jnp.asarray

    def _rec_inputs():
        import jax
        import jax.numpy as jnp
        _gk = jax.random.key(seed)
        x = 7.22e-05 + 1 * jax.random.normal(jax.random.fold_in(_gk, 1), (8, 256, 32, 32), jnp.float32)
        return x
    x = _rec_inputs()

    def _L0_conv_setup():
        import jax, jax.numpy as jnp
        import numpy as np
        from jax import lax
        C1 = 256
        C2 = 256
        D_STATE = 8
        HEADS = 2
        D_INNER = 256
        D_HEAD = D_INNER // HEADS

        def _mobius_perm(mobius, H, W):
            ys, xs = jnp.meshgrid(jnp.linspace(-1.0, 1.0, H), jnp.linspace(-1.0, 1.0, W), indexing='ij')
            z = (xs + 1j * ys).reshape(-1).astype(jnp.complex64)
            perms = []
            for h in range(mobius.shape[0]):
                a, b, c, d = (mobius[h, 0], mobius[h, 1], mobius[h, 2], mobius[h, 3])
                s = jnp.sqrt(jnp.clip(jnp.abs(a * d - b * c), 0.001))
                a, b, c, d = (a / s, b / s, c / s, d / s)
                w = (a * z + b) / (c * z + d + 1e-06)
                score = jnp.real(w) + 1.3 * jnp.imag(w)
                perms.append(jnp.argsort(score))
            return jnp.stack(perms, 0)

        def _gather_last(v, idx):
            return jnp.take_along_axis(v, jnp.broadcast_to(idx, v.shape[:-1] + (idx.shape[-1],)), axis=-1)

        def _selective_scan(x, dt, A, Bt, Ct, D):
            Bsz, Hh, Dh, N = x.shape
            S = A.shape[-1]
            dA = jnp.exp(dt[:, :, None, :] * A[None, :, :, None])
            dB = dt[:, :, None, :] * Bt

            def step(h, inp):
                dA_t, dB_t, x_t, C_t = inp
                h = dA_t[:, :, None, :] * h + dB_t[:, :, None, :] * x_t[..., None]
                y_t = jnp.einsum('bhds,bhs->bhd', h, C_t)
                return (h, y_t)
            h0 = jnp.zeros((Bsz, Hh, Dh, S), x.dtype)
            inputs = (jnp.moveaxis(dA, -1, 0), jnp.moveaxis(dB, -1, 0), jnp.moveaxis(x, -1, 0), jnp.moveaxis(Ct, -1, 0))
            _, ys = lax.scan(step, h0, inputs)
            return jnp.moveaxis(ys, 0, -1) + D[None, :, None, None] * x
        key = jax.random.key(seed)
        ks = jax.random.split(key, 8)
        S = D_STATE
        x = jax.random.normal(ks[0], (8, C1, 32, 32), jnp.float32)
        in_proj_w = jax.random.normal(ks[1], (3 * D_INNER, C1), jnp.float32) / np.sqrt(C1)
        in_proj_b = jnp.zeros((3 * D_INNER,), jnp.float32)
        dw_w = jax.random.normal(ks[2], (D_INNER, 1, 3), jnp.float32) / np.sqrt(3.0)
        dw_b = jnp.zeros((D_INNER,), jnp.float32)
        dbc_w = jax.random.normal(ks[3], (HEADS * (1 + 2 * S), D_INNER), jnp.float32) / np.sqrt(D_INNER)
        dbc_b = jnp.zeros((HEADS * (1 + 2 * S),), jnp.float32)
        A_log = jnp.log(jnp.tile(jnp.arange(1, S + 1, dtype=jnp.float32), (HEADS, 1)))
        Dparam = jnp.ones((HEADS,), jnp.float32)
        mobius = jnp.tile(jnp.array([[1.0, 0.0, 0.0, 1.0]], jnp.float32), (HEADS, 1)) + 0.05 * jax.random.normal(ks[4], (HEADS, 4), jnp.float32)
        out_proj_w = jax.random.normal(ks[5], (C2, D_INNER), jnp.float32) / np.sqrt(D_INNER)
        out_proj_b = jnp.zeros((C2,), jnp.float32)
        return dict(x=x, in_proj_w=in_proj_w, in_proj_b=in_proj_b, dw_w=dw_w, dw_b=dw_b, dbc_w=dbc_w, dbc_b=dbc_b, A_log=A_log, Dparam=Dparam, mobius=mobius, out_proj_w=out_proj_w, out_proj_b=out_proj_b)
    _L0_conv_all = _L0_conv_setup()
    _L0_conv_in = {k: v for k, v in _L0_conv_all.items() if k in ('in_proj_w', 'in_proj_b', 'dw_w', 'dw_b', 'dbc_w', 'dbc_b', 'A_log', 'Dparam', 'mobius', 'out_proj_w', 'out_proj_b')}
    del _L0_conv_all

    def _L1_conv_setup():
        import jax, jax.numpy as jnp
        import numpy as np
        B, C, H, W = (2, 256, 16, 16)
        E, TOP_K = (8, 2)
        FFN = C
        key = jax.random.key(seed)
        ks = jax.random.split(key, 5)
        s = 0.02
        return {'hidden_states': jax.random.normal(ks[0], (B, C, H, W), jnp.float32), 'gate_w': jax.random.normal(ks[1], (E, C), jnp.float32) * s, 'w1': jax.random.normal(ks[2], (E, FFN, C), jnp.float32) * s, 'w2': jax.random.normal(ks[3], (E, C, FFN), jnp.float32) * s, 'w3': jax.random.normal(ks[4], (E, FFN, C), jnp.float32) * s}
    _L1_conv_all = _L1_conv_setup()
    _L1_conv_in = {k: v for k, v in _L1_conv_all.items() if k in ('gate_w', 'w1', 'w2', 'w3')}
    del _L1_conv_all

    def _L2_conv_setup():
        import jax, jax.numpy as jnp
        import numpy as np
        from jax import lax
        EPS = 1e-05

        def _conv(x, w, pad):
            return lax.conv_general_dilated(x, w, (1, 1), [(pad, pad), (pad, pad)], dimension_numbers=('NCHW', 'OIHW', 'NCHW'))

        def _bn(x, g, b, m, v):
            inv = g * jax.lax.rsqrt(v + EPS)
            return x * inv[None, :, None, None] + (b - m * inv)[None, :, None, None]

        def _deform(x, ow, ob):
            B, C, H, W = x.shape
            off = _conv(x, ow, 1) + ob[None, :, None, None]
            off = off.reshape(B, C, 2, H, W)
            yy = jnp.arange(H, dtype=x.dtype)[:, None]
            xx = jnp.arange(W, dtype=x.dtype)[None, :]
            py = jnp.clip(yy + off[:, :, 0], 0.0, H - 1)
            px = jnp.clip(xx + off[:, :, 1], 0.0, W - 1)
            y0 = jnp.floor(py).astype(jnp.int32)
            x0 = jnp.floor(px).astype(jnp.int32)
            y1 = jnp.minimum(y0 + 1, H - 1)
            x1 = jnp.minimum(x0 + 1, W - 1)
            wy = py - y0.astype(x.dtype)
            wx = px - x0.astype(x.dtype)
            flat = x.reshape(B, C, H * W)

            def g(yi, xi):
                idx = (yi * W + xi).reshape(B, C, H * W)
                return jnp.take_along_axis(flat, idx, axis=2).reshape(B, C, H, W)
            v00, v01, v10, v11 = (g(y0, x0), g(y0, x1), g(y1, x0), g(y1, x1))
            return v00 * (1 - wy) * (1 - wx) + v01 * (1 - wy) * wx + v10 * wy * (1 - wx) + v11 * wy * wx
        key = jax.random.key(seed)
        ks = jax.random.split(key, 32)
        B, Cin, Cmid, H, W = (4, 256, 64, 16, 16)
        d = {}
        d['x'] = jax.random.normal(ks[0], (B, Cin, H, W), jnp.float32)
        d['ow1'] = jax.random.normal(ks[1], (2 * Cin, Cin, 3, 3), jnp.float32) * 0.01
        d['ob1'] = jnp.zeros((2 * Cin,), jnp.float32)
        d['ow2'] = jax.random.normal(ks[2], (2 * Cmid, Cmid, 3, 3), jnp.float32) * 0.01
        d['ob2'] = jnp.zeros((2 * Cmid,), jnp.float32)
        d['ow3'] = jax.random.normal(ks[3], (2 * Cmid, Cmid, 3, 3), jnp.float32) * 0.01
        d['ob3'] = jnp.zeros((2 * Cmid,), jnp.float32)
        d['w1'] = jax.random.normal(ks[4], (Cmid, Cin, 1, 1), jnp.float32) * (1.0 / np.sqrt(Cin))
        d['w2'] = jax.random.normal(ks[5], (Cmid, Cmid, 3, 3), jnp.float32) * (1.0 / np.sqrt(9 * Cmid))
        d['w3'] = jax.random.normal(ks[6], (Cin, Cmid, 1, 1), jnp.float32) * (1.0 / np.sqrt(Cmid))
        for i, c in zip((1, 2, 3), (Cmid, Cmid, Cin)):
            d[f'g{i}'] = jnp.ones((c,), jnp.float32)
            d[f'b{i}'] = jnp.zeros((c,), jnp.float32)
            d[f'm{i}'] = jax.random.normal(ks[10 + i], (c,), jnp.float32) * 0.1
            d[f'v{i}'] = jnp.ones((c,), jnp.float32) + jax.random.uniform(ks[20 + i], (c,), jnp.float32) * 0.1
        return d
    _L2_conv_all = _L2_conv_setup()
    _L2_conv_in = {k: v for k, v in _L2_conv_all.items() if k in ('ow1', 'ob1', 'w1', 'g1', 'b1', 'm1', 'v1', 'ow2', 'ob2', 'w2', 'g2', 'b2', 'm2', 'v2', 'ow3', 'ob3', 'w3', 'g3', 'b3', 'm3', 'v3')}
    del _L2_conv_all

    def _L3_conv_setup():
        import jax, jax.numpy as jnp
        import numpy as np
        key = jax.random.key(seed)
        k1, k2 = jax.random.split(key)
        B, C_in, H, W = (16, 256, 56, 56)
        C_out, unit = (256, 64)
        x = jax.random.normal(k1, (B, C_in, H, W), dtype=jnp.float32)
        stdv = 1.0 / np.sqrt(unit).astype(np.float32)
        weights = jax.random.uniform(k2, (C_out, unit), dtype=jnp.float32, minval=-stdv, maxval=stdv)
        return {'x': x, 'weights': weights, 'overlap': 32}
    _L3_conv_all = _L3_conv_setup()
    _L3_conv_in = {k: v for k, v in _L3_conv_all.items() if k in ('weights',)}
    del _L3_conv_all
    return {'x': x, 'L0_conv_in_proj_w': _L0_conv_in['in_proj_w'], 'L0_conv_in_proj_b': _L0_conv_in['in_proj_b'], 'L0_conv_dw_w': _L0_conv_in['dw_w'], 'L0_conv_dw_b': _L0_conv_in['dw_b'], 'L0_conv_dbc_w': _L0_conv_in['dbc_w'], 'L0_conv_dbc_b': _L0_conv_in['dbc_b'], 'L0_conv_A_log': _L0_conv_in['A_log'], 'L0_conv_Dparam': _L0_conv_in['Dparam'], 'L0_conv_mobius': _L0_conv_in['mobius'], 'L0_conv_out_proj_w': _L0_conv_in['out_proj_w'], 'L0_conv_out_proj_b': _L0_conv_in['out_proj_b'], 'L1_conv_gate_w': _L1_conv_in['gate_w'], 'L1_conv_w1': _L1_conv_in['w1'], 'L1_conv_w2': _L1_conv_in['w2'], 'L1_conv_w3': _L1_conv_in['w3'], 'L2_conv_ow1': _L2_conv_in['ow1'], 'L2_conv_ob1': _L2_conv_in['ob1'], 'L2_conv_w1': _L2_conv_in['w1'], 'L2_conv_g1': _L2_conv_in['g1'], 'L2_conv_b1': _L2_conv_in['b1'], 'L2_conv_m1': _L2_conv_in['m1'], 'L2_conv_v1': _L2_conv_in['v1'], 'L2_conv_ow2': _L2_conv_in['ow2'], 'L2_conv_ob2': _L2_conv_in['ob2'], 'L2_conv_w2': _L2_conv_in['w2'], 'L2_conv_g2': _L2_conv_in['g2'], 'L2_conv_b2': _L2_conv_in['b2'], 'L2_conv_m2': _L2_conv_in['m2'], 'L2_conv_v2': _L2_conv_in['v2'], 'L2_conv_ow3': _L2_conv_in['ow3'], 'L2_conv_ob3': _L2_conv_in['ob3'], 'L2_conv_w3': _L2_conv_in['w3'], 'L2_conv_g3': _L2_conv_in['g3'], 'L2_conv_b3': _L2_conv_in['b3'], 'L2_conv_m3': _L2_conv_in['m3'], 'L2_conv_v3': _L2_conv_in['v3'], 'L3_conv_weights': _L3_conv_in['weights']}

def reference(x, L0_conv_in_proj_w, L0_conv_in_proj_b, L0_conv_dw_w, L0_conv_dw_b, L0_conv_dbc_w, L0_conv_dbc_b, L0_conv_A_log, L0_conv_Dparam, L0_conv_mobius, L0_conv_out_proj_w, L0_conv_out_proj_b, L1_conv_gate_w, L1_conv_w1, L1_conv_w2, L1_conv_w3, L2_conv_ow1, L2_conv_ob1, L2_conv_w1, L2_conv_g1, L2_conv_b1, L2_conv_m1, L2_conv_v1, L2_conv_ow2, L2_conv_ob2, L2_conv_w2, L2_conv_g2, L2_conv_b2, L2_conv_m2, L2_conv_v2, L2_conv_ow3, L2_conv_ob3, L2_conv_w3, L2_conv_g3, L2_conv_b3, L2_conv_m3, L2_conv_v3, L3_conv_weights):
    import jax
    import jax.numpy as jnp

    def _L0_conv_ref(x, in_proj_w, in_proj_b, dw_w, dw_b, dbc_w, dbc_b, A_log, Dparam, mobius, out_proj_w, out_proj_b):
        import jax, jax.numpy as jnp
        import numpy as np
        from jax import lax
        C1 = 256
        C2 = 256
        D_STATE = 8
        HEADS = 2
        D_INNER = 256
        D_HEAD = D_INNER // HEADS

        def _mobius_perm(mobius, H, W):
            ys, xs = jnp.meshgrid(jnp.linspace(-1.0, 1.0, H), jnp.linspace(-1.0, 1.0, W), indexing='ij')
            z = (xs + 1j * ys).reshape(-1).astype(jnp.complex64)
            perms = []
            for h in range(mobius.shape[0]):
                a, b, c, d = (mobius[h, 0], mobius[h, 1], mobius[h, 2], mobius[h, 3])
                s = jnp.sqrt(jnp.clip(jnp.abs(a * d - b * c), 0.001))
                a, b, c, d = (a / s, b / s, c / s, d / s)
                w = (a * z + b) / (c * z + d + 1e-06)
                score = jnp.real(w) + 1.3 * jnp.imag(w)
                perms.append(jnp.argsort(score))
            return jnp.stack(perms, 0)

        def _gather_last(v, idx):
            return jnp.take_along_axis(v, jnp.broadcast_to(idx, v.shape[:-1] + (idx.shape[-1],)), axis=-1)

        def _selective_scan(x, dt, A, Bt, Ct, D):
            Bsz, Hh, Dh, N = x.shape
            S = A.shape[-1]
            dA = jnp.exp(dt[:, :, None, :] * A[None, :, :, None])
            dB = dt[:, :, None, :] * Bt

            def step(h, inp):
                dA_t, dB_t, x_t, C_t = inp
                h = dA_t[:, :, None, :] * h + dB_t[:, :, None, :] * x_t[..., None]
                y_t = jnp.einsum('bhds,bhs->bhd', h, C_t)
                return (h, y_t)
            h0 = jnp.zeros((Bsz, Hh, Dh, S), x.dtype)
            inputs = (jnp.moveaxis(dA, -1, 0), jnp.moveaxis(dB, -1, 0), jnp.moveaxis(x, -1, 0), jnp.moveaxis(Ct, -1, 0))
            _, ys = lax.scan(step, h0, inputs)
            return jnp.moveaxis(ys, 0, -1) + D[None, :, None, None] * x
        Bsz, _, H, W = x.shape
        N = H * W
        heads, S = A_log.shape
        d_inner = dw_w.shape[0]
        d_head = d_inner // heads
        xz = jax.nn.silu(jnp.einsum('oc,bchw->bohw', in_proj_w, x) + in_proj_b[None, :, None, None])
        x_ssm, res, gate = jnp.split(xz, 3, axis=1)
        xf = x_ssm.reshape(Bsz, d_inner, N)
        xf = lax.conv_general_dilated(xf, dw_w, (1,), [(1, 1)], dimension_numbers=('NCH', 'OIH', 'NCH'), feature_group_count=d_inner) + dw_b[None, :, None]
        xf = jax.nn.silu(xf)
        x_h = xf.reshape(Bsz, heads, d_head, N)
        perm = _mobius_perm(mobius, H, W)
        x_h = _gather_last(x_h, perm[None, :, None, :])
        dbc = (jnp.einsum('oc,bcn->bon', dbc_w, xf) + dbc_b[None, :, None]).reshape(Bsz, heads, 1 + 2 * S, N)
        dt = jax.nn.softplus(dbc[:, :, 0])
        B_t = dbc[:, :, 1:1 + S]
        C_t = dbc[:, :, 1 + S:]
        dt = _gather_last(dt, perm[None, :, :])
        B_t = _gather_last(B_t, perm[None, :, None, :])
        C_t = _gather_last(C_t, perm[None, :, None, :])
        A = -jnp.exp(A_log)
        y_h = _selective_scan(x_h, dt, A, B_t, C_t, Dparam)
        inv = jnp.argsort(perm, axis=-1)
        y_h = _gather_last(y_h, inv[None, :, None, :])
        y = y_h.reshape(Bsz, d_inner, H, W)
        y = y * jax.nn.silu(gate) + res
        return jax.nn.silu(jnp.einsum('oc,bchw->bohw', out_proj_w, y) + out_proj_b[None, :, None, None])

    def _L1_conv_ref(hidden_states, gate_w, w1, w2, w3):
        import jax, jax.numpy as jnp
        import numpy as np
        B, C, H, W = (2, 256, 16, 16)
        E, TOP_K = (8, 2)
        FFN = C
        b, c = (hidden_states.shape[0], hidden_states.shape[1])
        space = hidden_states.shape[2:]
        x = jnp.transpose(hidden_states, (0, 2, 3, 1)).reshape(-1, c)
        logits = x @ gate_w.T
        probs = jax.nn.softmax(logits.astype(jnp.float32), axis=-1)
        rw, sel = jax.lax.top_k(probs, TOP_K)
        rw = rw / jnp.sum(rw, axis=-1, keepdims=True)
        rw = rw.astype(x.dtype)
        combine = jnp.sum(jax.nn.one_hot(sel, E, dtype=x.dtype) * rw[..., None], axis=1)
        out = jnp.zeros_like(x)
        for e in range(E):
            h = jax.nn.gelu(x @ w1[e].T, approximate=False) * (x @ w3[e].T)
            out = out + combine[:, e:e + 1] * (h @ w2[e].T)
        out = out.reshape(b, *space, c)
        return jnp.transpose(out, (0, 3, 1, 2))

    def _L2_conv_ref(x, ow1, ob1, w1, g1, b1, m1, v1, ow2, ob2, w2, g2, b2, m2, v2, ow3, ob3, w3, g3, b3, m3, v3):
        import jax, jax.numpy as jnp
        import numpy as np
        from jax import lax
        EPS = 1e-05

        def _conv(x, w, pad):
            return lax.conv_general_dilated(x, w, (1, 1), [(pad, pad), (pad, pad)], dimension_numbers=('NCHW', 'OIHW', 'NCHW'))

        def _bn(x, g, b, m, v):
            inv = g * jax.lax.rsqrt(v + EPS)
            return x * inv[None, :, None, None] + (b - m * inv)[None, :, None, None]

        def _deform(x, ow, ob):
            B, C, H, W = x.shape
            off = _conv(x, ow, 1) + ob[None, :, None, None]
            off = off.reshape(B, C, 2, H, W)
            yy = jnp.arange(H, dtype=x.dtype)[:, None]
            xx = jnp.arange(W, dtype=x.dtype)[None, :]
            py = jnp.clip(yy + off[:, :, 0], 0.0, H - 1)
            px = jnp.clip(xx + off[:, :, 1], 0.0, W - 1)
            y0 = jnp.floor(py).astype(jnp.int32)
            x0 = jnp.floor(px).astype(jnp.int32)
            y1 = jnp.minimum(y0 + 1, H - 1)
            x1 = jnp.minimum(x0 + 1, W - 1)
            wy = py - y0.astype(x.dtype)
            wx = px - x0.astype(x.dtype)
            flat = x.reshape(B, C, H * W)

            def g(yi, xi):
                idx = (yi * W + xi).reshape(B, C, H * W)
                return jnp.take_along_axis(flat, idx, axis=2).reshape(B, C, H, W)
            v00, v01, v10, v11 = (g(y0, x0), g(y0, x1), g(y1, x0), g(y1, x1))
            return v00 * (1 - wy) * (1 - wx) + v01 * (1 - wy) * wx + v10 * wy * (1 - wx) + v11 * wy * wx
        h = _deform(x, ow1, ob1)
        h = _bn(_conv(h, w1, 0), g1, b1, m1, v1)
        h = _deform(h, ow2, ob2)
        h = _bn(_conv(h, w2, 1), g2, b2, m2, v2)
        h = _deform(h, ow3, ob3)
        h = _bn(_conv(h, w3, 0), g3, b3, m3, v3)
        return jax.nn.relu(h)

    def _L3_conv_ref(x, weights, overlap):
        import jax, jax.numpy as jnp
        import numpy as np
        C_out, unit = weights.shape
        C_in = x.shape[1]
        stride = unit - overlap
        o = jnp.arange(C_out)[:, None]
        j = jnp.arange(unit)[None, :]
        ch_idx = (o * stride + j) % C_in
        rows = jnp.broadcast_to(o, ch_idx.shape)
        W_full = jnp.zeros((C_out, C_in), dtype=weights.dtype)
        W_full = W_full.at[rows, ch_idx].add(weights)
        return jnp.einsum('oc,bchw->bohw', W_full, x)

    def _gn(v, G=32, eps=1e-05):
        B_, C_, H_, W_ = v.shape
        g = v.reshape(B_, G, C_ // G, H_, W_)
        m = jnp.mean(g, axis=(2, 3, 4), keepdims=True)
        s = jnp.var(g, axis=(2, 3, 4), keepdims=True)
        return ((g - m) / jnp.sqrt(s + eps)).reshape(v.shape)

    def _ln_c(v, eps=1e-06):
        m = jnp.mean(v, axis=1, keepdims=True)
        s = jnp.var(v, axis=1, keepdims=True)
        return (v - m) / jnp.sqrt(s + eps)

    def _ln_t(v, eps=1e-05):
        m = jnp.mean(v, axis=-1, keepdims=True)
        s = jnp.var(v, axis=-1, keepdims=True)
        return (v - m) / jnp.sqrt(s + eps)

    def _to_tokens(v):
        B_, C_, H_, W_ = v.shape
        return v.reshape(B_, C_, H_ * W_).transpose(0, 2, 1)

    def _from_tokens(t, like):
        B_, C_, H_, W_ = like.shape
        return t.transpose(0, 2, 1).reshape(B_, C_, H_, W_)
    x = x + _L0_conv_ref(_gn(x), L0_conv_in_proj_w, L0_conv_in_proj_b, L0_conv_dw_w, L0_conv_dw_b, L0_conv_dbc_w, L0_conv_dbc_b, L0_conv_A_log, L0_conv_Dparam, L0_conv_mobius, L0_conv_out_proj_w, L0_conv_out_proj_b)
    x = x + _L1_conv_ref(_gn(x), L1_conv_gate_w, L1_conv_w1, L1_conv_w2, L1_conv_w3)
    x = x + _L2_conv_ref(_gn(x), L2_conv_ow1, L2_conv_ob1, L2_conv_w1, L2_conv_g1, L2_conv_b1, L2_conv_m1, L2_conv_v1, L2_conv_ow2, L2_conv_ob2, L2_conv_w2, L2_conv_g2, L2_conv_b2, L2_conv_m2, L2_conv_v2, L2_conv_ow3, L2_conv_ob3, L2_conv_w3, L2_conv_g3, L2_conv_b3, L2_conv_m3, L2_conv_v3)
    x = x + _L3_conv_ref(_gn(x), L3_conv_weights, 32)
    return x

_drawn_inputs = setup_inputs


def setup_inputs(seed=0):
    import zlib

    import numpy as np

    out = dict(_drawn_inputs(seed))
    spreads = {'L0_conv_in_proj_b': (0.0, 0.1),
     'L0_conv_dw_b': (0.0, 0.414),
     'L0_conv_dbc_b': (0.0, 0.666),
     'L0_conv_Dparam': (1.0, 0.6),
     'L0_conv_out_proj_b': (0.0, 0.1),
     'L2_conv_ob1': (0.0, 0.8),
     'L2_conv_g1': (1.0, 0.6),
     'L2_conv_b1': (0.0, 0.8),
     'L2_conv_ob2': (0.0, 0.8),
     'L2_conv_g2': (1.0, 0.6),
     'L2_conv_b2': (0.0, 0.737),
     'L2_conv_ob3': (0.0, 0.8),
     'L2_conv_g3': (1.0, 0.6),
     'L2_conv_b3': (0.0, 0.1)}
    factors = {'L0_conv_A_log': 6.247,
     'L0_conv_mobius': 6.429,
     'L1_conv_gate_w': 5.221,
     'L1_conv_w1': 4.659,
     'L1_conv_w2': 4.518,
     'L1_conv_w3': 4.525,
     'L2_conv_v1': 64.0,
     'L2_conv_v2': 64.0,
     'L2_conv_v3': 64.0,
     'L2_conv_ow1': 8.0,
     'L2_conv_w1': 6.389,
     'L2_conv_m1': 8.0,
     'L2_conv_ow2': 8.0,
     'L2_conv_w2': 5.921,
     'L2_conv_m2': 8.0,
     'L2_conv_ow3': 8.0,
     'L2_conv_w3': 3.943,
     'L2_conv_m3': 4.411}
    for name, (base, spread) in spreads.items():
        noise = np.random.default_rng([zlib.crc32(name.encode()), seed]).standard_normal(out[name].shape)
        drawn = base * np.exp(spread * noise) if base else spread * noise
        out[name] = jnp.asarray(drawn.astype(out[name].dtype))
    for name, factor in factors.items():
        out[name] = (out[name] * factor).astype(out[name].dtype)
    return out
```

```python
from contextlib import ExitStack

import concourse.bass as bass
from concourse import mybir

F32 = mybir.dt.float32
BF16 = mybir.dt.bfloat16
ALU = mybir.AluOpType
ACT = mybir.ActivationFunctionType
AX = mybir.AxisListType.X

P = 128
B = 8
C = 256
KC = C // P
SIDE = 32
N = SIDE * SIDE
NT = N // P
HALF = 512
NH = N // HALF
PAD = SIDE + 2
HEADS = 2
S = 8
ROWS = 3 * S
DBC = 1 + 2 * S
E = 8
CM = 64
BLK = 32
NG = BLK // 4
UNITS = 4
GN_EPS = 1e-5
BN_EPS = 1e-5


class Stage:

    def __init__(self, nc, ctx, tag):
        self.nc, self.ctx, self.tag, self.sems = nc, ctx, tag, {}

    def sb(self, name, shape, dt=F32):
        return self.ctx.enter_context(self.nc.sbuf_tensor(f"{self.tag}_{name}", shape, dt))

    def sem(self, name):
        if name not in self.sems:
            self.sems[name] = self.ctx.enter_context(self.nc.semaphore(f"{self.tag}_{name}"))
        return self.sems[name]

    def clear(self):
        for s in self.sems.values():
            self.nc.gpsimd.sem_clear(s)
        self.nc.all_engine_barrier()


class Chain:

    def __init__(self, eng, sem):
        self.eng, self.sem, self.n = eng, sem, 0

    def __call__(self, ins):
        self.n += 1
        ins.then_inc(self.sem, 1)
        self.eng.wait_ge(self.sem, self.n)



def norm_stats_vector(nc, dve, st, link, x, stats, moments, psum):
    for k in range(KC):
        for h in range(NH):
            ins = nc.vector.bn_stats(stats[:, k, 6 * h:6 * h + 6], x[:, k, h * HALF:(h + 1) * HALF])
        link(ins)
    for k in range(KC):
        link(nc.vector.bn_aggr(moments[:, k, 0:2], stats[:, k, :]))
    nc.vector.tensor_copy(moments[:, 0:KC, 2], moments[:, 0:KC, 0]).then_inc(st.sem("means_ready"), 1)
    dve.wait_ge(st.sem("group_means"), 1)
    link(nc.vector.tensor_copy(moments[:, 0:KC, 3], psum[:, 0:KC]))
    link(nc.vector.tensor_tensor(moments[:, 0:KC, 4], moments[:, 0:KC, 0], moments[:, 0:KC, 3], ALU.subtract))
    link(nc.vector.tensor_tensor(moments[:, 0:KC, 4], moments[:, 0:KC, 4], moments[:, 0:KC, 4], ALU.mult))
    nc.vector.tensor_tensor(moments[:, 0:KC, 5], moments[:, 0:KC, 4], moments[:, 0:KC, 1],
                            ALU.add).then_inc(st.sem("spread_ready"), 1)
    dve.wait_ge(st.sem("group_vars"), 1)
    nc.vector.tensor_scalar(moments[:, 0:KC, 6], psum[:, 8:8 + KC], GN_EPS, None,
                            ALU.add).then_inc(st.sem("var_eps"), 1)
    dve.wait_ge(st.sem("rstd"), 1)


def norm_stats_tensor(nc, pe, st, moments, average, psum):
    pe.wait_ge(st.sem("means_ready"), 1)
    nc.tensor.matmul(psum[:, 0:KC], average[:, :], moments[:, 0:KC, 2], start=True,
                     stop=True).then_inc(st.sem("group_means"), 1)
    pe.wait_ge(st.sem("spread_ready"), 1)
    nc.tensor.matmul(psum[:, 8:8 + KC], average[:, :], moments[:, 0:KC, 5], start=True,
                     stop=True).then_inc(st.sem("group_vars"), 1)


def norm_stats_pool(nc, pool, st, moments, minus_half):
    pool.wait_ge(st.sem("var_eps"), 1)
    nc.gpsimd.tensor_tensor(moments[:, 0:KC, 7], moments[:, 0:KC, 6], minus_half[:, 0:KC],
                            ALU.pow).then_inc(st.sem("rstd"), 1)


def normalise(nc, out, x, moments, k):
    return nc.vector.tensor_scalar(out, x, moments[:, k, 3:4], moments[:, k, 7:8], ALU.subtract, ALU.mult)


def split_vector(nc, link, parts, full, rest):
    link(nc.vector.tensor_copy(parts[0], full))
    link(nc.vector.tensor_tensor(rest, full, parts[0], ALU.subtract))
    link(nc.vector.tensor_copy(parts[1], rest))
    return nc.vector.tensor_tensor(parts[2], rest, parts[1], ALU.subtract)


def image(ap, b):
    return ap[bass.ds(b, 1), :, :].rearrange("a (k p) n -> (a p) k n", p=P)


def build_scan_layer(nc, t, ps, xcur):
    with ExitStack() as ctx:
        st = Stage(nc, ctx, "l0")
        sem = st.sem
        sel = st.sb("sel", [3 * ROWS, ROWS, P], BF16)
        forward = st.sb("forward", [P, HEADS, NT, N], BF16)
        backward = st.sb("backward", [P, HEADS, NT, N], BF16)
        average = st.sb("average", [P, P])
        ident = st.sb("ident", [P, P])
        minus_half = st.sb("minus_half", [P, 4])
        in_w = st.sb("in_w", [P, KC, 3 * C])
        out_w = st.sb("out_w", [P, KC, C])
        dbc_w = st.sb("dbc_w", [P, KC, HEADS * DBC])
        in_b = st.sb("in_b", [P, 6])
        out_b = st.sb("out_b", [P, KC])
        dw_w = st.sb("dw_w", [P, KC, 3])
        dw_b = st.sb("dw_b", [P, KC])
        dbc_b = st.sb("dbc_b", [P, HEADS * DBC])
        decay = st.sb("decay", [P, HEADS, S])
        skip = st.sb("skip", [P, HEADS])

        with ExitStack() as own:
            so = Stage(nc, own, "order")
            zx = so.sb("zx", [P, N + NT])
            zy = so.sb("zy", [P, N + NT])
            token = so.sb("token", [P, N + NT])
            below = so.sb("below", [P, P])
            ones = so.sb("ones", [P, P])
            mob = so.sb("mob", [P, HEADS * 4])
            sc = so.sb("sc", [P, HEADS, 8])
            w = [so.sb(f"w{i}", [P, N + NT]) for i in range(7)]
            score = so.sb("score", [P, N + NT])
            junk = so.sb("junk", [P, N])
            counts = so.sb("counts", [P, NT, 4])
            rank = so.sb("rank", [P, NT])
            diag = so.sb("diag", [P, NT, P])
            loaded, chain = so.sem("loaded"), so.sem("chain")
            loads = [
                (zx, t["grid_x"].partition_broadcast(P)), (zy, t["grid_y"].partition_broadcast(P)),
                (token, t["grid_token"].partition_broadcast(P)),
                (mob, t["L0_conv_mobius"].rearrange("h m -> (h m)").partition_broadcast(P)),
            ]
            cols = [(zx, "col_x"), (zy, "col_y"), (token, "col_token")]
            rest = [
                (below[:, :], t["below"]), (average[:, :], t["average"]), (ident[:, :], t["ident"]),
                (sel[:, :, :], t["sel_rows"].bitcast(BF16)),
                (in_w[:, :, :], t["in_w"].rearrange("(k p) o -> p k o", p=P)),
                (out_w[:, :, :], t["out_w"].rearrange("(k p) o -> p k o", p=P)),
                (dbc_w[:, :, :], t["dbc_w"].rearrange("(k p) o -> p k o", p=P)),
                (in_b[:, :], t["in_b"]),
                (out_b[:, :], t["out_b"]),
                (dw_w[:, :, :], t["L0_conv_dw_w"].rearrange("(k p) a w -> p k (a w)", p=P)),
                (dw_b[:, :], t["dw_b"]),
                (dbc_b[:, :], t["L0_conv_dbc_b"].partition_broadcast(P)),
                (decay[:, :, :], t["L0_conv_A_log"].rearrange("h s -> (h s)").partition_broadcast(P).rearrange("p (h s) -> p h s", h=HEADS)),
                (skip[:, :], t["L0_conv_Dparam"].partition_broadcast(P)),
            ]
            with nc.Block() as block:
                n_loads = len(loads) + len(cols) + len(rest)

                @block.sync
                def _(sp):
                    for dst, src in loads:
                        sp.dma_start(dst[:, 0:src.shape[-1]], src).then_inc(loaded, 16)
                    for dst, name in cols:
                        sp.dma_start(dst[:, N:N + NT], t[name]).then_inc(loaded, 16)
                    for dst, src in rest:
                        sp.dma_start(dst, src).then_inc(loaded, 16)
                    sp.wait_ge(loaded, 16 * n_loads)

                @block.scalar
                def _(act):
                    act.wait_ge(loaded, 16 * n_loads)
                    nc.scalar.activation(decay[:, :, :], decay[:, :, :], ACT.Exp).then_inc(so.sem("decay_exp"), 1)

                @block.gpsimd
                def _(pool):
                    nc.gpsimd.memset(minus_half[:, :], -0.5).then_inc(so.sem("const"), 1)
                    nc.gpsimd.memset(ones[:, :], 1.0).then_inc(so.sem("const"), 1)
                    nc.gpsimd.memset(sc[:, :, 5], 0.5).then_inc(so.sem("const"), 1)
                    pool.wait_ge(so.sem("const"), 3)
                    pool.wait_ge(so.sem("det"), 1)
                    nc.gpsimd.tensor_tensor(sc[:, :, 4], sc[:, :, 4], sc[:, :, 5], ALU.pow).then_inc(so.sem("root"), 1)

                @block.vector
                def _(dve):
                    link = Chain(dve, chain)
                    tt, ts, stt = nc.vector.tensor_tensor, nc.vector.tensor_scalar, nc.vector.scalar_tensor_tensor
                    dve.wait_ge(so.sem("const"), 3)
                    dve.wait_ge(loaded, 16 * n_loads)
                    m = mob[:, :].rearrange("p (h m) -> p h m", h=HEADS)
                    link(tt(sc[:, :, 0], m[:, :, 0], m[:, :, 3], ALU.mult))
                    link(tt(sc[:, :, 1], m[:, :, 1], m[:, :, 2], ALU.mult))
                    link(tt(sc[:, :, 4], sc[:, :, 0], sc[:, :, 1], ALU.subtract))
                    link(stt(sc[:, :, 4], sc[:, :, 4], -1.0, sc[:, :, 4], ALU.mult, ALU.max))
                    ts(sc[:, :, 4], sc[:, :, 4], 0.001, None, ALU.max).then_inc(so.sem("det"), 1)
                    dve.wait_ge(so.sem("root"), 1)
                    link(nc.vector.reciprocal(sc[:, :, 6], sc[:, :, 4]))
                    for j in range(4):
                        link(tt(sc[:, :, j], m[:, :, j], sc[:, :, 6], ALU.mult))
                    link(ts(sc[:, :, 3], sc[:, :, 3], 1e-6, None, ALU.add))
                    for h in range(HEADS):
                        a, b, c, d = (sc[:, h, j:j + 1] for j in range(4))
                        nr, ni, dr, di, u, v, den = (x[:, :] for x in w)
                        link(ts(nr, zx[:, :], a, b, ALU.mult, ALU.add))
                        link(ts(ni, zy[:, :], a, None, ALU.mult))
                        link(ts(dr, zx[:, :], c, d, ALU.mult, ALU.add))
                        link(ts(di, zy[:, :], c, None, ALU.mult))
                        link(tt(den, dr, dr, ALU.mult))
                        link(tt(u, di, di, ALU.mult))
                        link(tt(den, den, u, ALU.add))
                        link(nc.vector.reciprocal(den, den))
                        link(tt(u, nr, dr, ALU.mult))
                        link(tt(v, ni, di, ALU.mult))
                        link(tt(u, u, v, ALU.add))
                        link(tt(u, u, den, ALU.mult))
                        link(tt(v, ni, dr, ALU.mult))
                        link(tt(nr, nr, di, ALU.mult))
                        link(tt(v, v, nr, ALU.subtract))
                        link(tt(v, v, den, ALU.mult))
                        link(stt(score[:, :], v, 1.3, u, ALU.mult, ALU.add))
                        link(nc.vector.memset(counts[:, :, :], 0.0))
                        for c_ in range(NT):
                            mine = score[:, N + c_:N + c_ + 1]
                            lo, hi = c_ * P, (c_ + 1) * P
                            if c_:
                                link(ts(junk[:, 0:lo], score[:, 0:lo], mine, None, ALU.is_le, ALU.add,
                                        accum_out=counts[:, c_, 0:1]))
                            link(ts(junk[:, lo:N], score[:, lo:N], mine, None, ALU.is_lt, ALU.add,
                                    accum_out=counts[:, c_, 1:2]))
                            link(stt(junk[:, 0:P], score[:, lo:hi], mine, below[:, :], ALU.is_equal, ALU.mult))
                            link(nc.vector.tensor_reduce(counts[:, c_, 2:3], junk[:, 0:P], AX, ALU.add))
                        link(nc.vector.tensor_reduce(rank[:, :], counts[:, :, :], AX, ALU.add))
                        if h:
                            dve.wait_ge(so.sem("ranks_used"), h)
                        for c_ in range(NT):
                            link(ts(forward[:, h, c_, :], token[:, 0:N], rank[:, c_:c_ + 1], None, ALU.is_equal))
                            last = ts(diag[:, c_, :], ident[:, :], rank[:, c_:c_ + 1], None, ALU.mult)
                            link(last)
                        nc.vector.memset(junk[:, 0:1], 0.0).then_inc(so.sem("diag_ready"), 1)
                        dve.wait_ge(so.sem("ranks_used"), h + 1)
                        for c_ in range(NT):
                            link(ts(backward[:, h, c_, :], ps[:, 0:N], token[:, N + c_:N + c_ + 1], None, ALU.is_equal))
                    dve.wait_ge(so.sem("decay_exp"), 1)
                    link(ts(decay[:, :, :], decay[:, :, :], -1.0, None, ALU.mult))

                @block.tensor
                def _(pe):
                    pe.wait_ge(so.sem("const"), 3)
                    for h in range(HEADS):
                        pe.wait_ge(so.sem("diag_ready"), h + 1)
                        for c_ in range(NT):
                            ins = nc.tensor.matmul(ps[:, c_ * P:(c_ + 1) * P], ones[:, :], diag[:, c_, :],
                                                   start=True, stop=True)
                        ins.then_inc(so.sem("ranks_used"), 1)
            so.clear()

        x = st.sb("x", [P, KC, N])
        xn = st.sb("xn", [P, KC, N])
        stats = st.sb("stats", [P, KC, 6 * NH])
        moments = st.sb("moments", [P, KC, 8])
        ssm = st.sb("ssm", [P, KC, N + 2])
        res = st.sb("res", [P, KC, N])
        gate = st.sb("gate", [P, KC, N])
        xf = st.sb("xf", [P, KC, N])
        dbc = st.sb("dbc", [P, NT, HEADS, DBC])
        sp_t = st.sb("sp_t", [P, 6, NT, HEADS])
        rows = st.sb("rows", [P, NT, HEADS, ROWS])
        rows_rest = st.sb("rows_rest", [P, NT, HEADS, ROWS])
        rows3 = st.sb("rows3", [P, NT, HEADS, 3, ROWS], BF16)
        rows_p = st.sb("rows_p", [3 * ROWS, HEADS, N], BF16)
        xt3 = st.sb("xt3", [P, HEADS, 3, N], BF16)
        xp = st.sb("xp", [P, HEADS, N])
        dbx = st.sb("dbx", [P, 2, N])
        states = st.sb("states", [P, 2, N])
        seen = st.sb("seen", [P, 2, N])
        acc = st.sb("acc", [P, HEADS, N])
        rest_x = seen[:, 0, :]

        with nc.Fori(0, B) as b:
            with nc.Block() as block:

                @block.sync
                def _(sp):
                    sp.dma_start(x[:, :, :], image(t["x"], b)).then_inc(sem("x_loaded"), 16)
                    sp.wait_ge(sem("new_x"), KC)
                    sp.dma_start(image(xcur, b), x[:, :, :]).then_inc(sem("stored"), 16)
                    sp.wait_ge(sem("stored"), 16)

                @block.gpsimd
                def _(pool):
                    nc.gpsimd.memset(ssm[:, :, 0:1], 0.0).then_inc(sem("border"), 1)
                    nc.gpsimd.memset(ssm[:, :, N + 1:N + 2], 0.0).then_inc(sem("border"), 1)
                    norm_stats_pool(nc, pool, st, moments, minus_half)
                    for i in range(HEADS * S):
                        h, s = divmod(i, S)
                        pool.wait_ge(sem("seen_ready"), i + 1)
                        if s == 0:
                            ins = nc.gpsimd.tensor_copy(acc[:, h, :], seen[:, i % 2, :])
                        else:
                            pool.wait_ge(sem("summed"), i)
                            ins = nc.gpsimd.tensor_tensor(acc[:, h, :], acc[:, h, :], seen[:, i % 2, :], ALU.add)
                        ins.then_inc(sem("summed"), 1)

                @block.scalar
                def _(act):
                    link = Chain(act, sem("act_chain"))
                    parts = [ssm[:, 0, 1:N + 1], ssm[:, 1, 1:N + 1], res[:, 0, :], res[:, 1, :], gate[:, 0, :], gate[:, 1, :]]
                    for m in range(6):
                        act.wait_ge(sem("projected"), m + 1)
                        lo = (m % 2) * N
                        nc.scalar.activation(parts[m], ps[:, lo:lo + N], ACT.Silu,
                                             bias=in_b[:, m:m + 1]).then_inc(sem("part_ready"), 1)
                        if m in (2, 3):
                            k = m - 2
                            act.wait_ge(sem("conv_ready"), k + 1)
                            nc.scalar.activation(xf[:, k, :], xf[:, k, :], ACT.Silu,
                                                 bias=dw_b[:, k:k + 1]).then_inc(sem("xf_ready"), 1)
                    act.wait_ge(sem("part_ready"), 6)
                    for k in range(KC):
                        nc.scalar.activation(gate[:, k, :], gate[:, k, :], ACT.Silu).then_inc(sem("gate_ready"), 1)
                    act.wait_ge(sem("minus_abs"), 1)
                    nc.scalar.activation(sp_t[:, 1, :, :], sp_t[:, 0, :, :], ACT.Exp).then_inc(sem("soft_exp"), 1)
                    act.wait_ge(sem("one_plus"), 1)
                    nc.scalar.activation(sp_t[:, 3, :, :], sp_t[:, 2, :, :], ACT.Ln).then_inc(sem("soft_ln"), 1)
                    act.wait_ge(sem("dt_decay"), 1)
                    nc.scalar.activation(rows[:, :, :, 0:S], rows[:, :, :, 0:S], ACT.Exp).then_inc(sem("decay_ready"), 1)
                    for h in range(HEADS):
                        for j in range(NH):
                            act.wait_ge(sem("rows_moved"), h * NH + j + 1)
                            lo = (6 + j) * HALF
                            nc.scalar.activation(rows_p[:, h, j * HALF:(j + 1) * HALF], ps[0:3 * ROWS, lo:lo + HALF],
                                                 ACT.Copy).then_inc(sem("rows_p_ready"), 1)
                    for h in range(HEADS):
                        for j in range(NH):
                            act.wait_ge(sem("x_moved"), h * NH + j + 1)
                            lo = (6 + j) * HALF
                            nc.scalar.activation(xp[:, h, j * HALF:(j + 1) * HALF], ps[:, lo:lo + HALF],
                                                 ACT.Copy).then_inc(sem("xp_ready"), 1)
                    for m in range(KC):
                        act.wait_ge(sem("out_projected"), m + 1)
                        lo = m * N
                        nc.scalar.activation(xf[:, m, :], ps[:, lo:lo + N], ACT.Silu,
                                             bias=out_b[:, m:m + 1]).then_inc(sem("out_ready"), 1)

                @block.vector
                def _(dve):
                    link = Chain(dve, sem("dve_chain"))
                    tt, ts, stt = nc.vector.tensor_tensor, nc.vector.tensor_scalar, nc.vector.scalar_tensor_tensor
                    dve.wait_ge(sem("x_loaded"), 16)
                    norm_stats_vector(nc, dve, st, link, x, stats, moments, ps[:, 7 * HALF:8 * HALF])
                    for k in range(KC):
                        normalise(nc, xn[:, k, :], x[:, k, :], moments, k).then_inc(sem("xn_ready"), 1)
                    dve.wait_ge(sem("border"), 2)
                    for k in range(KC):
                        dve.wait_ge(sem("part_ready"), k + 1)
                        link(ts(xf[:, k, :], ssm[:, k, 0:N], dw_w[:, k, 0:1], None, ALU.mult))
                        link(stt(xf[:, k, :], ssm[:, k, 1:N + 1], dw_w[:, k, 1:2], xf[:, k, :], ALU.mult, ALU.add))
                        stt(xf[:, k, :], ssm[:, k, 2:N + 2], dw_w[:, k, 2:3], xf[:, k, :], ALU.mult,
                            ALU.add).then_inc(sem("conv_ready"), 1)
                    dve.wait_ge(sem("dbc_ready"), 1)
                    flat = dbc[:, :, :, :].rearrange("p t h r -> p t (h r)")
                    link(tt(flat, ps[:, 6 * HALF:6 * HALF + NT * HEADS * DBC].rearrange("p (t r) -> p t r", t=NT),
                            dbc_b[:, :].unsqueeze(1).to_broadcast([P, NT, HEADS * DBC]), ALU.add))
                    raw = dbc[:, :, :, 0]
                    stt(sp_t[:, 0, :, :], raw, -1.0, raw, ALU.mult, ALU.min).then_inc(sem("minus_abs"), 1)
                    dve.wait_ge(sem("soft_exp"), 1)
                    ts(sp_t[:, 2, :, :], sp_t[:, 1, :, :], 1.0, None, ALU.add).then_inc(sem("one_plus"), 1)
                    dve.wait_ge(sem("soft_ln"), 1)
                    link(ts(sp_t[:, 4, :, :], sp_t[:, 2, :, :], -1.0, None, ALU.add))
                    link(ts(sp_t[:, 5, :, :], sp_t[:, 4, :, :], 0.0, None, ALU.is_equal))
                    link(tt(sp_t[:, 4, :, :], sp_t[:, 4, :, :], sp_t[:, 5, :, :], ALU.add))
                    link(nc.vector.reciprocal(sp_t[:, 4, :, :], sp_t[:, 4, :, :]))
                    link(tt(sp_t[:, 3, :, :], sp_t[:, 3, :, :], sp_t[:, 5, :, :], ALU.add))
                    link(tt(sp_t[:, 3, :, :], sp_t[:, 3, :, :], sp_t[:, 1, :, :], ALU.mult))
                    link(tt(sp_t[:, 3, :, :], sp_t[:, 3, :, :], sp_t[:, 4, :, :], ALU.mult))
                    link(stt(sp_t[:, 0, :, :], raw, 0.0, sp_t[:, 3, :, :], ALU.max, ALU.add))
                    for h in range(HEADS):
                        dt = sp_t[:, 0, :, h].unsqueeze(2).to_broadcast([P, NT, S])
                        a = decay[:, h, :].unsqueeze(1).to_broadcast([P, NT, S])
                        link(tt(rows[:, :, h, 0:S], dt, a, ALU.mult))
                        link(tt(rows[:, :, h, S:2 * S], dt, dbc[:, :, h, 1:1 + S], ALU.mult))
                        link(nc.vector.tensor_copy(rows[:, :, h, 2 * S:3 * S], dbc[:, :, h, 1 + S:1 + 2 * S]))
                    nc.vector.memset(sp_t[:, 4, 0, 0:1], 0.0).then_inc(sem("dt_decay"), 1)
                    dve.wait_ge(sem("decay_ready"), 1)
                    split_vector(nc, link, [rows3[:, :, :, i, :] for i in range(3)], rows[:, :, :, :],
                                 rows_rest[:, :, :, :]).then_inc(sem("rows3_ready"), 1)
                    for h in range(HEADS):
                        dve.wait_ge(sem("x_turned"), h + 1)
                        lo = h * N
                        split_vector(nc, link, [xt3[:, h, i, :] for i in range(3)], ps[:, lo:lo + N],
                                     rest_x).then_inc(sem("xt3_ready"), 1)
                        dve.wait_ge(sem("xt3_ready"), h + 1)
                    for i in range(HEADS * S):
                        h, s = divmod(i, S)
                        if s == 0:
                            dve.wait_ge(sem("xp_ready"), NH * (h + 1))
                        dve.wait_ge(sem("db_spread"), i + 1)
                        tt(dbx[:, i % 2, :], ps[:, 2 * HALF:4 * HALF], xp[:, h, :], ALU.mult).then_inc(sem("db_used"), 1)
                        dve.wait_ge(sem("db_used"), i + 1)
                        dve.wait_ge(sem("da_spread"), i + 1)
                        nc.vector.tensor_tensor_scan(states[:, i % 2, :], ps[:, 0:2 * HALF], dbx[:, i % 2, :], 0.0,
                                                     ALU.mult, ALU.add).then_inc(sem("da_used"), 1)
                        dve.wait_ge(sem("da_used"), i + 1)
                        dve.wait_ge(sem("c_spread"), i + 1)
                        if i >= 2:
                            dve.wait_ge(sem("summed"), i - 1)
                        tt(seen[:, i % 2, :], ps[:, 4 * HALF:6 * HALF], states[:, i % 2, :],
                           ALU.mult).then_inc(sem("seen_ready"), 1)
                    dve.wait_ge(sem("summed"), HEADS * S)
                    for h in range(HEADS):
                        stt(acc[:, h, :], xp[:, h, :], skip[:, h:h + 1], acc[:, h, :], ALU.mult,
                            ALU.add).then_inc(sem("y_ready"), 1)
                    for h in range(HEADS):
                        dve.wait_ge(sem("y_turned"), h + 1)
                        lo = h * N
                        split_vector(nc, link, [xt3[:, h, i, :] for i in range(3)], ps[:, lo:lo + N],
                                     rest_x).then_inc(sem("yt3_ready"), 1)
                        dve.wait_ge(sem("yt3_ready"), h + 1)
                    for h in range(HEADS):
                        dve.wait_ge(sem("y_moved"), h + 1)
                        dve.wait_ge(sem("gate_ready"), KC)
                        lo = (4 + 2 * h) * HALF
                        link(tt(xn[:, h, :], ps[:, lo:lo + N], gate[:, h, :], ALU.mult))
                        tt(xn[:, h, :], xn[:, h, :], res[:, h, :], ALU.add).then_inc(sem("mixed"), 1)
                    for m in range(KC):
                        dve.wait_ge(sem("out_ready"), m + 1)
                        tt(x[:, m, :], x[:, m, :], xf[:, m, :], ALU.add).then_inc(sem("new_x"), 1)

                @block.tensor
                def _(pe):
                    norm_stats_tensor(nc, pe, st, moments, average, ps[:, 7 * HALF:8 * HALF])
                    pe.wait_ge(sem("xn_ready"), KC)
                    for m in range(6):
                        if m >= 2:
                            pe.wait_ge(sem("part_ready"), m - 1)
                        for j in range(NH):
                            for k in range(KC):
                                lo = (m % 2) * N + j * HALF
                                ins = nc.tensor.matmul(ps[:, lo:lo + HALF], in_w[:, k, m * P:(m + 1) * P],
                                                       xn[:, k, j * HALF:(j + 1) * HALF], start=(k == 0), stop=(k == KC - 1))
                        ins.then_inc(sem("projected"), 1)
                    pe.wait_ge(sem("xf_ready"), KC)
                    for c_ in range(NT):
                        for k in range(KC):
                            lo = 6 * HALF + c_ * HEADS * DBC
                            ins = nc.tensor.matmul(ps[:, lo:lo + HEADS * DBC], xf[:, k, c_ * P:(c_ + 1) * P],
                                                   dbc_w[:, k, :], start=(k == 0), stop=(k == KC - 1))
                    ins.then_inc(sem("dbc_ready"), 1)
                    pe.wait_ge(sem("part_ready"), 6)
                    for h in range(HEADS):
                        for c_ in range(NT):
                            lo = h * N + c_ * P
                            ins = nc.tensor.transpose(ps[:, lo:lo + P], xf[:, h, c_ * P:(c_ + 1) * P], ident[:, :])
                        ins.then_inc(sem("x_turned"), 1)
                    pe.wait_ge(sem("rows3_ready"), 1)
                    for h in range(HEADS):
                        for j in range(NH):
                            if h:
                                pe.wait_ge(sem("rows_p_ready"), j + 1)
                            lo = (6 + j) * HALF
                            for c_ in range(NT):
                                ins = nc.tensor.matmul(ps[0:3 * ROWS, lo:lo + HALF],
                                                       rows3[:, c_, h, :, :].rearrange("p a r -> p (a r)"),
                                                       forward[:, h, c_, j * HALF:(j + 1) * HALF],
                                                       start=(c_ == 0), stop=(c_ == NT - 1))
                            ins.then_inc(sem("rows_moved"), 1)
                    for h in range(HEADS):
                        pe.wait_ge(sem("xt3_ready"), h + 1)
                        for j in range(NH):
                            if h:
                                pe.wait_ge(sem("xp_ready"), j + 1)
                            else:
                                pe.wait_ge(sem("rows_p_ready"), NH + j + 1)
                            lo = (6 + j) * HALF
                            for c_ in range(NT):
                                for i in range(3):
                                    ins = nc.tensor.matmul(ps[:, lo:lo + HALF], xt3[:, h, i, c_ * P:(c_ + 1) * P],
                                                           forward[:, h, c_, j * HALF:(j + 1) * HALF],
                                                           start=(c_ == 0 and i == 0), stop=(c_ == NT - 1 and i == 2))
                            ins.then_inc(sem("x_moved"), 1)
                    for i in range(HEADS * S):
                        h, s = divmod(i, S)
                        for q, bank, ready, used in ((S + s, 2, "db_spread", "db_used"), (s, 0, "da_spread", "da_used"),
                                                     (2 * S + s, 4, "c_spread", "seen_ready")):
                            if i:
                                pe.wait_ge(sem(used), i)
                            for j in range(NH):
                                lo = (bank + j) * HALF
                                ins = nc.tensor.matmul(ps[:, lo:lo + HALF], sel[:, q, :],
                                                       rows_p[:, h, j * HALF:(j + 1) * HALF], start=True, stop=True)
                            ins.then_inc(sem(ready), 1)
                    pe.wait_ge(sem("seen_ready"), HEADS * S)
                    for h in range(HEADS):
                        pe.wait_ge(sem("y_ready"), h + 1)
                        for c_ in range(NT):
                            lo = h * N + c_ * P
                            ins = nc.tensor.transpose(ps[:, lo:lo + P], acc[:, h, c_ * P:(c_ + 1) * P], ident[:, :])
                        ins.then_inc(sem("y_turned"), 1)
                    for h in range(HEADS):
                        pe.wait_ge(sem("yt3_ready"), h + 1)
                        for j in range(NH):
                            lo = (4 + 2 * h + j) * HALF
                            for c_ in range(NT):
                                for i in range(3):
                                    ins = nc.tensor.matmul(ps[:, lo:lo + HALF], xt3[:, h, i, c_ * P:(c_ + 1) * P],
                                                           backward[:, h, c_, j * HALF:(j + 1) * HALF],
                                                           start=(c_ == 0 and i == 0), stop=(c_ == NT - 1 and i == 2))
                        ins.then_inc(sem("y_moved"), 1)
                    pe.wait_ge(sem("mixed"), HEADS)
                    for m in range(KC):
                        for j in range(NH):
                            for k in range(KC):
                                lo = m * N + j * HALF
                                ins = nc.tensor.matmul(ps[:, lo:lo + HALF], out_w[:, k, m * P:(m + 1) * P],
                                                       xn[:, k, j * HALF:(j + 1) * HALF], start=(k == 0), stop=(k == KC - 1))
                        ins.then_inc(sem("out_projected"), 1)
            st.clear()


def build_expert_layer(nc, t, ps, src, dst):
    with ExitStack() as ctx:
        st = Stage(nc, ctx, "l1")
        sem = st.sem
        w1 = st.sb("w1", [P, KC, E, C])
        w3 = st.sb("w3", [P, KC, E, C])
        w2 = st.sb("w2", [P, KC, E, C])
        gate_w = st.sb("gate_w", [P, KC, E])
        sel = st.sb("sel", [3 * E, E, P], BF16)
        average = st.sb("average", [P, P])
        ident = st.sb("ident", [P, P], BF16)
        minus_half = st.sb("minus_half", [P, 4])
        index = st.sb("index", [P, E])
        x = st.sb("x", [P, KC, N])
        xn = st.sb("xn", [P, KC, N])
        stats = st.sb("stats", [P, KC, 6 * NH])
        moments = st.sb("moments", [P, KC, 8])
        prob = st.sb("prob", [P, NT, E])
        left = st.sb("left", [P, NT, E])
        work = st.sb("work", [P, NT, E])
        first = st.sb("first", [P, NT, E])
        best = st.sb("best", [P, NT, 6])
        comb = st.sb("comb", [P, NT, E])
        comb_rest = st.sb("comb_rest", [P, NT, E])
        comb3 = st.sb("comb3", [P, NT, 3, E], BF16)
        comb_t = st.sb("comb_t", [3 * E, N], BF16)
        act1 = st.sb("act1", [P, 2, HALF])
        hid = st.sb("hid", [P, 2, HALF])
        mixed = st.sb("mixed", [P, 2, HALF])
        loads = [
            (w1[:, :, :, :], t["w1"].rearrange("(k p) e f -> p k e f", p=P)),
            (w3[:, :, :, :], t["w3"].rearrange("(k p) e f -> p k e f", p=P)),
            (w2[:, :, :, :], t["w2"].rearrange("(k p) e f -> p k e f", p=P)),
            (gate_w[:, :, :], t["gate_w"].rearrange("(k p) e -> p k e", p=P)),
            (sel[:, :, :], t["sel_experts"].bitcast(BF16)), (average[:, :], t["average"]), (ident[:, :], t["ident_bf16"].bitcast(BF16)),
            (index[:, :], t["index"].partition_broadcast(P)),
        ]
        with nc.Block() as block:

            @block.sync
            def _(sp):
                for to, of in loads:
                    sp.dma_start(to, of).then_inc(sem("loaded"), 16)
                sp.wait_ge(sem("loaded"), 16 * len(loads))

            @block.gpsimd
            def _(pool):
                nc.gpsimd.memset(minus_half[:, :], -0.5).then_inc(sem("const"), 1)
                pool.wait_ge(sem("const"), 1)
        st.clear()

        steps = [(j, e, f) for j in range(NH) for e in range(E) for f in range(KC)]
        with nc.Fori(0, B) as b:
            with nc.Block() as block:

                @block.sync
                def _(sp):
                    sp.dma_start(x[:, :, :], image(src, b)).then_inc(sem("x_loaded"), 16)
                    sp.wait_ge(sem("new_x"), NH * KC)
                    sp.dma_start(image(dst, b), x[:, :, :]).then_inc(sem("stored"), 16)
                    sp.wait_ge(sem("stored"), 16)

                @block.gpsimd
                def _(pool):
                    norm_stats_pool(nc, pool, st, moments, minus_half)

                @block.scalar
                def _(act):
                    act.wait_ge(sem("shifted"), 1)
                    nc.scalar.activation(prob[:, :, :], prob[:, :, :], ACT.Exp).then_inc(sem("exped"), 1)
                    act.wait_ge(sem("comb_turned"), 1)
                    nc.scalar.activation(comb_t[:, :], ps[0:3 * E, 0:N], ACT.Copy).then_inc(sem("comb_t_ready"), 1)
                    for i, (j, e, f) in enumerate(steps):
                        act.wait_ge(sem("up_ready"), i + 1)
                        if i >= 2:
                            act.wait_ge(sem("hid_ready"), i - 1)
                        nc.scalar.activation(act1[:, i % 2, :], ps[:, (i % 2) * HALF:(i % 2 + 1) * HALF],
                                             ACT.Gelu).then_inc(sem("gelu_ready"), 1)

                @block.vector
                def _(dve):
                    link = Chain(dve, sem("dve_chain"))
                    tt, ts, stt = nc.vector.tensor_tensor, nc.vector.tensor_scalar, nc.vector.scalar_tensor_tensor

                    def spread(v):
                        return v.unsqueeze(2).to_broadcast([P, NT, E])

                    dve.wait_ge(sem("x_loaded"), 16)
                    norm_stats_vector(nc, dve, st, link, x, stats, moments, ps[:, 7 * HALF:8 * HALF])
                    for k in range(KC):
                        normalise(nc, xn[:, k, :], x[:, k, :], moments, k).then_inc(sem("xn_ready"), 1)
                    dve.wait_ge(sem("logits_ready"), 1)
                    logits = ps[:, 6 * HALF:6 * HALF + NT * E].rearrange("p (t e) -> p t e", t=NT)
                    link(nc.vector.tensor_reduce(best[:, :, 0], logits, AX, ALU.max))
                    tt(prob[:, :, :], logits, spread(best[:, :, 0]), ALU.subtract).then_inc(sem("shifted"), 1)
                    dve.wait_ge(sem("exped"), 1)
                    link(nc.vector.tensor_reduce(best[:, :, 1], prob[:, :, :], AX, ALU.add))
                    link(nc.vector.reciprocal(best[:, :, 1], best[:, :, 1]))
                    link(tt(prob[:, :, :], prob[:, :, :], spread(best[:, :, 1]), ALU.mult))
                    link(nc.vector.tensor_copy(left[:, :, :], prob[:, :, :]))
                    link(nc.vector.memset(comb[:, :, :], 0.0))
                    idx = index[:, :].unsqueeze(1).to_broadcast([P, NT, E])
                    for r in range(2):
                        link(nc.vector.tensor_reduce(best[:, :, 2 + r], left[:, :, :], AX, ALU.max))
                        link(tt(work[:, :, :], left[:, :, :], spread(best[:, :, 2 + r]), ALU.not_equal))
                        link(stt(work[:, :, :], work[:, :, :], float(E), idx, ALU.mult, ALU.add))
                        link(nc.vector.tensor_reduce(best[:, :, 4], work[:, :, :], AX, ALU.min))
                        link(tt(first[:, :, :], idx, spread(best[:, :, 4]), ALU.is_equal))
                        link(stt(left[:, :, :], first[:, :, :], -2.0, left[:, :, :], ALU.mult, ALU.add))
                        link(tt(first[:, :, :], first[:, :, :], prob[:, :, :], ALU.mult))
                        link(tt(comb[:, :, :], comb[:, :, :], first[:, :, :], ALU.add))
                    link(tt(best[:, :, 5], best[:, :, 2], best[:, :, 3], ALU.add))
                    link(nc.vector.reciprocal(best[:, :, 5], best[:, :, 5]))
                    link(tt(comb[:, :, :], comb[:, :, :], spread(best[:, :, 5]), ALU.mult))
                    split_vector(nc, link, [comb3[:, :, i, :] for i in range(3)], comb[:, :, :],
                                 comb_rest[:, :, :]).then_inc(sem("comb3_ready"), 1)
                    for i, (j, e, f) in enumerate(steps):
                        dve.wait_ge(sem("gelu_ready"), i + 1)
                        link(tt(hid[:, i % 2, :], ps[:, (2 + i % 2) * HALF:(3 + i % 2) * HALF], act1[:, i % 2, :], ALU.mult))
                        ins = nc.vector.memset(best[:, 0, 0:1], 0.0)
                        ins.then_inc(sem("hid_ready"), 1)
                        dve.wait_ge(sem("weight_spread"), i // KC + 1)
                        if i >= 2:
                            dve.wait_ge(sem("down_done"), i - 1)
                        tt(mixed[:, i % 2, :], ps[:, 4 * HALF:5 * HALF], hid[:, i % 2, :],
                           ALU.mult).then_inc(sem("mixed_ready"), 1)
                        if i % (E * KC) == E * KC - 1:
                            dve.wait_ge(sem("down_done"), i + 1)
                            for m in range(KC):
                                tt(x[:, m, j * HALF:(j + 1) * HALF], ps[:, (5 + m) * HALF:(6 + m) * HALF],
                                   x[:, m, j * HALF:(j + 1) * HALF], ALU.add).then_inc(sem("new_x"), 1)

                @block.tensor
                def _(pe):
                    norm_stats_tensor(nc, pe, st, moments, average, ps[:, 7 * HALF:8 * HALF])
                    pe.wait_ge(sem("xn_ready"), KC)
                    for c_ in range(NT):
                        for k in range(KC):
                            lo = 6 * HALF + c_ * E
                            ins = nc.tensor.matmul(ps[:, lo:lo + E], xn[:, k, c_ * P:(c_ + 1) * P], gate_w[:, k, :],
                                                   start=(k == 0), stop=(k == KC - 1))
                    ins.then_inc(sem("logits_ready"), 1)
                    pe.wait_ge(sem("comb3_ready"), 1)
                    for c_ in range(NT):
                        ins = nc.tensor.matmul(ps[0:3 * E, c_ * P:(c_ + 1) * P],
                                               comb3[:, c_, :, :].rearrange("p a e -> p (a e)"), ident[:, :],
                                               start=True, stop=True)
                    ins.then_inc(sem("comb_turned"), 1)
                    pe.wait_ge(sem("comb_t_ready"), 1)

                    def up(i):
                        j, e, f = steps[i]
                        if i >= 2:
                            pe.wait_ge(sem("hid_ready"), i - 1)
                        for bank, w in ((0, w1), (2, w3)):
                            lo = (bank + i % 2) * HALF
                            for k in range(KC):
                                ins = nc.tensor.matmul(ps[:, lo:lo + HALF], w[:, k, e, f * P:(f + 1) * P],
                                                       xn[:, k, j * HALF:(j + 1) * HALF], start=(k == 0), stop=(k == KC - 1))
                        ins.then_inc(sem("up_ready"), 1)

                    def down(i):
                        j, e, f = steps[i]
                        if f == 0:
                            if i:
                                pe.wait_ge(sem("mixed_ready"), i)
                            nc.tensor.matmul(ps[:, 4 * HALF:5 * HALF], sel[:, e, :], comb_t[:, j * HALF:(j + 1) * HALF],
                                             start=True, stop=True).then_inc(sem("weight_spread"), 1)
                        pe.wait_ge(sem("mixed_ready"), i + 1)
                        if e == 0 and f == 0 and j:
                            pe.wait_ge(sem("new_x"), KC * j)
                        for m in range(KC):
                            lo = (5 + m) * HALF
                            ins = nc.tensor.matmul(ps[:, lo:lo + HALF], w2[:, f, e, m * P:(m + 1) * P], mixed[:, i % 2, :],
                                                   start=(e == 0 and f == 0), stop=(e == E - 1 and f == KC - 1))
                        ins.then_inc(sem("down_done"), 1)

                    up(0)
                    for i in range(len(steps)):
                        if i + 1 < len(steps):
                            up(i + 1)
                        down(i)
            st.clear()


class Coordinates:

    def __init__(self, st, parts):
        self.pos = st.sb("pos", [parts, N])
        self.rest = st.sb("pos_rest", [parts, N])
        self.parts3 = st.sb("parts3", [parts, 2, 3, N], BF16)

    def vector(self, nc, link, i, off, bias, grid):
        stt, ts = nc.vector.scalar_tensor_tensor, nc.vector.tensor_scalar
        link(stt(self.pos[:, :], off, bias, grid, ALU.add, ALU.add))
        link(ts(self.pos[:, :], self.pos[:, :], 0.0, float(SIDE - 1), ALU.max, ALU.min))
        return split_vector(nc, link, [self.parts3[:, i % 2, j, :] for j in range(3)], self.pos[:, :], self.rest[:, :])


def padded_rows(pad, j, tap):
    dy, dx = divmod(tap, 3)
    rows = HALF // SIDE
    return pad[:, j * rows + dy:j * rows + dy + rows, dx:dx + SIDE]


def build_offsets_1(nc, t, ps, xcur, dense, coords):
    with ExitStack() as ctx:
        st = Stage(nc, ctx, "o1")
        sem = st.sem
        ow = st.sb("ow", [P, KC, 9, 2, C])
        ob = st.sb("ob", [P, 2 * KC])
        grid = st.sb("grid", [P, 2, N])
        average = st.sb("average", [P, P])
        minus_half = st.sb("minus_half", [P, 4])
        x = st.sb("x", [P, KC, N])
        pad = st.sb("pad", [P, KC, PAD, PAD])
        stats = st.sb("stats", [P, KC, 6 * NH])
        moments = st.sb("moments", [P, KC, 8])
        co = Coordinates(st, P)
        loads = [
            (ow[:, :, :, :, :], t["ow1"].rearrange("(k p) a y c -> p k a y c", p=P)), (ob[:, :], t["ob1"]),
            (grid[:, 0, :], t["row_of"].partition_broadcast(P)), (grid[:, 1, :], t["col_of"].partition_broadcast(P)),
            (average[:, :], t["average"]),
        ]
        with nc.Block() as block:

            @block.sync
            def _(sp):
                for dst, src in loads:
                    sp.dma_start(dst, src).then_inc(sem("loaded"), 16)
                sp.wait_ge(sem("loaded"), 16 * len(loads))

            @block.gpsimd
            def _(pool):
                nc.gpsimd.memset(minus_half[:, :], -0.5).then_inc(sem("const"), 1)
                nc.gpsimd.memset(pad[:, :, :, :], 0.0).then_inc(sem("const"), 1)
                pool.wait_ge(sem("const"), 2)
        st.clear()

        kinds = [(k, y) for k in range(KC) for y in range(2)]
        with nc.Fori(0, B) as b:
            with nc.Block() as block:

                @block.sync
                def _(sp):
                    sp.dma_start(x[:, :, :], image(xcur, b)).then_inc(sem("x_loaded"), 16)
                    sp.wait_ge(sem("xn_ready"), KC)
                    for k in range(KC):
                        sp.dma_start(dense[bass.ds(b * C + k * P, P), :].rearrange("p (y w) -> p y w", w=SIDE),
                                     pad[:, k, 1:SIDE + 1, 1:SIDE + 1]).then_inc(sem("stored"), 16)
                    for i, (k, y) in enumerate(kinds):
                        sp.wait_ge(sem("coords_ready"), i + 1)
                        for q in range(P // BLK):
                            blk = b * (C // BLK) + k * (P // BLK) + q
                            sp.dma_start(coords[bass.ds(blk, 1), y, :, :, :].rearrange("a s p n -> (a p) s n"),
                                         co.parts3[q * BLK:(q + 1) * BLK, i % 2, :, :]).then_inc(sem(f"coords_stored{i}"), 16)
                    for i in range(len(kinds)):
                        sp.wait_ge(sem(f"coords_stored{i}"), 16 * (P // BLK))
                    sp.wait_ge(sem("stored"), 16 * KC)

                @block.gpsimd
                def _(pool):
                    norm_stats_pool(nc, pool, st, moments, minus_half)

                @block.vector
                def _(dve):
                    link = Chain(dve, sem("dve_chain"))
                    dve.wait_ge(sem("x_loaded"), 16)
                    norm_stats_vector(nc, dve, st, link, x, stats, moments, ps[:, 7 * HALF:8 * HALF])
                    for k in range(KC):
                        normalise(nc, pad[:, k, 1:SIDE + 1, 1:SIDE + 1], x[:, k, :].rearrange("p (y w) -> p y w", w=SIDE),
                                  moments, k).then_inc(sem("xn_ready"), 1)
                    for i, (k, y) in enumerate(kinds):
                        dve.wait_ge(sem("offsets_ready"), i + 1)
                        if i >= 2:
                            dve.wait_ge(sem(f"coords_stored{i - 2}"), 16 * (P // BLK))
                        lo = (i % 2) * N
                        col = 2 * k + y
                        co.vector(nc, link, i, ps[:, lo:lo + N], ob[:, col:col + 1], grid[:, y, :])\
                          .then_inc(sem("coords_ready"), 1)
                        dve.wait_ge(sem("coords_ready"), i + 1)

                @block.tensor
                def _(pe):
                    norm_stats_tensor(nc, pe, st, moments, average, ps[:, 7 * HALF:8 * HALF])
                    pe.wait_ge(sem("xn_ready"), KC)
                    for i, (k, y) in enumerate(kinds):
                        if i >= 2:
                            pe.wait_ge(sem("coords_ready"), i - 1)
                        for j in range(NH):
                            lo = (i % 2) * N + j * HALF
                            for n in range(KC * 9):
                                kk, tap = divmod(n, 9)
                                ins = nc.tensor.matmul(ps[:, lo:lo + HALF], ow[:, kk, tap, y, k * P:(k + 1) * P],
                                                       padded_rows(pad[:, kk], j, tap), start=(n == 0), stop=(n == KC * 9 - 1))
                        ins.then_inc(sem("offsets_ready"), 1)
            st.clear()


def build_gather(nc, t, ps, dense, coords, gathered, blocks, tag):
    with ExitStack() as ctx:
        st = Stage(nc, ctx, tag)
        sem = st.sem
        spread = st.sb("spread", [3 * BLK, NG, P], BF16)
        fold = st.sb("fold", [P, NG, BLK])
        index = st.sb("index", [P, 1])
        coord = st.sb("coord", [3 * BLK, UNITS, 2, N], BF16)
        img = st.sb("img", [P, UNITS, NG, P])
        wts = st.sb("wts", [P, 2, 2, HALF])
        prod = st.sb("prod", [P, 2, HALF])
        res = st.sb("res", [BLK, UNITS, N])
        loads = [(spread[:, :, :], t["sel_spread"].bitcast(BF16)), (fold[:, :, :], t["sel_fold"]), (index[:, :], t["minus_index"])]
        with nc.Block() as block:

            @block.sync
            def _(sp):
                for dst, src in loads:
                    sp.dma_start(dst, src).then_inc(sem("loaded"), 16)
                sp.wait_ge(sem("loaded"), 16 * len(loads))

            @block.gpsimd
            def _(pool):
                nc.gpsimd.memset(img[:, :, :, :], 0.0).then_inc(sem("const"), 1)
                pool.wait_ge(sem("const"), 1)
        st.clear()

        steps = [(u, g, j) for u in range(UNITS) for g in range(NG) for j in range(NH)]
        per = NG * NH
        with nc.Fori(0, blocks // UNITS) as turn:
            n0 = turn * UNITS
            with nc.Block() as block:

                @block.sync
                def _(sp):
                    for u in range(UNITS):
                        sp.dma_start(coord[:, u, :, :], coords[bass.ds(n0 + u, 1), :, :, :, :]
                                     .rearrange("a y s p n -> (a s p) y n")).then_inc(sem(f"coord_loaded{u}"), 16)
                    for u in range(UNITS):
                        sp.wait_ge(sem("folded"), per * (u + 1))
                        sp.wait_ge(sem("res_ready"), u + 1)
                        sp.dma_start(gathered[bass.ds((n0 + u) * BLK, BLK), :], res[:, u, :]).then_inc(sem("stored"), 16)
                    sp.wait_ge(sem("stored"), 16 * UNITS)

                def evacuate(act, u):
                    act.wait_ge(sem("folded"), per * (u + 1))
                    nc.scalar.activation(res[:, u, :], ps[0:BLK, 6 * HALF:8 * HALF], ACT.Copy).then_inc(sem("res_ready"), 1)

                @block.scalar
                def _(act):
                    for u in range(UNITS):
                        src = dense[bass.ds((n0 + u) * BLK, BLK), :].rearrange("(g c) (i j) -> c i g j", c=4, j=SIDE)
                        for c in range(4):
                            act.dma_start(img[c * SIDE:(c + 1) * SIDE, u, :, c * SIDE:(c + 1) * SIDE],
                                          src[c]).then_inc(sem(f"img_loaded{u}"), 16)
                    for i, (u, g, j) in enumerate(steps):
                        act.wait_ge(sem("spread_ready"), i + 1)
                        if i >= 2:
                            act.wait_ge(sem("weighted"), i - 1)
                        lo = 2 * (i % 2) * HALF
                        nc.scalar.activation(wts[:, i % 2, :, :].rearrange("p y n -> p (y n)"), ps[:, lo:lo + 2 * HALF],
                                             ACT.Abs, bias=index[:, 0:1]).then_inc(sem("distance_ready"), 1)
                        if i % per == 3 and u:
                            evacuate(act, u - 1)
                    evacuate(act, UNITS - 1)

                @block.vector
                def _(dve):
                    for i in range(len(steps) + 1):
                        if i < len(steps):
                            dve.wait_ge(sem("distance_ready"), i + 1)
                            nc.vector.tensor_scalar(wts[:, i % 2, :, :], wts[:, i % 2, :, :], 1.0, -1.0, ALU.min,
                                                    ALU.add).then_inc(sem("weights_ready"), 1)
                        if i:
                            k = i - 1
                            dve.wait_ge(sem("weights_ready"), i)
                            dve.wait_ge(sem("rows_summed"), k + 1)
                            if k >= 2:
                                dve.wait_ge(sem("folded"), k - 1)
                            nc.vector.tensor_tensor(prod[:, k % 2, :], ps[:, (4 + k % 2) * HALF:(5 + k % 2) * HALF],
                                                    wts[:, k % 2, 1, :], ALU.mult).then_inc(sem("weighted"), 1)

                @block.tensor
                def _(pe):
                    def spread_step(i):
                        u, g, j = steps[i]
                        if i % per == 0:
                            pe.wait_ge(sem(f"coord_loaded{u}"), 16)
                        if i >= 2:
                            pe.wait_ge(sem("distance_ready"), i - 1)
                        for y in range(2):
                            lo = (2 * (i % 2) + y) * HALF
                            ins = nc.tensor.matmul(ps[:, lo:lo + HALF], spread[:, g, :],
                                                   coord[:, u, y, j * HALF:(j + 1) * HALF], start=True, stop=True)
                        ins.then_inc(sem("spread_ready"), 1)

                    def rows_step(i):
                        u, g, j = steps[i]
                        if i % per == 0:
                            pe.wait_ge(sem(f"img_loaded{u}"), 64)
                        pe.wait_ge(sem("weights_ready"), i + 1)
                        if i >= 2:
                            pe.wait_ge(sem("weighted"), i - 1)
                        lo = (4 + i % 2) * HALF
                        nc.tensor.matmul(ps[:, lo:lo + HALF], img[:, u, g, :], wts[:, i % 2, 0, :], start=True,
                                         stop=True).then_inc(sem("rows_summed"), 1)

                    def fold_step(i):
                        u, g, j = steps[i]
                        pe.wait_ge(sem("weighted"), i + 1)
                        if i % per == 0 and u:
                            pe.wait_ge(sem("res_ready"), u)
                        lo = (6 + j) * HALF
                        nc.tensor.matmul(ps[0:BLK, lo:lo + HALF], fold[:, g, :], prod[:, i % 2, :], start=(g == 0),
                                         stop=(g == NG - 1)).then_inc(sem("folded"), 1)

                    n = len(steps)
                    spread_step(0)
                    spread_step(1)
                    for i in range(n + 1):
                        if i < n:
                            rows_step(i)
                        if i + 2 < n:
                            spread_step(i + 2)
                        if i:
                            fold_step(i - 1)
            st.clear()


def batch_norm_setup(nc, dve, link, sem, cols, out, minus_half):
    link(nc.vector.tensor_scalar(out[:, 2], cols[:, 3], BN_EPS, None, ALU.add))
    nc.vector.tensor_scalar(out[:, 2], out[:, 2], 1.0, None, ALU.mult).then_inc(sem("bn_var"), 1)
    dve.wait_ge(sem("bn_root"), 1)
    link(nc.vector.tensor_tensor(out[:, 0], cols[:, 0], out[:, 3], ALU.mult))
    link(nc.vector.tensor_tensor(out[:, 1], cols[:, 2], out[:, 0], ALU.mult))
    link(nc.vector.tensor_tensor(out[:, 1], cols[:, 1], out[:, 1], ALU.subtract))


def build_middle(nc, t, ps, gathered, dense, coords, n):
    taps = 1 if n == 2 else 9
    kc, kp = (KC, P) if n == 2 else (1, CM)
    with ExitStack() as ctx:
        st = Stage(nc, ctx, f"o{n}")
        sem = st.sem
        w = st.sb("w", [kp, kc, taps, CM])
        ow = st.sb("ow", [CM, 9, P])
        ob = st.sb("ob", [P, 1])
        cols = st.sb("cols", [CM, 4])
        bn = st.sb("bn", [CM, 4])
        grid = st.sb("grid", [P, N])
        minus_half = st.sb("minus_half", [CM, 1])
        x = st.sb("x", [kp, kc, PAD, PAD])
        pad = st.sb("pad", [CM, PAD, PAD])
        co = Coordinates(st, P)
        loads = [
            (w[:, :, :, :], t[f"w_{n}"].rearrange("(k p) a c -> p k a c", p=kp)), (ow[:, :, :], t[f"ow{n}"]),
            (ob[:, :], t[f"ob{n}"]), (cols[:, :], t[f"bn{n - 1}"]),
            (grid[0:CM, :], t["row_of"].partition_broadcast(CM)), (grid[CM:P, :], t["col_of"].partition_broadcast(CM)),
        ]
        with nc.Block() as block:

            @block.sync
            def _(sp):
                for dst, src in loads:
                    sp.dma_start(dst, src).then_inc(sem("loaded"), 16)
                sp.wait_ge(sem("loaded"), 16 * len(loads))

            @block.gpsimd
            def _(pool):
                nc.gpsimd.memset(minus_half[:, :], -0.5).then_inc(sem("const"), 1)
                nc.gpsimd.memset(pad[:, :, :], 0.0).then_inc(sem("const"), 1)
                nc.gpsimd.memset(x[:, :, :, :], 0.0).then_inc(sem("const"), 1)
                pool.wait_ge(sem("const"), 3)
                pool.wait_ge(sem("bn_var"), 1)
                nc.gpsimd.tensor_tensor(bn[:, 3:4], bn[:, 2:3], minus_half[:, :], ALU.pow).then_inc(sem("bn_root"), 1)

            @block.vector
            def _(dve):
                dve.wait_ge(sem("loaded"), 16 * len(loads))
                link = Chain(dve, sem("dve_chain"))
                batch_norm_setup(nc, dve, link, sem, [cols[:, i:i + 1] for i in range(4)] and cols[:, :].unsqueeze(2),
                                 bn[:, :].unsqueeze(2), minus_half)
        st.clear()

        with nc.Fori(0, B) as b:
            with nc.Block() as block:

                @block.sync
                def _(sp):
                    for k in range(kc):
                        sp.dma_start(x[:, k, 1:SIDE + 1, 1:SIDE + 1], gathered[bass.ds(b * (kc * kp) + k * kp, kp), :]
                                     .rearrange("p (y w) -> p y w", w=SIDE)).then_inc(sem("x_loaded"), 16)
                    sp.wait_ge(sem("h_ready"), NH)
                    sp.dma_start(dense[bass.ds(b * CM, CM), :].rearrange("p (y w) -> p y w", w=SIDE),
                                 pad[:, 1:SIDE + 1, 1:SIDE + 1]).then_inc(sem("stored"), 16)
                    sp.wait_ge(sem("coords_ready"), 1)
                    for q in range(P // BLK):
                        y, half = divmod(q, 2)
                        sp.dma_start(coords[bass.ds(b * 2 + half, 1), y, :, :, :].rearrange("a s p n -> (a p) s n"),
                                     co.parts3[q * BLK:(q + 1) * BLK, 0, :, :]).then_inc(sem("coords_stored"), 16)
                    sp.wait_ge(sem("coords_stored"), 16 * (P // BLK))
                    sp.wait_ge(sem("stored"), 16)

                @block.scalar
                def _(act):
                    for j in range(NH):
                        act.wait_ge(sem("conv_ready"), j + 1)
                        nc.scalar.activation(padded_rows(pad, j, 4), ps[0:CM, j * HALF:(j + 1) * HALF]
                                             .rearrange("p (y w) -> p y w", w=SIDE), ACT.Identity, bias=bn[:, 1:2],
                                             scale=bn[:, 0:1]).then_inc(sem("h_ready"), 1)

                @block.vector
                def _(dve):
                    link = Chain(dve, sem("dve_chain"))
                    dve.wait_ge(sem("offsets_ready"), 1)
                    co.vector(nc, link, 0, ps[:, 2 * HALF:4 * HALF], ob[:, 0:1], grid[:, :]).then_inc(sem("coords_ready"), 1)

                @block.tensor
                def _(pe):
                    pe.wait_ge(sem("x_loaded"), 16 * kc)
                    for j in range(NH):
                        for i in range(kc * taps):
                            k, tap = divmod(i, taps)
                            ins = nc.tensor.matmul(ps[0:CM, j * HALF:(j + 1) * HALF], w[:, k, tap, :],
                                                   padded_rows(x[:, k], j, tap if taps == 9 else 4),
                                                   start=(i == 0), stop=(i == kc * taps - 1))
                        ins.then_inc(sem("conv_ready"), 1)
                    pe.wait_ge(sem("h_ready"), NH)
                    for j in range(NH):
                        for tap in range(9):
                            lo = (2 + j) * HALF
                            ins = nc.tensor.matmul(ps[:, lo:lo + HALF], ow[:, tap, :], padded_rows(pad, j, tap),
                                                   start=(tap == 0), stop=(tap == 8))
                    ins.then_inc(sem("offsets_ready"), 1)
            st.clear()


def build_last(nc, t, ps, xcur, gathered, out):
    with ExitStack() as ctx:
        st = Stage(nc, ctx, "l3")
        sem = st.sem
        w3 = st.sb("w3", [CM, C])
        wide = st.sb("wide", [P, KC, C])
        cols = st.sb("cols", [P, 4, KC])
        bn = st.sb("bn", [P, 4, KC])
        average = st.sb("average", [P, P])
        minus_half = st.sb("minus_half", [P, 4])
        x = st.sb("x", [P, KC, N])
        xn = st.sb("xn", [P, KC, N])
        stats = st.sb("stats", [P, KC, 6 * NH])
        moments = st.sb("moments", [P, KC, 8])
        h = st.sb("h", [CM, N])
        r = st.sb("r", [P, KC, N])
        loads = [
            (w3[:, :], t["w_4"]), (wide[:, :, :], t["wide"].rearrange("(k p) o -> p k o", p=P)),
            (cols[:, :, :], t["bn3"]), (average[:, :], t["average"]),
        ]
        with nc.Block() as block:

            @block.sync
            def _(sp):
                for dst, src in loads:
                    sp.dma_start(dst, src).then_inc(sem("loaded"), 16)
                sp.wait_ge(sem("loaded"), 16 * len(loads))

            @block.gpsimd
            def _(pool):
                nc.gpsimd.memset(minus_half[:, :], -0.5).then_inc(sem("const"), 1)
                pool.wait_ge(sem("const"), 1)
                pool.wait_ge(sem("bn_var"), 1)
                nc.gpsimd.tensor_tensor(bn[:, 3], bn[:, 2], minus_half[:, 0:KC], ALU.pow).then_inc(sem("bn_root"), 1)

            @block.vector
            def _(dve):
                dve.wait_ge(sem("loaded"), 16 * len(loads))
                link = Chain(dve, sem("dve_chain"))
                batch_norm_setup(nc, dve, link, sem, cols, bn, minus_half)
        st.clear()

        with nc.Fori(0, B) as b:
            with nc.Block() as block:

                @block.sync
                def _(sp):
                    sp.dma_start(h[:, :], gathered[bass.ds(b * CM, CM), :]).then_inc(sem("h_loaded"), 16)
                    sp.dma_start(x[:, :, :], image(xcur, b)).then_inc(sem("x_loaded"), 16)
                    sp.wait_ge(sem("new_x"), KC)
                    sp.dma_start(image(out, b), x[:, :, :]).then_inc(sem("stored"), 16)
                    sp.wait_ge(sem("stored"), 16)

                @block.gpsimd
                def _(pool):
                    norm_stats_pool(nc, pool, st, moments, minus_half)

                @block.scalar
                def _(act):
                    for m in range(KC):
                        act.wait_ge(sem("wide_ready"), m + 1)
                        nc.scalar.activation(r[:, m, :], ps[:, m * N:(m + 1) * N], ACT.Relu, bias=bn[:, 1, m:m + 1],
                                             scale=bn[:, 0, m:m + 1]).then_inc(sem("relu_ready"), 1)

                @block.vector
                def _(dve):
                    link = Chain(dve, sem("dve_chain"))
                    tt = nc.vector.tensor_tensor
                    dve.wait_ge(sem("x_loaded"), 16)
                    for m in range(KC):
                        dve.wait_ge(sem("relu_ready"), m + 1)
                        link(tt(x[:, m, :], x[:, m, :], r[:, m, :], ALU.add))
                    norm_stats_vector(nc, dve, st, link, x, stats, moments, ps[:, 7 * HALF:8 * HALF])
                    for k in range(KC):
                        normalise(nc, xn[:, k, :], x[:, k, :], moments, k).then_inc(sem("xn_ready"), 1)
                    for m in range(KC):
                        dve.wait_ge(sem("last_ready"), m + 1)
                        tt(x[:, m, :], ps[:, m * N:(m + 1) * N], x[:, m, :], ALU.add).then_inc(sem("new_x"), 1)

                @block.tensor
                def _(pe):
                    pe.wait_ge(sem("h_loaded"), 16)
                    for m in range(KC):
                        for j in range(NH):
                            lo = m * N + j * HALF
                            ins = nc.tensor.matmul(ps[:, lo:lo + HALF], w3[:, m * P:(m + 1) * P],
                                                   h[:, j * HALF:(j + 1) * HALF], start=True, stop=True)
                        ins.then_inc(sem("wide_ready"), 1)
                    norm_stats_tensor(nc, pe, st, moments, average, ps[:, 7 * HALF:8 * HALF])
                    pe.wait_ge(sem("xn_ready"), KC)
                    for m in range(KC):
                        for j in range(NH):
                            for k in range(KC):
                                lo = m * N + j * HALF
                                ins = nc.tensor.matmul(ps[:, lo:lo + HALF], wide[:, k, m * P:(m + 1) * P],
                                                       xn[:, k, j * HALF:(j + 1) * HALF], start=(k == 0), stop=(k == KC - 1))
                        ins.then_inc(sem("last_ready"), 1)
            st.clear()


LAYERS = "0123"


def kernel_program(nc, t, out):
    with ExitStack() as ctx:
        def dram(name, shape, dt=F32):
            return nc.dram_tensor(name, shape, dt, kind="Internal").ap()

        ps = ctx.enter_context(nc.psum_tensor("ps", [P, 8 * HALF], F32))
        xcur = dram("xcur", (B, C, N))
        if LAYERS == "0":
            return build_scan_layer(nc, t, ps, out)
        if LAYERS == "1":
            return build_expert_layer(nc, t, ps, t["x"], out)
        dense = dram("dense", (B * C, N))
        gathered = dram("gathered", (B * C, N))
        coords = dram("coords", (B * C // BLK, 2, 3, BLK, N), BF16)
        src = t["x"] if LAYERS == "23" else xcur
        if LAYERS == "0123":
            build_scan_layer(nc, t, ps, xcur)
            build_expert_layer(nc, t, ps, xcur, xcur)
        build_offsets_1(nc, t, ps, src, dense, coords)
        build_gather(nc, t, ps, dense, coords, gathered, B * C // BLK, "g1")
        build_middle(nc, t, ps, gathered, dense, coords, 2)
        build_gather(nc, t, ps, dense, coords, gathered, B * CM // BLK, "g2")
        build_middle(nc, t, ps, gathered, dense, coords, 3)
        build_gather(nc, t, ps, dense, coords, gathered, B * CM // BLK, "g3")
        build_last(nc, t, ps, src, gathered, out)


def constants():
    import numpy as np

    def ones_bf16(where):
        return where.astype(np.uint16) * np.uint16(0x3F80)

    tok = np.arange(N)
    lin = np.linspace(-1.0, 1.0, SIDE, dtype=np.float32)
    col = lambda v: np.ascontiguousarray(v.reshape(NT, P).T.astype(np.float32))
    gx, gy = lin[tok % SIDE], lin[tok // SIDE]
    p = np.arange(P)
    sel_rows = np.zeros((3 * ROWS, ROWS, P), np.float32)
    for q in range(ROWS):
        sel_rows[q::ROWS, q, :] = 1
    sel_experts = np.zeros((3 * E, E, P), np.float32)
    for e in range(E):
        sel_experts[e::E, e, :] = 1
    spread = np.zeros((3 * BLK, NG, P), np.float32)
    fold = np.zeros((P, NG, BLK), np.float32)
    for g in range(NG):
        for q in p:
            spread[4 * g + q // SIDE::BLK, g, q] = 1
            fold[q, g, 4 * g + q // SIDE] = 1
    return {
        "sel_experts": ones_bf16(sel_experts), "ident_bf16": ones_bf16(np.eye(P)),
        "index": np.arange(E, dtype=np.float32), "minus_index": -(p % SIDE).astype(np.float32).reshape(P, 1),
        "row_of": (tok // SIDE).astype(np.float32), "col_of": (tok % SIDE).astype(np.float32),
        "sel_spread": ones_bf16(spread), "sel_fold": fold,
        "grid_x": gx, "grid_y": gy, "grid_token": tok.astype(np.float32),
        "col_x": col(gx), "col_y": col(gy), "col_token": col(tok),
        "below": (p[None, :] < p[:, None]).astype(np.float32),
        "average": (p[None, :] // 8 == p[:, None] // 8).astype(np.float32) / 8,
        "ident": np.eye(P, dtype=np.float32),
        "sel_rows": ones_bf16(sel_rows),
    }


def kernel(**inputs):
    import numpy as np
    import concourse.bacc as bacc
    from concourse import mybir as _mybir
    from concourse.bass_utils import run_bass_kernel_spmd as _run

    nc = bacc.Bacc("TRN2", target_bir_lowering=False, num_devices=1)
    a = {k: np.asarray(v) for k, v in inputs.items()}
    sent = {
        "x": a["x"].reshape(B, C, N),
        "in_w": a["L0_conv_in_proj_w"].T, "out_w": a["L0_conv_out_proj_w"].T, "dbc_w": a["L0_conv_dbc_w"].T,
    }
    for name, key in (("in_b", "L0_conv_in_proj_b"), ("out_b", "L0_conv_out_proj_b"), ("dw_b", "L0_conv_dw_b")):
        sent[name] = a[key].reshape(-1, P).T
    for name in ("dw_w", "dbc_b", "A_log", "Dparam", "mobius"):
        sent[f"L0_conv_{name}"] = a[f"L0_conv_{name}"]
    for name in ("w1", "w2", "w3"):
        sent[name] = a[f"L1_conv_{name}"].transpose(2, 0, 1)
    sent["gate_w"] = a["L1_conv_gate_w"].T
    for n, cin in ((1, C), (2, CM), (3, CM)):
        v = a[f"L2_conv_ow{n}"].reshape(cin, 2, cin, 9).transpose(2, 3, 1, 0)
        o = a[f"L2_conv_ob{n}"].reshape(cin, 2)
        sent[f"ow{n}"] = v if n == 1 else v.reshape(cin, 9, 2 * cin)
        sent[f"ob{n}"] = o.reshape(KC, P, 2).transpose(1, 0, 2).reshape(P, 2 * KC) if n == 1 else o.T.reshape(P, 1)
    sent["w_2"] = a["L2_conv_w1"].reshape(CM, C, 1).transpose(1, 2, 0)
    sent["w_3"] = a["L2_conv_w2"].reshape(CM, CM, 9).transpose(1, 2, 0)
    sent["w_4"] = a["L2_conv_w3"].reshape(C, CM).T
    for n in (1, 2, 3):
        v = np.stack([a[f"L2_conv_{k}{n}"] for k in "gbmv"], 1)
        sent[f"bn{n}"] = v if n < 3 else v.reshape(KC, P, 4).transpose(1, 2, 0)
    lw = a["L3_conv_weights"]
    wide = np.zeros((C, C), lw.dtype)
    o, u = np.arange(C)[:, None], np.arange(lw.shape[1])[None, :]
    wide[(o * 32 + u) % C, np.broadcast_to(o, lw.shape)] = lw
    sent["wide"] = wide
    sent.update(constants())
    arrays, t = {}, {}
    for name, v in sent.items():
        v = np.ascontiguousarray(v)
        arrays[f"in_{name}"] = v
        t[name] = nc.dram_tensor(f"in_{name}", v.shape, _mybir.dt.from_np(v.dtype), kind="ExternalInput").ap()
    out = nc.dram_tensor("out_0", (B, C, N), F32, kind="ExternalOutput").ap()
    kernel_program(nc, t, out)
    r = _run(nc, [arrays], core_ids=[0])
    return np.asarray(r.results[0]["out_0"]).reshape(B, C, SIDE, SIDE)
```

```python
from contextlib import ExitStack

import concourse.bass as bass
from concourse import mybir

F32 = mybir.dt.float32
BF16 = mybir.dt.bfloat16
F32R = mybir.dt.float32r
ALU = mybir.AluOpType
ACT = mybir.ActivationFunctionType
AX = mybir.AxisListType.X

P = 128
B = 8
C = 256
KC = C // P
SIDE = 32
N = SIDE * SIDE
NT = N // P
HALF = 512
NH = N // HALF
PAD = SIDE + 2
HEADS = 2
S = 8
ROWS = 3 * S
DBC = 1 + 2 * S
E = 8
CM = 64
BLK = 32
NG = BLK // 4
UNITS = P // BLK
SETS = 2
IMGS = 2
EXPERT_IMGS = 4
PASS = 4
GN_EPS = 1e-5
BN_EPS = 1e-5


class Stage:

    def __init__(self, nc, ctx, tag):
        self.nc, self.ctx, self.tag, self.sems = nc, ctx, tag, {}

    def sb(self, name, shape, dt=F32):
        return self.ctx.enter_context(self.nc.sbuf_tensor(f"{self.tag}_{name}", shape, dt))

    def sem(self, name):
        if name not in self.sems:
            self.sems[name] = self.ctx.enter_context(self.nc.semaphore(f"{self.tag}_{name}"))
        return self.sems[name]

    def clear(self):
        for s in self.sems.values():
            self.nc.gpsimd.sem_clear(s)
        self.nc.all_engine_barrier()


class Chain:

    def __init__(self, eng, sem):
        self.eng, self.sem, self.n = eng, sem, 0

    def __call__(self, ins):
        self.n += 1
        ins.then_inc(self.sem, 1)
        self.eng.wait_ge(self.sem, self.n)



def norm_begin(nc, st, link, x, stats, moments):
    for k in range(KC):
        for h in range(NH):
            ins = nc.vector.bn_stats(stats[:, k, 6 * h:6 * h + 6], x[:, k, h * HALF:(h + 1) * HALF])
        link(ins)
    for k in range(KC):
        link(nc.vector.bn_aggr(moments[:, k, 0:2], stats[:, k, :]))
    nc.vector.tensor_copy(moments[:, 0:KC, 2], moments[:, 0:KC, 0]).then_inc(st.sem("means_ready"), 1)


def norm_spread(nc, dve, st, link, moments, psum, m=0):
    dve.wait_ge(st.sem("group_means"), m + 1)
    link(nc.vector.tensor_copy(moments[:, 0:KC, 3], psum[:, 0:KC]))
    link(nc.vector.tensor_tensor(moments[:, 0:KC, 4], moments[:, 0:KC, 0], moments[:, 0:KC, 3], ALU.subtract))
    link(nc.vector.tensor_tensor(moments[:, 0:KC, 4], moments[:, 0:KC, 4], moments[:, 0:KC, 4], ALU.mult))
    nc.vector.tensor_tensor(moments[:, 0:KC, 5], moments[:, 0:KC, 4], moments[:, 0:KC, 1],
                            ALU.add).then_inc(st.sem("spread_ready"), 1)


def norm_end(nc, dve, st, moments, psum, m=0):
    dve.wait_ge(st.sem("group_vars"), m + 1)
    nc.vector.tensor_scalar(moments[:, 0:KC, 6], psum[:, 8:8 + KC], GN_EPS, None,
                            ALU.add).then_inc(st.sem("var_eps"), 1)
    dve.wait_ge(st.sem("rstd"), m + 1)


def norm_stats_vector(nc, dve, st, link, x, stats, moments, psum, m=0):
    norm_begin(nc, st, link, x, stats, moments)
    norm_spread(nc, dve, st, link, moments, psum, m)
    norm_end(nc, dve, st, moments, psum, m)


def norm_means_tensor(nc, pe, st, moments, average, psum, m=0):
    pe.wait_ge(st.sem("means_ready"), m + 1)
    nc.tensor.matmul(psum[:, 0:KC], average[:, :], moments[:, 0:KC, 2], start=True,
                     stop=True).then_inc(st.sem("group_means"), 1)


def norm_vars_tensor(nc, pe, st, moments, average, psum, m=0):
    pe.wait_ge(st.sem("spread_ready"), m + 1)
    nc.tensor.matmul(psum[:, 8:8 + KC], average[:, :], moments[:, 0:KC, 5], start=True,
                     stop=True).then_inc(st.sem("group_vars"), 1)


def norm_stats_tensor(nc, pe, st, moments, average, psum, m=0):
    norm_means_tensor(nc, pe, st, moments, average, psum, m)
    norm_vars_tensor(nc, pe, st, moments, average, psum, m)


def norm_stats_pool(nc, pool, st, moments, minus_half, m=0):
    pool.wait_ge(st.sem("var_eps"), m + 1)
    nc.gpsimd.tensor_tensor(moments[:, 0:KC, 7], moments[:, 0:KC, 6], minus_half[:, 0:KC],
                            ALU.pow).then_inc(st.sem("rstd"), 1)


def normalise(nc, out, x, moments, k):
    return nc.vector.tensor_scalar(out, x, moments[:, k, 3:4], moments[:, k, 7:8], ALU.subtract, ALU.mult)


def split_vector(nc, link, parts, full, rest):
    link(nc.vector.tensor_copy(parts[0], full))
    link(nc.vector.tensor_tensor(rest, full, parts[0], ALU.subtract))
    link(nc.vector.tensor_copy(parts[1], rest))
    return nc.vector.tensor_tensor(parts[2], rest, parts[1], ALU.subtract)


def image(ap, b):
    return ap[bass.ds(b, 1), :, :].rearrange("a (k p) n -> (a p) k n", p=P)


def build_scan_layer(nc, t, ps, xcur):
    with ExitStack() as ctx:
        st = Stage(nc, ctx, "l0")
        sem = st.sem
        sel = st.sb("sel", [3 * ROWS, ROWS, P], BF16)
        forward = st.sb("forward", [P, HEADS, NT, N], BF16)
        backward = st.sb("backward", [P, HEADS, NT, N], BF16)
        average = st.sb("average", [P, P])
        ident = st.sb("ident", [P, P])
        minus_half = st.sb("minus_half", [P, 4])
        in_w = st.sb("in_w", [P, KC, 3 * C])
        out_w = st.sb("out_w", [P, KC, C])
        dbc_w = st.sb("dbc_w", [P, KC, HEADS * DBC])
        in_b = st.sb("in_b", [P, 6])
        out_b = st.sb("out_b", [P, KC])
        dw_w = st.sb("dw_w", [P, KC, 3])
        dw_b = st.sb("dw_b", [P, KC])
        dbc_b = st.sb("dbc_b", [P, HEADS * DBC])
        decay = st.sb("decay", [P, HEADS, S])
        skip = st.sb("skip", [P, HEADS])

        with ExitStack() as own:
            so = Stage(nc, own, "order")
            zx = so.sb("zx", [P, N + NT])
            zy = so.sb("zy", [P, N + NT])
            token = so.sb("token", [P, N + NT])
            below = so.sb("below", [P, P])
            ones = so.sb("ones", [P, P])
            mob = so.sb("mob", [P, HEADS * 4])
            sc = so.sb("sc", [P, HEADS, 8])
            w = [so.sb(f"w{i}", [P, N + NT]) for i in range(7)]
            score = so.sb("score", [P, N + NT])
            junk = so.sb("junk", [P, N])
            counts = so.sb("counts", [P, NT, 4])
            rank = so.sb("rank", [P, NT])
            diag = so.sb("diag", [P, NT, P])
            loaded, chain = so.sem("loaded"), so.sem("chain")
            loads = [
                (zx, t["grid_x"].partition_broadcast(P)), (zy, t["grid_y"].partition_broadcast(P)),
                (token, t["grid_token"].partition_broadcast(P)),
                (mob, t["L0_conv_mobius"].rearrange("h m -> (h m)").partition_broadcast(P)),
            ]
            cols = [(zx, "col_x"), (zy, "col_y"), (token, "col_token")]
            rest = [
                (below[:, :], t["below"]), (average[:, :], t["average"]), (ident[:, :], t["ident"]),
                (sel[:, :, :], t["sel_rows"].bitcast(BF16)),
                (in_w[:, :, :], t["in_w"].rearrange("(k p) o -> p k o", p=P)),
                (out_w[:, :, :], t["out_w"].rearrange("(k p) o -> p k o", p=P)),
                (dbc_w[:, :, :], t["dbc_w"].rearrange("(k p) o -> p k o", p=P)),
                (in_b[:, :], t["in_b"]),
                (out_b[:, :], t["out_b"]),
                (dw_w[:, :, :], t["L0_conv_dw_w"].rearrange("(k p) a w -> p k (a w)", p=P)),
                (dw_b[:, :], t["dw_b"]),
                (dbc_b[:, :], t["L0_conv_dbc_b"].partition_broadcast(P)),
                (decay[:, :, :], t["L0_conv_A_log"].rearrange("h s -> (h s)").partition_broadcast(P).rearrange("p (h s) -> p h s", h=HEADS)),
                (skip[:, :], t["L0_conv_Dparam"].partition_broadcast(P)),
            ]
            with nc.Block() as block:
                n_loads = len(loads) + len(cols) + len(rest)

                @block.sync
                def _(sp):
                    for dst, src in loads:
                        sp.dma_start(dst[:, 0:src.shape[-1]], src).then_inc(loaded, 16)
                    for dst, name in cols:
                        sp.dma_start(dst[:, N:N + NT], t[name]).then_inc(loaded, 16)
                    for dst, src in rest:
                        sp.dma_start(dst, src).then_inc(loaded, 16)
                    sp.wait_ge(loaded, 16 * n_loads)

                @block.scalar
                def _(act):
                    act.wait_ge(loaded, 16 * n_loads)
                    nc.scalar.activation(decay[:, :, :], decay[:, :, :], ACT.Exp).then_inc(so.sem("decay_exp"), 1)

                @block.gpsimd
                def _(pool):
                    nc.gpsimd.memset(minus_half[:, :], -0.5).then_inc(so.sem("const"), 1)
                    nc.gpsimd.memset(ones[:, :], 1.0).then_inc(so.sem("const"), 1)
                    nc.gpsimd.memset(sc[:, :, 5], 0.5).then_inc(so.sem("const"), 1)
                    pool.wait_ge(so.sem("const"), 3)
                    pool.wait_ge(so.sem("det"), 1)
                    nc.gpsimd.tensor_tensor(sc[:, :, 4], sc[:, :, 4], sc[:, :, 5], ALU.pow).then_inc(so.sem("root"), 1)

                @block.vector
                def _(dve):
                    link = Chain(dve, chain)
                    tt, ts, stt = nc.vector.tensor_tensor, nc.vector.tensor_scalar, nc.vector.scalar_tensor_tensor
                    dve.wait_ge(so.sem("const"), 3)
                    dve.wait_ge(loaded, 16 * n_loads)
                    m = mob[:, :].rearrange("p (h m) -> p h m", h=HEADS)
                    link(tt(sc[:, :, 0], m[:, :, 0], m[:, :, 3], ALU.mult))
                    link(tt(sc[:, :, 1], m[:, :, 1], m[:, :, 2], ALU.mult))
                    link(tt(sc[:, :, 4], sc[:, :, 0], sc[:, :, 1], ALU.subtract))
                    link(stt(sc[:, :, 4], sc[:, :, 4], -1.0, sc[:, :, 4], ALU.mult, ALU.max))
                    ts(sc[:, :, 4], sc[:, :, 4], 0.001, None, ALU.max).then_inc(so.sem("det"), 1)
                    dve.wait_ge(so.sem("root"), 1)
                    link(nc.vector.reciprocal(sc[:, :, 6], sc[:, :, 4]))
                    for j in range(4):
                        link(tt(sc[:, :, j], m[:, :, j], sc[:, :, 6], ALU.mult))
                    link(ts(sc[:, :, 3], sc[:, :, 3], 1e-6, None, ALU.add))
                    for h in range(HEADS):
                        a, b, c, d = (sc[:, h, j:j + 1] for j in range(4))
                        nr, ni, dr, di, u, v, den = (x[:, :] for x in w)
                        link(ts(nr, zx[:, :], a, b, ALU.mult, ALU.add))
                        link(ts(ni, zy[:, :], a, None, ALU.mult))
                        link(ts(dr, zx[:, :], c, d, ALU.mult, ALU.add))
                        link(ts(di, zy[:, :], c, None, ALU.mult))
                        link(tt(den, dr, dr, ALU.mult))
                        link(tt(u, di, di, ALU.mult))
                        link(tt(den, den, u, ALU.add))
                        link(nc.vector.reciprocal(den, den))
                        link(tt(u, nr, dr, ALU.mult))
                        link(tt(v, ni, di, ALU.mult))
                        link(tt(u, u, v, ALU.add))
                        link(tt(u, u, den, ALU.mult))
                        link(tt(v, ni, dr, ALU.mult))
                        link(tt(nr, nr, di, ALU.mult))
                        link(tt(v, v, nr, ALU.subtract))
                        link(tt(v, v, den, ALU.mult))
                        link(stt(score[:, :], v, 1.3, u, ALU.mult, ALU.add))
                        link(nc.vector.memset(counts[:, :, :], 0.0))
                        for c_ in range(NT):
                            mine = score[:, N + c_:N + c_ + 1]
                            lo, hi = c_ * P, (c_ + 1) * P
                            if c_:
                                link(ts(junk[:, 0:lo], score[:, 0:lo], mine, None, ALU.is_le, ALU.add,
                                        accum_out=counts[:, c_, 0:1]))
                            link(ts(junk[:, lo:N], score[:, lo:N], mine, None, ALU.is_lt, ALU.add,
                                    accum_out=counts[:, c_, 1:2]))
                            link(stt(junk[:, 0:P], score[:, lo:hi], mine, below[:, :], ALU.is_equal, ALU.mult))
                            link(nc.vector.tensor_reduce(counts[:, c_, 2:3], junk[:, 0:P], AX, ALU.add))
                        link(nc.vector.tensor_reduce(rank[:, :], counts[:, :, :], AX, ALU.add))
                        if h:
                            dve.wait_ge(so.sem("ranks_used"), h)
                        for c_ in range(NT):
                            link(ts(forward[:, h, c_, :], token[:, 0:N], rank[:, c_:c_ + 1], None, ALU.is_equal))
                            last = ts(diag[:, c_, :], ident[:, :], rank[:, c_:c_ + 1], None, ALU.mult)
                            link(last)
                        nc.vector.memset(junk[:, 0:1], 0.0).then_inc(so.sem("diag_ready"), 1)
                        dve.wait_ge(so.sem("ranks_used"), h + 1)
                        for c_ in range(NT):
                            link(ts(backward[:, h, c_, :], ps[:, 0:N], token[:, N + c_:N + c_ + 1], None, ALU.is_equal))
                    dve.wait_ge(so.sem("decay_exp"), 1)
                    link(ts(decay[:, :, :], decay[:, :, :], -1.0, None, ALU.mult))

                @block.tensor
                def _(pe):
                    pe.wait_ge(so.sem("const"), 3)
                    for h in range(HEADS):
                        pe.wait_ge(so.sem("diag_ready"), h + 1)
                        for c_ in range(NT):
                            ins = nc.tensor.matmul(ps[:, c_ * P:(c_ + 1) * P], ones[:, :], diag[:, c_, :],
                                                   start=True, stop=True)
                        ins.then_inc(so.sem("ranks_used"), 1)
            so.clear()

        x = st.sb("x", [P, KC, N])
        xn = st.sb("xn", [P, KC, N])
        stats = st.sb("stats", [P, KC, 6 * NH])
        moments = st.sb("moments", [P, KC, 8])
        ssm = st.sb("ssm", [P, KC, N + 2])
        res = st.sb("res", [P, KC, N])
        gate = st.sb("gate", [P, KC, N])
        xf = st.sb("xf", [P, KC, N])
        dbc = st.sb("dbc", [P, NT, HEADS, DBC])
        sp_t = st.sb("sp_t", [P, 6, NT, HEADS])
        rows = st.sb("rows", [P, NT, HEADS, ROWS])
        rows_rest = st.sb("rows_rest", [P, NT, HEADS, ROWS])
        rows3 = st.sb("rows3", [P, NT, HEADS, 3, ROWS], BF16)
        rows_p = st.sb("rows_p", [3 * ROWS, HEADS, N], BF16)
        xt3 = st.sb("xt3", [P, HEADS, 3, N], BF16)
        xp = st.sb("xp", [P, HEADS, N])
        dbx = st.sb("dbx", [P, 2, N])
        states = st.sb("states", [P, 2, N])
        seen = st.sb("seen", [P, 2, N])
        acc = st.sb("acc", [P, HEADS, N])
        rest_x = seen[:, 0, :]

        with nc.Fori(0, B) as b:
            with nc.Block() as block:

                @block.sync
                def _(sp):
                    sp.dma_start(x[:, :, :], image(t["x"], b)).then_inc(sem("x_loaded"), 16)
                    sp.wait_ge(sem("new_x"), KC)
                    sp.dma_start(image(xcur, b), x[:, :, :]).then_inc(sem("stored"), 16)
                    sp.wait_ge(sem("stored"), 16)

                @block.gpsimd
                def _(pool):
                    nc.gpsimd.memset(ssm[:, :, 0:1], 0.0).then_inc(sem("border"), 1)
                    nc.gpsimd.memset(ssm[:, :, N + 1:N + 2], 0.0).then_inc(sem("border"), 1)
                    norm_stats_pool(nc, pool, st, moments, minus_half)
                    for i in range(HEADS * S):
                        h, s = divmod(i, S)
                        pool.wait_ge(sem("seen_ready"), i + 1)
                        if s == 0:
                            ins = nc.gpsimd.tensor_copy(acc[:, h, :], seen[:, i % 2, :])
                        else:
                            pool.wait_ge(sem("summed"), i)
                            ins = nc.gpsimd.tensor_tensor(acc[:, h, :], acc[:, h, :], seen[:, i % 2, :], ALU.add)
                        ins.then_inc(sem("summed"), 1)

                @block.scalar
                def _(act):
                    link = Chain(act, sem("act_chain"))
                    parts = [ssm[:, 0, 1:N + 1], ssm[:, 1, 1:N + 1], res[:, 0, :], res[:, 1, :], gate[:, 0, :], gate[:, 1, :]]
                    for m in range(6):
                        act.wait_ge(sem("projected"), m + 1)
                        lo = (m % 2) * N
                        nc.scalar.activation(parts[m], ps[:, lo:lo + N], ACT.Silu,
                                             bias=in_b[:, m:m + 1]).then_inc(sem("part_ready"), 1)
                        if m in (2, 3):
                            k = m - 2
                            act.wait_ge(sem("conv_ready"), k + 1)
                            nc.scalar.activation(xf[:, k, :], xf[:, k, :], ACT.Silu,
                                                 bias=dw_b[:, k:k + 1]).then_inc(sem("xf_ready"), 1)
                    act.wait_ge(sem("part_ready"), 6)
                    for k in range(KC):
                        nc.scalar.activation(gate[:, k, :], gate[:, k, :], ACT.Silu).then_inc(sem("gate_ready"), 1)
                    act.wait_ge(sem("minus_abs"), 1)
                    nc.scalar.activation(sp_t[:, 1, :, :], sp_t[:, 0, :, :], ACT.Exp).then_inc(sem("soft_exp"), 1)
                    act.wait_ge(sem("one_plus"), 1)
                    nc.scalar.activation(sp_t[:, 3, :, :], sp_t[:, 2, :, :], ACT.Ln).then_inc(sem("soft_ln"), 1)
                    act.wait_ge(sem("dt_decay"), 1)
                    nc.scalar.activation(rows[:, :, :, 0:S], rows[:, :, :, 0:S], ACT.Exp).then_inc(sem("decay_ready"), 1)
                    for h in range(HEADS):
                        for j in range(NH):
                            act.wait_ge(sem("rows_moved"), h * NH + j + 1)
                            lo = (6 + j) * HALF
                            nc.scalar.activation(rows_p[:, h, j * HALF:(j + 1) * HALF], ps[0:3 * ROWS, lo:lo + HALF],
                                                 ACT.Copy).then_inc(sem("rows_p_ready"), 1)
                    for h in range(HEADS):
                        for j in range(NH):
                            act.wait_ge(sem("x_moved"), h * NH + j + 1)
                            lo = (6 + j) * HALF
                            nc.scalar.activation(xp[:, h, j * HALF:(j + 1) * HALF], ps[:, lo:lo + HALF],
                                                 ACT.Copy).then_inc(sem("xp_ready"), 1)
                    for m in range(KC):
                        act.wait_ge(sem("out_projected"), m + 1)
                        lo = m * N
                        nc.scalar.activation(xf[:, m, :], ps[:, lo:lo + N], ACT.Silu,
                                             bias=out_b[:, m:m + 1]).then_inc(sem("out_ready"), 1)

                @block.vector
                def _(dve):
                    link = Chain(dve, sem("dve_chain"))
                    tt, ts, stt = nc.vector.tensor_tensor, nc.vector.tensor_scalar, nc.vector.scalar_tensor_tensor
                    dve.wait_ge(sem("x_loaded"), 16)
                    norm_stats_vector(nc, dve, st, link, x, stats, moments, ps[:, 7 * HALF:8 * HALF])
                    for k in range(KC):
                        normalise(nc, xn[:, k, :], x[:, k, :], moments, k).then_inc(sem("xn_ready"), 1)
                    dve.wait_ge(sem("border"), 2)
                    for k in range(KC):
                        dve.wait_ge(sem("part_ready"), k + 1)
                        link(ts(xf[:, k, :], ssm[:, k, 0:N], dw_w[:, k, 0:1], None, ALU.mult))
                        link(stt(xf[:, k, :], ssm[:, k, 1:N + 1], dw_w[:, k, 1:2], xf[:, k, :], ALU.mult, ALU.add))
                        stt(xf[:, k, :], ssm[:, k, 2:N + 2], dw_w[:, k, 2:3], xf[:, k, :], ALU.mult,
                            ALU.add).then_inc(sem("conv_ready"), 1)
                    dve.wait_ge(sem("dbc_ready"), 1)
                    flat = dbc[:, :, :, :].rearrange("p t h r -> p t (h r)")
                    link(tt(flat, ps[:, 6 * HALF:6 * HALF + NT * HEADS * DBC].rearrange("p (t r) -> p t r", t=NT),
                            dbc_b[:, :].unsqueeze(1).to_broadcast([P, NT, HEADS * DBC]), ALU.add))
                    raw = dbc[:, :, :, 0]
                    stt(sp_t[:, 0, :, :], raw, -1.0, raw, ALU.mult, ALU.min).then_inc(sem("minus_abs"), 1)
                    dve.wait_ge(sem("soft_exp"), 1)
                    ts(sp_t[:, 2, :, :], sp_t[:, 1, :, :], 1.0, None, ALU.add).then_inc(sem("one_plus"), 1)
                    dve.wait_ge(sem("soft_ln"), 1)
                    link(ts(sp_t[:, 4, :, :], sp_t[:, 2, :, :], -1.0, None, ALU.add))
                    link(ts(sp_t[:, 5, :, :], sp_t[:, 4, :, :], 0.0, None, ALU.is_equal))
                    link(tt(sp_t[:, 4, :, :], sp_t[:, 4, :, :], sp_t[:, 5, :, :], ALU.add))
                    link(nc.vector.reciprocal(sp_t[:, 4, :, :], sp_t[:, 4, :, :]))
                    link(tt(sp_t[:, 3, :, :], sp_t[:, 3, :, :], sp_t[:, 5, :, :], ALU.add))
                    link(tt(sp_t[:, 3, :, :], sp_t[:, 3, :, :], sp_t[:, 1, :, :], ALU.mult))
                    link(tt(sp_t[:, 3, :, :], sp_t[:, 3, :, :], sp_t[:, 4, :, :], ALU.mult))
                    link(stt(sp_t[:, 0, :, :], raw, 0.0, sp_t[:, 3, :, :], ALU.max, ALU.add))
                    for h in range(HEADS):
                        dt = sp_t[:, 0, :, h].unsqueeze(2).to_broadcast([P, NT, S])
                        a = decay[:, h, :].unsqueeze(1).to_broadcast([P, NT, S])
                        link(tt(rows[:, :, h, 0:S], dt, a, ALU.mult))
                        link(tt(rows[:, :, h, S:2 * S], dt, dbc[:, :, h, 1:1 + S], ALU.mult))
                        link(nc.vector.tensor_copy(rows[:, :, h, 2 * S:3 * S], dbc[:, :, h, 1 + S:1 + 2 * S]))
                    nc.vector.memset(sp_t[:, 4, 0, 0:1], 0.0).then_inc(sem("dt_decay"), 1)
                    dve.wait_ge(sem("decay_ready"), 1)
                    split_vector(nc, link, [rows3[:, :, :, i, :] for i in range(3)], rows[:, :, :, :],
                                 rows_rest[:, :, :, :]).then_inc(sem("rows3_ready"), 1)
                    for h in range(HEADS):
                        dve.wait_ge(sem("x_turned"), h + 1)
                        lo = h * N
                        split_vector(nc, link, [xt3[:, h, i, :] for i in range(3)], ps[:, lo:lo + N],
                                     rest_x).then_inc(sem("xt3_ready"), 1)
                        dve.wait_ge(sem("xt3_ready"), h + 1)
                    for i in range(HEADS * S):
                        h, s = divmod(i, S)
                        if s == 0:
                            dve.wait_ge(sem("xp_ready"), NH * (h + 1))
                        dve.wait_ge(sem("db_spread"), i + 1)
                        tt(dbx[:, i % 2, :], ps[:, 2 * HALF:4 * HALF], xp[:, h, :], ALU.mult).then_inc(sem("db_used"), 1)
                        dve.wait_ge(sem("db_used"), i + 1)
                        dve.wait_ge(sem("da_spread"), i + 1)
                        nc.vector.tensor_tensor_scan(states[:, i % 2, :], ps[:, 0:2 * HALF], dbx[:, i % 2, :], 0.0,
                                                     ALU.mult, ALU.add).then_inc(sem("da_used"), 1)
                        dve.wait_ge(sem("da_used"), i + 1)
                        dve.wait_ge(sem("c_spread"), i + 1)
                        if i >= 2:
                            dve.wait_ge(sem("summed"), i - 1)
                        tt(seen[:, i % 2, :], ps[:, 4 * HALF:6 * HALF], states[:, i % 2, :],
                           ALU.mult).then_inc(sem("seen_ready"), 1)
                    dve.wait_ge(sem("summed"), HEADS * S)
                    for h in range(HEADS):
                        stt(acc[:, h, :], xp[:, h, :], skip[:, h:h + 1], acc[:, h, :], ALU.mult,
                            ALU.add).then_inc(sem("y_ready"), 1)
                    for h in range(HEADS):
                        dve.wait_ge(sem("y_turned"), h + 1)
                        lo = h * N
                        split_vector(nc, link, [xt3[:, h, i, :] for i in range(3)], ps[:, lo:lo + N],
                                     rest_x).then_inc(sem("yt3_ready"), 1)
                        dve.wait_ge(sem("yt3_ready"), h + 1)
                    for h in range(HEADS):
                        dve.wait_ge(sem("y_moved"), h + 1)
                        dve.wait_ge(sem("gate_ready"), KC)
                        lo = (4 + 2 * h) * HALF
                        link(tt(xn[:, h, :], ps[:, lo:lo + N], gate[:, h, :], ALU.mult))
                        tt(xn[:, h, :], xn[:, h, :], res[:, h, :], ALU.add).then_inc(sem("mixed"), 1)
                    for m in range(KC):
                        dve.wait_ge(sem("out_ready"), m + 1)
                        tt(x[:, m, :], x[:, m, :], xf[:, m, :], ALU.add).then_inc(sem("new_x"), 1)

                @block.tensor
                def _(pe):
                    norm_stats_tensor(nc, pe, st, moments, average, ps[:, 7 * HALF:8 * HALF])
                    pe.wait_ge(sem("xn_ready"), KC)
                    for m in range(6):
                        if m >= 2:
                            pe.wait_ge(sem("part_ready"), m - 1)
                        for j in range(NH):
                            for k in range(KC):
                                lo = (m % 2) * N + j * HALF
                                ins = nc.tensor.matmul(ps[:, lo:lo + HALF], in_w[:, k, m * P:(m + 1) * P],
                                                       xn[:, k, j * HALF:(j + 1) * HALF], start=(k == 0), stop=(k == KC - 1))
                        ins.then_inc(sem("projected"), 1)
                    pe.wait_ge(sem("xf_ready"), KC)
                    for c_ in range(NT):
                        for k in range(KC):
                            lo = 6 * HALF + c_ * HEADS * DBC
                            ins = nc.tensor.matmul(ps[:, lo:lo + HEADS * DBC], xf[:, k, c_ * P:(c_ + 1) * P],
                                                   dbc_w[:, k, :], start=(k == 0), stop=(k == KC - 1))
                    ins.then_inc(sem("dbc_ready"), 1)
                    pe.wait_ge(sem("part_ready"), 6)
                    for h in range(HEADS):
                        for c_ in range(NT):
                            lo = h * N + c_ * P
                            ins = nc.tensor.transpose(ps[:, lo:lo + P], xf[:, h, c_ * P:(c_ + 1) * P], ident[:, :])
                        ins.then_inc(sem("x_turned"), 1)
                    pe.wait_ge(sem("rows3_ready"), 1)
                    for h in range(HEADS):
                        for j in range(NH):
                            if h:
                                pe.wait_ge(sem("rows_p_ready"), j + 1)
                            lo = (6 + j) * HALF
                            for c_ in range(NT):
                                ins = nc.tensor.matmul(ps[0:3 * ROWS, lo:lo + HALF],
                                                       rows3[:, c_, h, :, :].rearrange("p a r -> p (a r)"),
                                                       forward[:, h, c_, j * HALF:(j + 1) * HALF],
                                                       start=(c_ == 0), stop=(c_ == NT - 1))
                            ins.then_inc(sem("rows_moved"), 1)
                    for h in range(HEADS):
                        pe.wait_ge(sem("xt3_ready"), h + 1)
                        for j in range(NH):
                            if h:
                                pe.wait_ge(sem("xp_ready"), j + 1)
                            else:
                                pe.wait_ge(sem("rows_p_ready"), NH + j + 1)
                            lo = (6 + j) * HALF
                            for c_ in range(NT):
                                for i in range(3):
                                    ins = nc.tensor.matmul(ps[:, lo:lo + HALF], xt3[:, h, i, c_ * P:(c_ + 1) * P],
                                                           forward[:, h, c_, j * HALF:(j + 1) * HALF],
                                                           start=(c_ == 0 and i == 0), stop=(c_ == NT - 1 and i == 2))
                            ins.then_inc(sem("x_moved"), 1)
                    for i in range(HEADS * S):
                        h, s = divmod(i, S)
                        for q, bank, ready, used in ((S + s, 2, "db_spread", "db_used"), (s, 0, "da_spread", "da_used"),
                                                     (2 * S + s, 4, "c_spread", "seen_ready")):
                            if i:
                                pe.wait_ge(sem(used), i)
                            for j in range(NH):
                                lo = (bank + j) * HALF
                                ins = nc.tensor.matmul(ps[:, lo:lo + HALF], sel[:, q, :],
                                                       rows_p[:, h, j * HALF:(j + 1) * HALF], start=True, stop=True)
                            ins.then_inc(sem(ready), 1)
                    pe.wait_ge(sem("seen_ready"), HEADS * S)
                    for h in range(HEADS):
                        pe.wait_ge(sem("y_ready"), h + 1)
                        for c_ in range(NT):
                            lo = h * N + c_ * P
                            ins = nc.tensor.transpose(ps[:, lo:lo + P], acc[:, h, c_ * P:(c_ + 1) * P], ident[:, :])
                        ins.then_inc(sem("y_turned"), 1)
                    for h in range(HEADS):
                        pe.wait_ge(sem("yt3_ready"), h + 1)
                        for j in range(NH):
                            lo = (4 + 2 * h + j) * HALF
                            for c_ in range(NT):
                                for i in range(3):
                                    ins = nc.tensor.matmul(ps[:, lo:lo + HALF], xt3[:, h, i, c_ * P:(c_ + 1) * P],
                                                           backward[:, h, c_, j * HALF:(j + 1) * HALF],
                                                           start=(c_ == 0 and i == 0), stop=(c_ == NT - 1 and i == 2))
                        ins.then_inc(sem("y_moved"), 1)
                    pe.wait_ge(sem("mixed"), HEADS)
                    for m in range(KC):
                        for j in range(NH):
                            for k in range(KC):
                                lo = m * N + j * HALF
                                ins = nc.tensor.matmul(ps[:, lo:lo + HALF], out_w[:, k, m * P:(m + 1) * P],
                                                       xn[:, k, j * HALF:(j + 1) * HALF], start=(k == 0), stop=(k == KC - 1))
                        ins.then_inc(sem("out_projected"), 1)
            st.clear()


def split_pair(nc, link, high, low, full):
    link(nc.vector.tensor_copy(high, full))
    return nc.vector.tensor_tensor(low, full, high.bitcast(F32), ALU.subtract)


PRODUCTS = ((0, 0), (0, 1), (1, 0))


def build_expert_layer(nc, t, ps, src, dst):
    with ExitStack() as ctx:
        st = Stage(nc, ctx, "l1")
        sem = st.sem
        w1, w3, w2 = (st.sb(n, [P, 2, KC, E, C], F32R) for n in ("w1", "w3", "w2"))
        gate_w = st.sb("gate_w", [P, KC, E])
        sel = st.sb("sel", [3 * E, E, P], BF16)
        average = st.sb("average", [P, P])
        ident = st.sb("ident", [P, P], BF16)
        minus_half = st.sb("minus_half", [P, 4])
        index = st.sb("index", [P, E])
        with ExitStack() as own:
            staged = own.enter_context(nc.sbuf_tensor("w_staged", [P, 2, KC, E, C], F32))
            loads = [
                (gate_w[:, :, :], t["gate_w"].rearrange("(k p) e -> p k e", p=P)),
                (sel[:, :, :], t["sel_experts"].bitcast(BF16)), (average[:, :], t["average"]),
                (ident[:, :], t["ident_bf16"].bitcast(BF16)), (index[:, :], t["index"].partition_broadcast(P)),
            ]
            weights = ((w1, "w1"), (w3, "w3"), (w2, "w2"))
            with nc.Block() as block:

                @block.sync
                def _(sp):
                    for i, (_, name) in enumerate(weights):
                        if i >= 2:
                            sp.wait_ge(sem("weights_split"), i - 1)
                        sp.dma_start(staged[:, i % 2], t[name].rearrange("(k p) e f -> p k e f", p=P))\
                          .then_inc(sem(f"staged{i}"), 16)
                    for to, of in loads:
                        sp.dma_start(to, of).then_inc(sem("loaded"), 16)
                    sp.wait_ge(sem("loaded"), 16 * len(loads))

                @block.vector
                def _(dve):
                    link = Chain(dve, sem("dve_chain"))
                    for i, (w, _) in enumerate(weights):
                        dve.wait_ge(sem(f"staged{i}"), 16)
                        split_pair(nc, link, w[:, 0], w[:, 1], staged[:, i % 2]).then_inc(sem("weights_split"), 1)
                    dve.wait_ge(sem("weights_split"), 3)

                @block.gpsimd
                def _(pool):
                    nc.gpsimd.memset(minus_half[:, :], -0.5).then_inc(sem("const"), 1)
                    pool.wait_ge(sem("const"), 1)
            st.clear()

        x = st.sb("x", [P, 2, KC, N])
        xn = st.sb("xn", [P, KC, N])
        pair = st.sb("pair", [P, 2, 2, KC, N], F32R)
        stats = st.sb("stats", [P, KC, 6 * NH])
        moments = st.sb("moments", [P, KC, 8])
        prob = st.sb("prob", [P, NT, E])
        left = st.sb("left", [P, NT, E])
        work = st.sb("work", [P, NT, E])
        first = st.sb("first", [P, NT, E])
        best = st.sb("best", [P, NT, 6])
        comb = st.sb("comb", [P, NT, E])
        comb_rest = st.sb("comb_rest", [P, NT, E])
        comb3 = st.sb("comb3", [P, NT, 3, E], BF16)
        comb_t = st.sb("comb_t", [3 * E, 2, N], BF16)
        weight = st.sb("weight", [P, 2, HALF])
        act1 = st.sb("act1", [P, 2, HALF])
        mixed = st.sb("mixed", [P, HALF])
        mixed2 = st.sb("mixed2", [P, 3, 2, HALF], F32R)

        steps = [(m, j, e, f) for m in range(EXPERT_IMGS) for j in range(NH) for e in range(E) for f in range(KC)]
        per = NH * E * KC
        bank = lambda i: ps[:, i * HALF:(i + 1) * HALF]
        small = bank(7)

        AT = {"begin": 8, "means": 10, "spread": 11, "vars": 12, "end": 13, "logits": 15, "shift": 16, "exp": 17,
              "choose": 18, "turn0": 21, "copy0": 22, "turn1": 23, "copy1": 24}

        def parts_at(i, parts):
            m, k = divmod(i, per)
            out = [(p, 0) for p in parts] if i == 0 else []
            if m + 1 < EXPERT_IMGS:
                out += [(p, m + 1) for p in parts if AT[p] == k]
            return out

        with nc.Fori(0, B // EXPERT_IMGS) as turn:
            b0 = turn * EXPERT_IMGS
            with nc.Block() as block:

                @block.sync
                def _(sp):
                    for m in range(EXPERT_IMGS + 1):
                        if m < EXPERT_IMGS:
                            if m >= 2:
                                sp.wait_ge(sem(f"stored{m - 2}"), 16)
                            sp.dma_start(x[:, m % 2], image(src, b0 + m)).then_inc(sem(f"x_loaded{m}"), 16)
                        if m:
                            sp.wait_ge(sem("new_x"), NH * KC * m)
                            sp.dma_start(image(dst, b0 + m - 1), x[:, (m - 1) % 2]).then_inc(sem(f"stored{m - 1}"), 16)
                    for m in range(max(0, EXPERT_IMGS - 2), EXPERT_IMGS):
                        sp.wait_ge(sem(f"stored{m}"), 16)

                @block.gpsimd
                def _(pool):
                    for m in range(EXPERT_IMGS):
                        norm_stats_pool(nc, pool, st, moments, minus_half, m)

                @block.scalar
                def _(act):
                    def router(part, m):
                        if part == "exp":
                            act.wait_ge(sem("shifted"), m + 1)
                            nc.scalar.activation(prob[:, :, :], prob[:, :, :], ACT.Exp).then_inc(sem("exped"), 1)
                        else:
                            h = int(part[-1])
                            act.wait_ge(sem("comb_turned"), 2 * m + h + 1)
                            nc.scalar.activation(comb_t[:, m % 2, h * HALF:(h + 1) * HALF], small[0:3 * E, :],
                                                 ACT.Copy).then_inc(sem("comb_t_ready"), 1)

                    for i, (m, j, e, f) in enumerate(steps):
                        for p in parts_at(i, ("exp", "copy0", "copy1")):
                            router(*p)
                        if f == 0:
                            act.wait_ge(sem("weight_spread"), i // KC + 1)
                            if i >= 2 * KC:
                                act.wait_ge(sem("mixed_ready"), i - KC)
                            nc.scalar.activation(weight[:, (i // KC) % 2, :], bank(4), ACT.Copy).then_inc(sem("weight_ready"), 1)
                        act.wait_ge(sem("up_ready"), i + 1)
                        if i >= 2:
                            act.wait_ge(sem("mixed_ready"), i - 1)
                        nc.scalar.activation(act1[:, i % 2, :], bank(i % 2), ACT.Gelu).then_inc(sem("gelu_ready"), 1)

                @block.vector
                def _(dve):
                    link = Chain(dve, sem("dve_chain"))
                    tt, ts, stt = nc.vector.tensor_tensor, nc.vector.tensor_scalar, nc.vector.scalar_tensor_tensor

                    def spread(v):
                        return v.unsqueeze(2).to_broadcast([P, NT, E])

                    def choose(m):
                        dve.wait_ge(sem("exped"), m + 1)
                        link(nc.vector.tensor_reduce(best[:, :, 1], prob[:, :, :], AX, ALU.add))
                        link(nc.vector.reciprocal(best[:, :, 1], best[:, :, 1]))
                        link(tt(prob[:, :, :], prob[:, :, :], spread(best[:, :, 1]), ALU.mult))
                        link(nc.vector.tensor_copy(left[:, :, :], prob[:, :, :]))
                        link(nc.vector.memset(comb[:, :, :], 0.0))
                        idx = index[:, :].unsqueeze(1).to_broadcast([P, NT, E])
                        for r in range(2):
                            link(nc.vector.tensor_reduce(best[:, :, 2 + r], left[:, :, :], AX, ALU.max))
                            link(tt(work[:, :, :], left[:, :, :], spread(best[:, :, 2 + r]), ALU.not_equal))
                            link(stt(work[:, :, :], work[:, :, :], float(E), idx, ALU.mult, ALU.add))
                            link(nc.vector.tensor_reduce(best[:, :, 4], work[:, :, :], AX, ALU.min))
                            link(tt(first[:, :, :], idx, spread(best[:, :, 4]), ALU.is_equal))
                            link(stt(left[:, :, :], first[:, :, :], -2.0, left[:, :, :], ALU.mult, ALU.add))
                            link(tt(first[:, :, :], first[:, :, :], prob[:, :, :], ALU.mult))
                            link(tt(comb[:, :, :], comb[:, :, :], first[:, :, :], ALU.add))
                        link(tt(best[:, :, 5], best[:, :, 2], best[:, :, 3], ALU.add))
                        link(nc.vector.reciprocal(best[:, :, 5], best[:, :, 5]))
                        link(tt(comb[:, :, :], comb[:, :, :], spread(best[:, :, 5]), ALU.mult))
                        split_vector(nc, link, [comb3[:, :, i, :] for i in range(3)], comb[:, :, :],
                                     comb_rest[:, :, :]).then_inc(sem("comb3_ready"), 1)

                    def router(part, m):
                        if part == "begin":
                            dve.wait_ge(sem(f"x_loaded{m}"), 16)
                            norm_begin(nc, st, link, x[:, m % 2], stats, moments)
                        elif part == "spread":
                            norm_spread(nc, dve, st, link, moments, small, m)
                        elif part == "end":
                            norm_end(nc, dve, st, moments, small, m)
                            for k in range(KC):
                                normalise(nc, xn[:, k, :], x[:, m % 2, k, :], moments, k).then_inc(sem("xn_ready"), 1)
                            dve.wait_ge(sem("xn_ready"), KC * (m + 1))
                            split_pair(nc, link, pair[:, m % 2, 0], pair[:, m % 2, 1], xn[:, :, :]).then_inc(sem("pair_ready"), 1)
                        elif part == "shift":
                            dve.wait_ge(sem("logits_ready"), m + 1)
                            logits = small[:, 64:64 + NT * E].rearrange("p (t e) -> p t e", t=NT)
                            link(nc.vector.tensor_reduce(best[:, :, 0], logits, AX, ALU.max))
                            tt(prob[:, :, :], logits, spread(best[:, :, 0]), ALU.subtract).then_inc(sem("shifted"), 1)
                        else:
                            choose(m)

                    def new_x(k):
                        m, j, _, _ = steps[k]
                        dve.wait_ge(sem("down_done"), k + 1)
                        for c in range(KC):
                            part = x[:, m % 2, c, j * HALF:(j + 1) * HALF]
                            nc.vector.tensor_tensor(part, bank(5 + c), part, ALU.add).then_inc(sem("new_x"), 1)

                    for i, (m, j, e, f) in enumerate(steps):
                        for p in parts_at(i, ("begin", "spread", "end", "shift", "choose")):
                            router(*p)
                        dve.wait_ge(sem("gelu_ready"), i + 1)
                        link(tt(act1[:, i % 2, :], bank(2 + i % 2), act1[:, i % 2, :], ALU.mult))
                        dve.wait_ge(sem("weight_ready"), i // KC + 1)
                        tt(mixed[:, :], act1[:, i % 2, :], weight[:, (i // KC) % 2, :], ALU.mult).then_inc(sem("mixed_ready"), 1)
                        dve.wait_ge(sem("mixed_ready"), i + 1)
                        if i >= 3:
                            dve.wait_ge(sem("down_done"), i - 2)
                        split_pair(nc, link, mixed2[:, i % 3, 0, :], mixed2[:, i % 3, 1, :], mixed[:, :])\
                            .then_inc(sem("split_ready"), 1)
                        dve.wait_ge(sem("split_ready"), i + 1)
                        k = i - 3
                        if k >= 0 and (k + 1) % (E * KC) == 0:
                            new_x(k)
                    new_x(len(steps) - 1)

                @block.tensor
                def _(pe):
                    def router(part, m):
                        if part == "means":
                            norm_means_tensor(nc, pe, st, moments, average, small, m)
                        elif part == "vars":
                            norm_vars_tensor(nc, pe, st, moments, average, small, m)
                        elif part == "logits":
                            pe.wait_ge(sem("xn_ready"), KC * (m + 1))
                            for c_ in range(NT):
                                for k in range(KC):
                                    lo = 64 + c_ * E
                                    ins = nc.tensor.matmul(small[:, lo:lo + E], xn[:, k, c_ * P:(c_ + 1) * P],
                                                           gate_w[:, k, :], start=(k == 0), stop=(k == KC - 1))
                            ins.then_inc(sem("logits_ready"), 1)
                        else:
                            h = int(part[-1])
                            pe.wait_ge(sem("comb3_ready"), m + 1)
                            if h:
                                pe.wait_ge(sem("comb_t_ready"), 2 * m + 1)
                            for c_ in range(NT // 2):
                                ins = nc.tensor.matmul(small[0:3 * E, c_ * P:(c_ + 1) * P],
                                                       comb3[:, h * NT // 2 + c_, :, :].rearrange("p a e -> p (a e)"),
                                                       ident[:, :], start=True, stop=True)
                            ins.then_inc(sem("comb_turned"), 1)

                    def up(i):
                        m, j, e, f = steps[i]
                        if i % per == 0:
                            pe.wait_ge(sem("pair_ready"), m + 1)
                        if f == 0:
                            pe.wait_ge(sem("comb_t_ready"), 2 * m + 2)
                            if i:
                                pe.wait_ge(sem("weight_ready"), i // KC)
                            nc.tensor.matmul(bank(4), sel[:, e, :], comb_t[:, m % 2, j * HALF:(j + 1) * HALF],
                                             start=True, stop=True).then_inc(sem("weight_spread"), 1)
                        if i >= 2:
                            pe.wait_ge(sem("mixed_ready"), i - 1)
                        for b_, w in ((0, w1), (2, w3)):
                            for k in range(KC):
                                for r, (a, c) in enumerate(PRODUCTS):
                                    ins = nc.tensor.matmul(bank(b_ + i % 2), w[:, a, k, e, f * P:(f + 1) * P],
                                                           pair[:, m % 2, c, k, j * HALF:(j + 1) * HALF],
                                                           start=(k == 0 and r == 0), stop=(k == KC - 1 and r == 2))
                        ins.then_inc(sem("up_ready"), 1)

                    def down(i):
                        m, j, e, f = steps[i]
                        pe.wait_ge(sem("split_ready"), i + 1)
                        if e == 0 and f == 0 and i:
                            pe.wait_ge(sem("new_x"), KC * (i // (E * KC)))
                        for c in range(KC):
                            for r, (a, d) in enumerate(PRODUCTS):
                                ins = nc.tensor.matmul(bank(5 + c), w2[:, a, f, e, c * P:(c + 1) * P], mixed2[:, i % 3, d, :],
                                                       start=(e == 0 and f == 0 and r == 0),
                                                       stop=(e == E - 1 and f == KC - 1 and r == 2))
                        ins.then_inc(sem("down_done"), 1)

                    for i in range(len(steps)):
                        for p in parts_at(i, ("means", "vars", "logits", "turn0", "turn1")):
                            router(*p)
                        up(i)
                        if i >= 2:
                            down(i - 2)
                    down(len(steps) - 2)
                    down(len(steps) - 1)
            st.clear()


class Coordinates:

    def __init__(self, st, parts):
        self.pos = st.sb("pos", [parts, N])
        self.parts2 = st.sb("parts2", [parts, 2, 2, N], F32R)

    def vector(self, nc, link, i, off, bias, grid):
        stt, ts = nc.vector.scalar_tensor_tensor, nc.vector.tensor_scalar
        high, low = (self.parts2[:, i % 2, j, :] for j in range(2))
        link(stt(self.pos[:, :], off, bias, grid, ALU.add, ALU.add))
        link(ts(self.pos[:, :], self.pos[:, :], 0.0, float(SIDE - 1), ALU.max, ALU.min))
        link(nc.vector.tensor_copy(high, self.pos[:, :]))
        return nc.vector.tensor_tensor(low, self.pos[:, :], high.bitcast(F32), ALU.subtract)

    def stored(self, q, i):
        return self.parts2[q * BLK:(q + 1) * BLK, i % 2, :, :].bitcast(F32)


def padded_rows(pad, j, tap):
    dy, dx = divmod(tap, 3)
    rows = HALF // SIDE
    return pad[:, j * rows + dy:j * rows + dy + rows, dx:dx + SIDE]


def build_offsets_1(nc, t, ps, xcur, dense, coords):
    with ExitStack() as ctx:
        st = Stage(nc, ctx, "o1")
        sem = st.sem
        ow = st.sb("ow", [P, 2, KC, 9, 2, C], F32R)
        ob = st.sb("ob", [P, 2 * KC])
        grid = st.sb("grid", [P, 2, N])
        average = st.sb("average", [P, P])
        minus_half = st.sb("minus_half", [P, 4])
        pad = st.sb("pad", [P, IMGS, 2, KC, PAD, PAD], F32R)
        with ExitStack() as own:
            staged = own.enter_context(nc.sbuf_tensor("ow_staged", [P, KC, 9, 2, C], F32))
            ow_src = t["ow1"].rearrange("(k p) a y c -> p k a y c", p=P)
            loads = [
                (staged[:, 0], ow_src[:, 0]), (staged[:, 1], ow_src[:, 1]), (ob[:, :], t["ob1"]),
                (grid[:, 0, :], t["row_of"].partition_broadcast(P)), (grid[:, 1, :], t["col_of"].partition_broadcast(P)),
                (average[:, :], t["average"]),
            ]
            with nc.Block() as block:

                @block.sync
                def _(sp):
                    for dst, src in loads:
                        sp.dma_start(dst, src).then_inc(sem("loaded"), 16)

                @block.vector
                def _(dve):
                    link = Chain(dve, sem("dve_chain"))
                    dve.wait_ge(sem("loaded"), 16 * len(loads))
                    link(split_pair(nc, link, ow[:, 0], ow[:, 1], staged[:, :, :, :, :]))

                @block.gpsimd
                def _(pool):
                    nc.gpsimd.memset(minus_half[:, :], -0.5).then_inc(sem("const"), 1)
                    nc.gpsimd.memset(pad[:, :, :, :, :, :].bitcast(F32), 0.0).then_inc(sem("const"), 1)
                    pool.wait_ge(sem("const"), 2)
            st.clear()

        x = st.sb("x", [P, IMGS, KC, N])
        stats = st.sb("stats", [P, KC, 6 * NH])
        moments = st.sb("moments", [P, KC, 8])
        co = Coordinates(st, P)
        kinds = [(m, k, y) for m in range(IMGS) for k in range(KC) for y in range(2)]
        with nc.Fori(0, B // IMGS) as turn:
            b0 = turn * IMGS
            with nc.Block() as block:

                @block.sync
                def _(sp):
                    for m in range(IMGS):
                        sp.dma_start(x[:, m], image(xcur, b0 + m)).then_inc(sem(f"x_loaded{m}"), 16)
                    for m in range(IMGS):
                        sp.wait_ge(sem("xn_ready"), KC * (m + 1))
                        sp.dma_start(dense[bass.ds((b0 + m) * C, C), :].rearrange("(k p) n -> p k n", p=P),
                                     x[:, m]).then_inc(sem("stored"), 16)
                    for i, (m, k, y) in enumerate(kinds):
                        sp.wait_ge(sem("coords_ready"), i + 1)
                        for q in range(P // BLK):
                            blk = (b0 + m) * (C // BLK) + k * (P // BLK) + q
                            sp.dma_start(coords[bass.ds(blk, 1), y, :, :, :].rearrange("a s p n -> (a p) s n"),
                                         co.stored(q, i)).then_inc(sem(f"coords_stored{i}"), 16)
                    for i in range(len(kinds)):
                        sp.wait_ge(sem(f"coords_stored{i}"), 16 * (P // BLK))
                    sp.wait_ge(sem("stored"), 16 * IMGS)

                @block.gpsimd
                def _(pool):
                    for m in range(IMGS):
                        norm_stats_pool(nc, pool, st, moments, minus_half, m)

                @block.vector
                def _(dve):
                    link = Chain(dve, sem("dve_chain"))
                    for m in range(IMGS):
                        dve.wait_ge(sem(f"x_loaded{m}"), 16)
                        norm_stats_vector(nc, dve, st, link, x[:, m], stats, moments, ps[:, 7 * HALF:8 * HALF], m)
                        for k in range(KC):
                            normalise(nc, x[:, m, k, :], x[:, m, k, :], moments, k).then_inc(sem("xn_ready"), 1)
                            dve.wait_ge(sem("xn_ready"), m * KC + k + 1)
                            inner = [pad[:, m, i, k, 1:SIDE + 1, 1:SIDE + 1] for i in range(2)]
                            split_pair(nc, link, inner[0], inner[1], x[:, m, k, :].rearrange("p (y w) -> p y w", w=SIDE))\
                                .then_inc(sem("split_ready"), 1)
                    for i, (m, k, y) in enumerate(kinds):
                        dve.wait_ge(sem("offsets_ready"), i + 1)
                        if i >= 2:
                            dve.wait_ge(sem(f"coords_stored{i - 2}"), 16 * (P // BLK))
                        lo = (i % 2) * N
                        col = 2 * k + y
                        co.vector(nc, link, i, ps[:, lo:lo + N], ob[:, col:col + 1], grid[:, y, :])\
                          .then_inc(sem("coords_ready"), 1)
                        dve.wait_ge(sem("coords_ready"), i + 1)

                @block.tensor
                def _(pe):
                    for i, (m, k, y) in enumerate(kinds):
                        if i < IMGS:
                            norm_stats_tensor(nc, pe, st, moments, average, ps[:, 7 * HALF:8 * HALF], i)
                        if k == 0 and y == 0:
                            pe.wait_ge(sem("split_ready"), KC * (m + 1))
                        if i >= 2:
                            pe.wait_ge(sem("coords_ready"), i - 1)
                        for j in range(NH):
                            lo = (i % 2) * N + j * HALF
                            for n in range(KC * 9):
                                kk, tap = divmod(n, 9)
                                for r, (a, c) in enumerate(PRODUCTS):
                                    ins = nc.tensor.matmul(ps[:, lo:lo + HALF], ow[:, a, kk, tap, y, k * P:(k + 1) * P],
                                                           padded_rows(pad[:, m, c, kk], j, tap), start=(n == 0 and r == 0),
                                                           stop=(n == KC * 9 - 1 and r == 2))
                        ins.then_inc(sem("offsets_ready"), 1)
            st.clear()


def build_gather(nc, t, ps, dense, coords, gathered, blocks, tag):
    with ExitStack() as ctx:
        st = Stage(nc, ctx, tag)
        sem = st.sem
        spread_f = st.sb("spread_f", [P, 2, NG, P])
        spread = st.sb("spread", [P, 2, NG, P], F32R)
        fold = st.sb("fold", [P, NG, BLK])
        index = st.sb("index", [P, 1])
        coord = st.sb("coord", [P, SETS, UNITS, N], F32R)
        img = st.sb("img", [P, SETS, UNITS * NG, P])
        WB, PB = 4, 8
        wts = st.sb("wts", [P, WB, 2, HALF])
        prod = st.sb("prod", [P, PB, HALF])
        res = st.sb("res", [P, 2, HALF])
        loads = [(spread_f[:, :, :, :], t["sel_spread"]), (fold[:, :, :], t["sel_fold"]), (index[:, :], t["minus_index"])]
        with nc.Block() as block:

            @block.sync
            def _(sp):
                for dst, src in loads:
                    sp.dma_start(dst, src).then_inc(sem("loaded"), 16)

            @block.vector
            def _(dve):
                dve.wait_ge(sem("loaded"), 16 * len(loads))
                nc.vector.tensor_copy(spread[:, :, :, :], spread_f[:, :, :, :]).then_inc(sem("spread_const"), 1)
                dve.wait_ge(sem("spread_const"), 1)

            @block.gpsimd
            def _(pool):
                nc.gpsimd.memset(img[:, :, :, :], 0.0).then_inc(sem("const"), 1)
                pool.wait_ge(sem("const"), 1)
        st.clear()

        steps = [(s, j, g, u) for s in range(SETS) for j in range(NH) for g in range(NG) for u in range(UNITS)]
        n = len(steps)
        per = NG * UNITS
        with nc.Fori(0, blocks // (SETS * UNITS)) as turn:
            n0 = turn * (SETS * UNITS)
            with nc.Block() as block:

                @block.sync
                def _(sp):
                    for s in range(SETS):
                        sp.dma_start(coord[:, s, :, :].bitcast(F32), coords[bass.ds(n0 + s * UNITS, UNITS), :, :, :, :]
                                     .rearrange("a y s p n -> (y s p) a n")).then_inc(sem(f"coord_loaded{s}"), 16)
                        src = dense[bass.ds((n0 + s * UNITS) * BLK, UNITS * BLK), :]\
                            .rearrange("(g c) (i j) -> c i g j", c=4, j=SIDE)
                        for c in range(4):
                            sp.dma_start(img[c * SIDE:(c + 1) * SIDE, s, :, c * SIDE:(c + 1) * SIDE],
                                         src[c]).then_inc(sem(f"img_loaded{s}"), 16)
                    for r in range(SETS * NH):
                        s, j = divmod(r, NH)
                        sp.wait_ge(sem("res_ready"), r + 1)
                        sp.dma_start(gathered[bass.ds((n0 + s * UNITS) * BLK, P), j * HALF:(j + 1) * HALF],
                                     res[:, r % 2, :]).then_inc(sem(f"stored{r}"), 16)
                    for r in range(SETS * NH):
                        sp.wait_ge(sem(f"stored{r}"), 16)

                @block.scalar
                def _(act):
                    def evacuate(r):
                        act.wait_ge(sem("folded"), NG * (r + 1))
                        if r >= 2:
                            act.wait_ge(sem(f"stored{r - 2}"), 16)
                        nc.scalar.activation(res[:, r % 2, :], ps[:, (6 + r % 2) * HALF:(7 + r % 2) * HALF],
                                             ACT.Copy).then_inc(sem("res_ready"), 1)

                    for i in range(n):
                        act.wait_ge(sem("spread_ready"), i + 1)
                        if i >= WB:
                            act.wait_ge(sem("weighted"), i - WB + 1)
                        lo = 2 * (i % 2) * HALF
                        nc.scalar.activation(wts[:, i % WB, :, :].rearrange("p y n -> p (y n)"), ps[:, lo:lo + 2 * HALF],
                                             ACT.Abs, bias=index[:, 0:1]).then_inc(sem("distance_ready"), 1)
                        if i % per == 8 and i > per:
                            evacuate(i // per - 1)
                    evacuate(SETS * NH - 1)

                @block.vector
                def _(dve):
                    for i in range(n + 1):
                        if i < n:
                            dve.wait_ge(sem("distance_ready"), i + 1)
                            nc.vector.tensor_scalar(wts[:, i % WB, :, :], wts[:, i % WB, :, :], 1.0, -1.0, ALU.min,
                                                    ALU.add).then_inc(sem("weights_ready"), 1)
                        if i:
                            k = i - 1
                            dve.wait_ge(sem("weights_ready"), i)
                            dve.wait_ge(sem("rows_summed"), k + 1)
                            if k >= PB:
                                dve.wait_ge(sem("folded"), (k - PB) // UNITS + 1)
                            nc.vector.tensor_tensor(prod[:, k % PB, :], ps[:, (4 + k % 2) * HALF:(5 + k % 2) * HALF],
                                                    wts[:, k % WB, 1, :], ALU.mult).then_inc(sem("weighted"), 1)

                @block.tensor
                def _(pe):
                    def spread_step(i):
                        s, j, g, u = steps[i]
                        if i % (per * NH) == 0:
                            pe.wait_ge(sem(f"coord_loaded{s}"), 16)
                        if i >= 2:
                            pe.wait_ge(sem("distance_ready"), i - 1)
                        for y in range(2):
                            lo = (2 * (i % 2) + y) * HALF
                            ins = nc.tensor.matmul(ps[:, lo:lo + HALF], spread[:, y, g, :],
                                                   coord[:, s, u, j * HALF:(j + 1) * HALF],
                                                   start=True, stop=True)
                        ins.then_inc(sem("spread_ready"), 1)

                    def rows_step(i):
                        s, j, g, u = steps[i]
                        if i % (per * NH) == 0:
                            pe.wait_ge(sem(f"img_loaded{s}"), 64)
                        pe.wait_ge(sem("weights_ready"), i + 1)
                        if i >= 2:
                            pe.wait_ge(sem("weighted"), i - 1)
                        lo = (4 + i % 2) * HALF
                        nc.tensor.matmul(ps[:, lo:lo + HALF], img[:, s, u * NG + g, :], wts[:, i % WB, 0, :], start=True,
                                         stop=True).then_inc(sem("rows_summed"), 1)

                    def fold_steps(q):
                        r, g = divmod(q, NG)
                        pe.wait_ge(sem("weighted"), UNITS * (q + 1))
                        if g == 0 and r >= 2:
                            pe.wait_ge(sem("res_ready"), r - 1)
                        lo = (6 + r % 2) * HALF
                        for u in range(UNITS):
                            ins = nc.tensor.matmul(ps[u * BLK:(u + 1) * BLK, lo:lo + HALF], fold[:, g, :],
                                                   prod[:, (UNITS * q + u) % PB, :], start=(g == 0), stop=(g == NG - 1))
                        ins.then_inc(sem("folded"), 1)

                    spread_step(0)
                    spread_step(1)
                    for i in range(n):
                        if i + 2 < n:
                            spread_step(i + 2)
                        rows_step(i)
                        if i % UNITS == 1 and i > UNITS:
                            fold_steps(i // UNITS - 1)
                    fold_steps(n // UNITS - 1)
            st.clear()


def batch_norm_setup(nc, dve, link, sem, cols, out, minus_half):
    link(nc.vector.tensor_scalar(out[:, 2], cols[:, 3], BN_EPS, None, ALU.add))
    nc.vector.tensor_scalar(out[:, 2], out[:, 2], 1.0, None, ALU.mult).then_inc(sem("bn_var"), 1)
    dve.wait_ge(sem("bn_root"), 1)
    link(nc.vector.tensor_tensor(out[:, 0], cols[:, 0], out[:, 3], ALU.mult))
    link(nc.vector.tensor_tensor(out[:, 1], cols[:, 2], out[:, 0], ALU.mult))
    link(nc.vector.tensor_tensor(out[:, 1], cols[:, 1], out[:, 1], ALU.subtract))


def stacked_taps():
    return [(dx, 0, P) for dx in range(3)] + [(dx, 2, CM) for dx in range(3)]


def stacked_conv(nc, weights, stack, out, concurrent):
    for i, (dx, dy, rows) in enumerate(stacked_taps()):
        for j in range(NH):
            if rows == P or concurrent:
                base, lift = 0, 0
            else:
                base, lift = j * CM, j
            y0 = j * (HALF // SIDE) + dy - lift
            ins = nc.tensor.matmul(out[j], weights[base:base + rows, i, :],
                                   stack[base:base + rows, y0:y0 + HALF // SIDE, dx:dx + SIDE],
                                   start=(i == 0), stop=(i == 5), skip_group_check=True)
    return ins


def build_middle(nc, t, ps, gathered, dense, coords, n):
    with ExitStack() as ctx:
        st = Stage(nc, ctx, f"o{n}")
        sem = st.sem
        w = st.sb("w", [P, KC, CM] if n == 2 else [P, 6, CM])
        ow = st.sb("ow", [P, 6, P])
        ob = st.sb("ob", [P, 1])
        cols = st.sb("cols", [P, 4])
        bn = st.sb("bn", [P, 4])
        grid = st.sb("grid", [P, N])
        minus_half = st.sb("minus_half", [P, 1])
        x = st.sb("x", [P, PASS, KC, N] if n == 2 else [P, PASS, PAD, PAD])
        stack = st.sb("stack", [P, PASS, PAD, PAD])
        co = Coordinates(st, P)
        loads = [
            (w[:, :, :], t[f"w_{n}"].rearrange("(k p) c -> p k c", p=P) if n == 2 else t["w_3"]),
            (ow[:, :, :], t[f"ow{n}"]), (ob[:, :], t[f"ob{n}"]),
            (cols[0:CM, :], t[f"bn{n - 1}"]), (cols[CM:P, :], t[f"bn{n - 1}"]),
            (grid[0:CM, :], t["row_of"].partition_broadcast(CM)), (grid[CM:P, :], t["col_of"].partition_broadcast(CM)),
        ]
        with nc.Block() as block:

            @block.sync
            def _(sp):
                for dst, src in loads:
                    sp.dma_start(dst, src).then_inc(sem("loaded"), 16)

            @block.gpsimd
            def _(pool):
                nc.gpsimd.memset(minus_half[:, :], -0.5).then_inc(sem("const"), 1)
                nc.gpsimd.memset(stack[:, :, :, :], 0.0).then_inc(sem("const"), 1)
                if n == 3:
                    nc.gpsimd.memset(x[:, :, :, :], 0.0).then_inc(sem("const"), 1)
                pool.wait_ge(sem("const"), n)
                pool.wait_ge(sem("bn_var"), 1)
                nc.gpsimd.tensor_tensor(bn[:, 3:4], bn[:, 2:3], minus_half[:, :], ALU.pow).then_inc(sem("bn_root"), 1)

            @block.vector
            def _(dve):
                dve.wait_ge(sem("loaded"), 16 * len(loads))
                link = Chain(dve, sem("dve_chain"))
                batch_norm_setup(nc, dve, link, sem, cols[:, :].unsqueeze(2), bn[:, :].unsqueeze(2), minus_half)
        st.clear()

        rows = HALF // SIDE
        with nc.Fori(0, B // PASS) as turn:
            b0 = turn * PASS
            with nc.Block() as block:

                @block.sync
                def _(sp):
                    for m in range(PASS):
                        b = b0 + m
                        if n == 2:
                            sp.dma_start(x[:, m], gathered[bass.ds(b * C, C), :].rearrange("(k p) n -> p k n", p=P))\
                              .then_inc(sem(f"x_loaded{m}"), 16)
                        else:
                            src = gathered[bass.ds(b * CM, CM), :].rearrange("p (y w) -> p y w", w=SIDE)
                            for r in range(2):
                                sp.dma_start(x[r * CM:(r + 1) * CM, m, 1 - r:SIDE + 1 - r, 1:SIDE + 1], src)\
                                  .then_inc(sem(f"x_loaded{m}"), 16)
                    for m in range(PASS):
                        b = b0 + m
                        sp.wait_ge(sem("h_ready"), 4 * (m + 1))
                        sp.dma_start(dense[bass.ds(b * CM, CM), :].rearrange("p (y w) -> p y w", w=SIDE),
                                     stack[0:CM, m, 1:SIDE + 1, 1:SIDE + 1]).then_inc(sem("stored"), 16)
                        sp.wait_ge(sem("coords_ready"), m + 1)
                        for q in range(P // BLK):
                            y, half = divmod(q, 2)
                            sp.dma_start(coords[bass.ds(b * 2 + half, 1), y, :, :, :].rearrange("a s p n -> (a p) s n"),
                                         co.stored(q, m)).then_inc(sem(f"coords_stored{m}"), 16)
                    for m in range(PASS):
                        sp.wait_ge(sem(f"coords_stored{m}"), 16 * (P // BLK))
                    sp.wait_ge(sem("stored"), 16 * PASS)

                @block.scalar
                def _(act):
                    for m in range(PASS):
                        act.wait_ge(sem("conv_ready"), m + 1)
                        lo = (m % 2) * HALF
                        for j in range(NH):
                            for r in range(2):
                                part = slice(j * CM, (j + 1) * CM)
                                y0 = j * rows + 1 - r
                                nc.scalar.activation(stack[r * CM:(r + 1) * CM, m, y0:y0 + rows, 1:SIDE + 1],
                                                     ps[part, lo:lo + HALF].rearrange("p (y w) -> p y w", w=SIDE),
                                                     ACT.Identity, bias=bn[part, 1:2],
                                                     scale=bn[part, 0:1]).then_inc(sem("h_ready"), 1)

                @block.vector
                def _(dve):
                    link = Chain(dve, sem("dve_chain"))
                    for m in range(PASS):
                        dve.wait_ge(sem("offsets_ready"), m + 1)
                        if m >= 2:
                            dve.wait_ge(sem(f"coords_stored{m - 2}"), 16 * (P // BLK))
                        lo = (4 + 2 * (m % 2)) * HALF
                        co.vector(nc, link, m, ps[:, lo:lo + N], ob[:, 0:1], grid[:, :]).then_inc(sem("coords_ready"), 1)
                        dve.wait_ge(sem("coords_ready"), m + 1)

                @block.tensor
                def _(pe):
                    def conv(m):
                        pe.wait_ge(sem(f"x_loaded{m}"), 16 if n == 2 else 32)
                        if m >= 2:
                            pe.wait_ge(sem("h_ready"), 4 * (m - 1))
                        lo = (m % 2) * HALF
                        halves = [ps[j * CM:(j + 1) * CM, lo:lo + HALF] for j in range(NH)]
                        if n == 2:
                            for k in range(KC):
                                for j in range(NH):
                                    ins = nc.tensor.matmul(halves[j], w[:, k, :], x[:, m, k, j * HALF:(j + 1) * HALF],
                                                           start=(k == 0), stop=(k == KC - 1), skip_group_check=True)
                        else:
                            ins = stacked_conv(nc, w, x[:, m], halves, True)
                        ins.then_inc(sem("conv_ready"), 1)

                    def offsets(m):
                        pe.wait_ge(sem("h_ready"), 4 * (m + 1))
                        if m >= 2:
                            pe.wait_ge(sem("coords_ready"), m - 1)
                        lo = (4 + 2 * (m % 2)) * HALF
                        halves = [ps[:, lo + j * HALF:lo + (j + 1) * HALF] for j in range(NH)]
                        stacked_conv(nc, ow, stack[:, m], halves, False).then_inc(sem("offsets_ready"), 1)

                    conv(0)
                    for m in range(PASS):
                        if m + 1 < PASS:
                            conv(m + 1)
                        offsets(m)
            st.clear()


def build_last(nc, t, ps, xcur, gathered, out):
    with ExitStack() as ctx:
        st = Stage(nc, ctx, "l3")
        sem = st.sem
        w3 = st.sb("w3", [CM, C])
        wide = st.sb("wide", [P, KC, C])
        cols = st.sb("cols", [P, 4, KC])
        bn = st.sb("bn", [P, 4, KC])
        average = st.sb("average", [P, P])
        minus_half = st.sb("minus_half", [P, 4])
        x = st.sb("x", [P, KC, N])
        xn = st.sb("xn", [P, KC, N])
        stats = st.sb("stats", [P, KC, 6 * NH])
        moments = st.sb("moments", [P, KC, 8])
        h = st.sb("h", [CM, N])
        r = st.sb("r", [P, KC, N])
        loads = [
            (w3[:, :], t["w_4"]), (wide[:, :, :], t["wide"].rearrange("(k p) o -> p k o", p=P)),
            (cols[:, :, :], t["bn3"]), (average[:, :], t["average"]),
        ]
        with nc.Block() as block:

            @block.sync
            def _(sp):
                for dst, src in loads:
                    sp.dma_start(dst, src).then_inc(sem("loaded"), 16)
                sp.wait_ge(sem("loaded"), 16 * len(loads))

            @block.gpsimd
            def _(pool):
                nc.gpsimd.memset(minus_half[:, :], -0.5).then_inc(sem("const"), 1)
                pool.wait_ge(sem("const"), 1)
                pool.wait_ge(sem("bn_var"), 1)
                nc.gpsimd.tensor_tensor(bn[:, 3], bn[:, 2], minus_half[:, 0:KC], ALU.pow).then_inc(sem("bn_root"), 1)

            @block.vector
            def _(dve):
                dve.wait_ge(sem("loaded"), 16 * len(loads))
                link = Chain(dve, sem("dve_chain"))
                batch_norm_setup(nc, dve, link, sem, cols, bn, minus_half)
        st.clear()

        with nc.Fori(0, B) as b:
            with nc.Block() as block:

                @block.sync
                def _(sp):
                    sp.dma_start(h[:, :], gathered[bass.ds(b * CM, CM), :]).then_inc(sem("h_loaded"), 16)
                    sp.dma_start(x[:, :, :], image(xcur, b)).then_inc(sem("x_loaded"), 16)
                    sp.wait_ge(sem("new_x"), KC)
                    sp.dma_start(image(out, b), x[:, :, :]).then_inc(sem("stored"), 16)
                    sp.wait_ge(sem("stored"), 16)

                @block.gpsimd
                def _(pool):
                    norm_stats_pool(nc, pool, st, moments, minus_half)

                @block.scalar
                def _(act):
                    for m in range(KC):
                        act.wait_ge(sem("wide_ready"), m + 1)
                        nc.scalar.activation(r[:, m, :], ps[:, m * N:(m + 1) * N], ACT.Relu, bias=bn[:, 1, m:m + 1],
                                             scale=bn[:, 0, m:m + 1]).then_inc(sem("relu_ready"), 1)

                @block.vector
                def _(dve):
                    link = Chain(dve, sem("dve_chain"))
                    tt = nc.vector.tensor_tensor
                    dve.wait_ge(sem("x_loaded"), 16)
                    for m in range(KC):
                        dve.wait_ge(sem("relu_ready"), m + 1)
                        link(tt(x[:, m, :], x[:, m, :], r[:, m, :], ALU.add))
                    norm_stats_vector(nc, dve, st, link, x, stats, moments, ps[:, 7 * HALF:8 * HALF])
                    for k in range(KC):
                        normalise(nc, xn[:, k, :], x[:, k, :], moments, k).then_inc(sem("xn_ready"), 1)
                    for m in range(KC):
                        dve.wait_ge(sem("last_ready"), m + 1)
                        tt(x[:, m, :], ps[:, m * N:(m + 1) * N], x[:, m, :], ALU.add).then_inc(sem("new_x"), 1)

                @block.tensor
                def _(pe):
                    pe.wait_ge(sem("h_loaded"), 16)
                    for m in range(KC):
                        for j in range(NH):
                            lo = m * N + j * HALF
                            ins = nc.tensor.matmul(ps[:, lo:lo + HALF], w3[:, m * P:(m + 1) * P],
                                                   h[:, j * HALF:(j + 1) * HALF], start=True, stop=True)
                        ins.then_inc(sem("wide_ready"), 1)
                    norm_stats_tensor(nc, pe, st, moments, average, ps[:, 7 * HALF:8 * HALF])
                    pe.wait_ge(sem("xn_ready"), KC)
                    for m in range(KC):
                        for j in range(NH):
                            for k in range(KC):
                                lo = m * N + j * HALF
                                ins = nc.tensor.matmul(ps[:, lo:lo + HALF], wide[:, k, m * P:(m + 1) * P],
                                                       xn[:, k, j * HALF:(j + 1) * HALF], start=(k == 0), stop=(k == KC - 1))
                        ins.then_inc(sem("last_ready"), 1)
            st.clear()


LAYERS = "0123"


def kernel_program(nc, t, out):
    with ExitStack() as ctx:
        def dram(name, shape, dt=F32):
            return nc.dram_tensor(name, shape, dt, kind="Internal").ap()

        ps = ctx.enter_context(nc.psum_tensor("ps", [P, 8 * HALF], F32))
        xcur = dram("xcur", (B, C, N))
        if LAYERS == "0":
            return build_scan_layer(nc, t, ps, out)
        if LAYERS == "1":
            return build_expert_layer(nc, t, ps, t["x"], out)
        dense = dram("dense", (B * C, N))
        gathered = dram("gathered", (B * C, N))
        coords = dram("coords", (B * C // BLK, 2, 2, BLK, N))
        src = t["x"] if LAYERS == "23" else xcur
        if LAYERS == "0123":
            build_scan_layer(nc, t, ps, xcur)
            build_expert_layer(nc, t, ps, xcur, xcur)
        build_offsets_1(nc, t, ps, src, dense, coords)
        build_gather(nc, t, ps, dense, coords, gathered, B * C // BLK, "g1")
        build_middle(nc, t, ps, gathered, dense, coords, 2)
        build_gather(nc, t, ps, dense, coords, gathered, B * CM // BLK, "g2")
        build_middle(nc, t, ps, gathered, dense, coords, 3)
        build_gather(nc, t, ps, dense, coords, gathered, B * CM // BLK, "g3")
        build_last(nc, t, ps, src, gathered, out)


def constants():
    import numpy as np

    def ones_bf16(where):
        return where.astype(np.uint16) * np.uint16(0x3F80)

    tok = np.arange(N)
    lin = np.linspace(-1.0, 1.0, SIDE, dtype=np.float32)
    col = lambda v: np.ascontiguousarray(v.reshape(NT, P).T.astype(np.float32))
    gx, gy = lin[tok % SIDE], lin[tok // SIDE]
    p = np.arange(P)
    sel_rows = np.zeros((3 * ROWS, ROWS, P), np.float32)
    for q in range(ROWS):
        sel_rows[q::ROWS, q, :] = 1
    sel_experts = np.zeros((3 * E, E, P), np.float32)
    for e in range(E):
        sel_experts[e::E, e, :] = 1
    spread = np.zeros((P, 2, NG, P), np.float32)
    fold = np.zeros((P, NG, BLK), np.float32)
    for g in range(NG):
        for q in p:
            for y in range(2):
                spread[y * 2 * BLK + 4 * g + q // SIDE:(y + 1) * 2 * BLK:BLK, y, g, q] = 1
            fold[q, g, 4 * g + q // SIDE] = 1
    return {
        "sel_experts": ones_bf16(sel_experts), "ident_bf16": ones_bf16(np.eye(P)),
        "index": np.arange(E, dtype=np.float32), "minus_index": -(p % SIDE).astype(np.float32).reshape(P, 1),
        "row_of": (tok // SIDE).astype(np.float32), "col_of": (tok % SIDE).astype(np.float32),
        "sel_spread": spread, "sel_fold": fold,
        "grid_x": gx, "grid_y": gy, "grid_token": tok.astype(np.float32),
        "col_x": col(gx), "col_y": col(gy), "col_token": col(tok),
        "below": (p[None, :] < p[:, None]).astype(np.float32),
        "average": (p[None, :] // 8 == p[:, None] // 8).astype(np.float32) / 8,
        "ident": np.eye(P, dtype=np.float32),
        "sel_rows": ones_bf16(sel_rows),
    }


def kernel(**inputs):
    import numpy as np
    import concourse.bacc as bacc
    from concourse import mybir as _mybir
    from concourse.bass_utils import run_bass_kernel_spmd as _run

    nc = bacc.Bacc("TRN2", target_bir_lowering=False, num_devices=1)
    a = {k: np.asarray(v) for k, v in inputs.items()}
    sent = {
        "x": a["x"].reshape(B, C, N),
        "in_w": a["L0_conv_in_proj_w"].T, "out_w": a["L0_conv_out_proj_w"].T, "dbc_w": a["L0_conv_dbc_w"].T,
    }
    for name, key in (("in_b", "L0_conv_in_proj_b"), ("out_b", "L0_conv_out_proj_b"), ("dw_b", "L0_conv_dw_b")):
        sent[name] = a[key].reshape(-1, P).T
    for name in ("dw_w", "dbc_b", "A_log", "Dparam", "mobius"):
        sent[f"L0_conv_{name}"] = a[f"L0_conv_{name}"]

    def stacked(w):
        w = w.reshape(CM, 3, 3, -1)
        return np.concatenate([np.concatenate([w[:, 0], w[:, 1]], 0), np.concatenate([w[:, 2], w[:, 2]], 0)], 1)

    for name in ("w1", "w2", "w3"):
        sent[name] = a[f"L1_conv_{name}"].transpose(2, 0, 1)
    sent["gate_w"] = a["L1_conv_gate_w"].T
    for n, cin in ((1, C), (2, CM), (3, CM)):
        v = a[f"L2_conv_ow{n}"].reshape(cin, 2, cin, 9).transpose(2, 3, 1, 0)
        o = a[f"L2_conv_ob{n}"].reshape(cin, 2)
        sent[f"ow{n}"] = v if n == 1 else stacked(v.reshape(cin, 9, 2 * cin))
        sent[f"ob{n}"] = o.reshape(KC, P, 2).transpose(1, 0, 2).reshape(P, 2 * KC) if n == 1 else o.T.reshape(P, 1)
    sent["w_2"] = a["L2_conv_w1"].reshape(CM, C).T
    sent["w_3"] = stacked(a["L2_conv_w2"].reshape(CM, CM, 9).transpose(1, 2, 0))
    sent["w_4"] = a["L2_conv_w3"].reshape(C, CM).T
    for n in (1, 2, 3):
        v = np.stack([a[f"L2_conv_{k}{n}"] for k in "gbmv"], 1)
        sent[f"bn{n}"] = v if n < 3 else v.reshape(KC, P, 4).transpose(1, 2, 0)
    lw = a["L3_conv_weights"]
    wide = np.zeros((C, C), lw.dtype)
    o, u = np.arange(C)[:, None], np.arange(lw.shape[1])[None, :]
    wide[(o * 32 + u) % C, np.broadcast_to(o, lw.shape)] = lw
    sent["wide"] = wide
    sent.update(constants())
    arrays, t = {}, {}
    for name, v in sent.items():
        v = np.ascontiguousarray(v)
        arrays[f"in_{name}"] = v
        t[name] = nc.dram_tensor(f"in_{name}", v.shape, _mybir.dt.from_np(v.dtype), kind="ExternalInput").ap()
    out = nc.dram_tensor("out_0", (B, C, N), F32, kind="ExternalOutput").ap()
    kernel_program(nc, t, out)
    r = _run(nc, [arrays], core_ids=[0])
    return np.asarray(r.results[0]["out_0"]).reshape(B, C, SIDE, SIDE)
```

```python
from contextlib import ExitStack

import concourse.bass as bass
from concourse import mybir

F32 = mybir.dt.float32
BF16 = mybir.dt.bfloat16
F32R = mybir.dt.float32r
ALU = mybir.AluOpType
ACT = mybir.ActivationFunctionType
AX = mybir.AxisListType.X

P = 128
B = 8
C = 256
KC = C // P
SIDE = 32
N = SIDE * SIDE
NT = N // P
HALF = 512
NH = N // HALF
PAD = SIDE + 2
HEADS = 2
S = 8
ROWS = 3 * S
DBC = 1 + 2 * S
E = 8
CM = 64
BLK = 32
NG = BLK // 4
UNITS = P // BLK
SETS = 4
IMGS = 4
EXPERT_IMGS = 4
LAST_IMGS = 4
PASS = 4
GN_EPS = 1e-5
BN_EPS = 1e-5


class Stage:

    def __init__(self, nc, ctx, tag):
        self.nc, self.ctx, self.tag, self.sems = nc, ctx, tag, {}

    def sb(self, name, shape, dt=F32):
        return self.ctx.enter_context(self.nc.sbuf_tensor(f"{self.tag}_{name}", shape, dt))

    def sem(self, name):
        if name not in self.sems:
            self.sems[name] = self.ctx.enter_context(self.nc.semaphore(f"{self.tag}_{name}"))
        return self.sems[name]

    def clear(self):
        for s in self.sems.values():
            self.nc.gpsimd.sem_clear(s)
        self.nc.all_engine_barrier()


class Chain:

    def __init__(self, eng, sem):
        self.eng, self.sem, self.n = eng, sem, 0

    def __call__(self, ins):
        self.n += 1
        ins.then_inc(self.sem, 1)
        self.eng.wait_ge(self.sem, self.n)



def norm_begin(nc, st, link, x, stats, moments):
    for k in range(KC):
        for h in range(NH):
            ins = nc.vector.bn_stats(stats[:, k, 6 * h:6 * h + 6], x[:, k, h * HALF:(h + 1) * HALF])
        link(ins)
    for k in range(KC):
        link(nc.vector.bn_aggr(moments[:, k, 0:2], stats[:, k, :]))
    nc.vector.tensor_copy(moments[:, 0:KC, 2], moments[:, 0:KC, 0]).then_inc(st.sem("means_ready"), 1)


def norm_spread(nc, dve, st, link, moments, psum, m=0):
    dve.wait_ge(st.sem("group_means"), m + 1)
    link(nc.vector.tensor_copy(moments[:, 0:KC, 3], psum[:, 0:KC]))
    link(nc.vector.tensor_tensor(moments[:, 0:KC, 4], moments[:, 0:KC, 0], moments[:, 0:KC, 3], ALU.subtract))
    link(nc.vector.tensor_tensor(moments[:, 0:KC, 4], moments[:, 0:KC, 4], moments[:, 0:KC, 4], ALU.mult))
    nc.vector.tensor_tensor(moments[:, 0:KC, 5], moments[:, 0:KC, 4], moments[:, 0:KC, 1],
                            ALU.add).then_inc(st.sem("spread_ready"), 1)


def norm_end(nc, dve, st, moments, psum, m=0):
    dve.wait_ge(st.sem("group_vars"), m + 1)
    nc.vector.tensor_scalar(moments[:, 0:KC, 6], psum[:, 8:8 + KC], GN_EPS, None,
                            ALU.add).then_inc(st.sem("var_eps"), 1)
    dve.wait_ge(st.sem("rstd"), m + 1)


def norm_stats_vector(nc, dve, st, link, x, stats, moments, psum, m=0):
    norm_begin(nc, st, link, x, stats, moments)
    norm_spread(nc, dve, st, link, moments, psum, m)
    norm_end(nc, dve, st, moments, psum, m)


def norm_means_tensor(nc, pe, st, moments, average, psum, m=0):
    pe.wait_ge(st.sem("means_ready"), m + 1)
    nc.tensor.matmul(psum[:, 0:KC], average[:, :], moments[:, 0:KC, 2], start=True,
                     stop=True).then_inc(st.sem("group_means"), 1)


def norm_vars_tensor(nc, pe, st, moments, average, psum, m=0):
    pe.wait_ge(st.sem("spread_ready"), m + 1)
    nc.tensor.matmul(psum[:, 8:8 + KC], average[:, :], moments[:, 0:KC, 5], start=True,
                     stop=True).then_inc(st.sem("group_vars"), 1)


def norm_stats_tensor(nc, pe, st, moments, average, psum, m=0):
    norm_means_tensor(nc, pe, st, moments, average, psum, m)
    norm_vars_tensor(nc, pe, st, moments, average, psum, m)


def norm_stats_pool(nc, pool, st, moments, minus_half, m=0):
    pool.wait_ge(st.sem("var_eps"), m + 1)
    nc.gpsimd.tensor_tensor(moments[:, 0:KC, 7], moments[:, 0:KC, 6], minus_half[:, 0:KC],
                            ALU.pow).then_inc(st.sem("rstd"), 1)


def normalise(nc, out, x, moments, k):
    return nc.vector.tensor_scalar(out, x, moments[:, k, 3:4], moments[:, k, 7:8], ALU.subtract, ALU.mult)


def split_vector(nc, link, parts, full, rest):
    link(nc.vector.tensor_copy(parts[0], full))
    link(nc.vector.tensor_tensor(rest, full, parts[0], ALU.subtract))
    link(nc.vector.tensor_copy(parts[1], rest))
    return nc.vector.tensor_tensor(parts[2], rest, parts[1], ALU.subtract)


def image(ap, b):
    return ap[bass.ds(b, 1), :, :].rearrange("a (k p) n -> (a p) k n", p=P)


def build_scan_layer(nc, t, ps, xcur):
    with ExitStack() as ctx:
        st = Stage(nc, ctx, "l0")
        sem = st.sem
        sel = st.sb("sel", [3 * ROWS, ROWS, P], BF16)
        forward = st.sb("forward", [P, HEADS, NT, N], BF16)
        backward = st.sb("backward", [P, HEADS, NT, N], BF16)
        average = st.sb("average", [P, P])
        ident = st.sb("ident", [P, P])
        minus_half = st.sb("minus_half", [P, 4])
        in_w = st.sb("in_w", [P, KC, 3 * C])
        out_w = st.sb("out_w", [P, KC, C])
        dbc_w = st.sb("dbc_w", [P, KC, HEADS * DBC])
        in_b = st.sb("in_b", [P, 6])
        out_b = st.sb("out_b", [P, KC])
        dw_w = st.sb("dw_w", [P, KC, 3])
        dw_b = st.sb("dw_b", [P, KC])
        dbc_b = st.sb("dbc_b", [P, HEADS * DBC])
        decay = st.sb("decay", [P, HEADS, S])
        skip = st.sb("skip", [P, HEADS])

        with ExitStack() as own:
            so = Stage(nc, own, "order")
            zx = so.sb("zx", [P, NT])
            zy = so.sb("zy", [P, NT])
            token_col = so.sb("token_col", [P, NT])
            token = so.sb("token", [P, N])
            below = so.sb("below", [P, P])
            ones = so.sb("ones", [P, P])
            mob = so.sb("mob", [P, HEADS * 4])
            sc = so.sb("sc", [P, HEADS, 8])
            w = [so.sb(f"w{i}", [P, HEADS, NT]) for i in range(8)]
            score = so.sb("score", [P, HEADS, NT])
            row = so.sb("row", [P, 2, HEADS, N])
            junk = so.sb("junk", [P, N])
            counts = so.sb("counts", [P, NT, 4])
            rank = so.sb("rank", [P, HEADS, NT])
            diag = so.sb("diag", [P, HEADS, NT, P])
            loaded, chain = so.sem("loaded"), so.sem("chain")
            loads = [
                (zx, t["col_x"]), (zy, t["col_y"]), (token_col, t["col_token"]),
                (token, t["grid_token"].partition_broadcast(P)),
                (mob, t["L0_conv_mobius"].rearrange("h m -> (h m)").partition_broadcast(P)),
            ]
            rest = [
                (below[:, :], t["below"]), (average[:, :], t["average"]), (ident[:, :], t["ident"]),
                (sel[:, :, :], t["sel_rows"].bitcast(BF16)),
                (in_w[:, :, :], t["in_w"].rearrange("(k p) o -> p k o", p=P)),
                (out_w[:, :, :], t["out_w"].rearrange("(k p) o -> p k o", p=P)),
                (dbc_w[:, :, :], t["dbc_w"].rearrange("(k p) o -> p k o", p=P)),
                (in_b[:, :], t["in_b"]),
                (out_b[:, :], t["out_b"]),
                (dw_w[:, :, :], t["L0_conv_dw_w"].rearrange("(k p) a w -> p k (a w)", p=P)),
                (dw_b[:, :], t["dw_b"]),
                (dbc_b[:, :], t["L0_conv_dbc_b"].partition_broadcast(P)),
                (decay[:, :, :], t["L0_conv_A_log"].rearrange("h s -> (h s)").partition_broadcast(P).rearrange("p (h s) -> p h s", h=HEADS)),
                (skip[:, :], t["L0_conv_Dparam"].partition_broadcast(P)),
            ]
            with nc.Block() as block:

                @block.sync
                def _(sp):
                    for dst, src in loads:
                        sp.dma_start(dst[:, :], src).then_inc(so.sem("grid_loaded"), 16)
                    for dst, src in rest:
                        sp.dma_start(dst, src).then_inc(loaded, 16)
                    sp.wait_ge(loaded, 16 * len(rest))

                @block.scalar
                def _(act):
                    act.wait_ge(loaded, 16 * len(rest))
                    nc.scalar.activation(decay[:, :, :], decay[:, :, :], ACT.Exp).then_inc(so.sem("decay_exp"), 1)
                    for n in range(2 * HEADS):
                        act.wait_ge(so.sem("row_spread"), n + 1)
                        kind, h = divmod(n, HEADS)
                        nc.scalar.activation(row[:, kind, h, :], ps[:, n * N:(n + 1) * N],
                                             ACT.Copy).then_inc(so.sem("row_ready"), 1)

                @block.gpsimd
                def _(pool):
                    nc.gpsimd.memset(minus_half[:, :], -0.5).then_inc(so.sem("const"), 1)
                    nc.gpsimd.memset(ones[:, :], 1.0).then_inc(so.sem("const"), 1)
                    nc.gpsimd.memset(sc[:, :, 5], 0.5).then_inc(so.sem("const"), 1)
                    pool.wait_ge(so.sem("const"), 3)
                    pool.wait_ge(so.sem("det"), 1)
                    nc.gpsimd.tensor_tensor(sc[:, :, 4], sc[:, :, 4], sc[:, :, 5], ALU.pow).then_inc(so.sem("root"), 1)

                @block.vector
                def _(dve):
                    link = Chain(dve, chain)
                    tt, ts, stt = nc.vector.tensor_tensor, nc.vector.tensor_scalar, nc.vector.scalar_tensor_tensor
                    dve.wait_ge(so.sem("const"), 3)
                    dve.wait_ge(so.sem("grid_loaded"), 16 * len(loads))
                    m = mob[:, :].rearrange("p (h m) -> p h m", h=HEADS)
                    link(tt(sc[:, :, 0], m[:, :, 0], m[:, :, 3], ALU.mult))
                    link(tt(sc[:, :, 1], m[:, :, 1], m[:, :, 2], ALU.mult))
                    link(tt(sc[:, :, 4], sc[:, :, 0], sc[:, :, 1], ALU.subtract))
                    link(stt(sc[:, :, 4], sc[:, :, 4], -1.0, sc[:, :, 4], ALU.mult, ALU.max))
                    ts(sc[:, :, 4], sc[:, :, 4], 0.001, None, ALU.max).then_inc(so.sem("det"), 1)
                    dve.wait_ge(so.sem("root"), 1)
                    link(nc.vector.reciprocal(sc[:, :, 6], sc[:, :, 4]))
                    for j in range(4):
                        link(tt(sc[:, :, j], m[:, :, j], sc[:, :, 6], ALU.mult))
                    link(ts(sc[:, :, 3], sc[:, :, 3], 1e-6, None, ALU.add))
                    a, b, c, d = (sc[:, :, j:j + 1].to_broadcast([P, HEADS, NT]) for j in range(4))
                    gx, gy = (z[:, :].unsqueeze(1).to_broadcast([P, HEADS, NT]) for z in (zx, zy))
                    nr, ni, dr, di, u, v, den, top = (x[:, :, :] for x in w)
                    link(tt(nr, gx, a, ALU.mult))
                    link(tt(nr, nr, b, ALU.add))
                    link(tt(ni, gy, a, ALU.mult))
                    link(tt(dr, gx, c, ALU.mult))
                    link(tt(dr, dr, d, ALU.add))
                    link(tt(di, gy, c, ALU.mult))
                    link(tt(den, dr, dr, ALU.mult))
                    link(tt(u, di, di, ALU.mult))
                    link(tt(den, den, u, ALU.add))
                    link(nc.vector.reciprocal(den, den))
                    link(tt(u, nr, dr, ALU.mult))
                    link(tt(v, ni, di, ALU.mult))
                    link(tt(u, u, v, ALU.add))
                    link(tt(u, u, den, ALU.mult))
                    link(tt(v, ni, dr, ALU.mult))
                    link(tt(top, nr, di, ALU.mult))
                    link(tt(v, v, top, ALU.subtract))
                    link(tt(v, v, den, ALU.mult))
                    link(stt(score[:, :, :], v, 1.3, u, ALU.mult, ALU.add))
                    link(ts(score[:, :, :], score[:, :, :], 3e38, -3e38, ALU.min, ALU.max))
                    link(nc.vector.memset(counts[:, :, :], 0.0))
                    dve.wait_ge(loaded, 16 * len(rest))
                    for h in range(HEADS):
                        for c_ in range(NT):
                            ins = ts(diag[:, h, c_, :], ident[:, :], score[:, h, c_:c_ + 1], None, ALU.mult)
                        ins.then_inc(so.sem("diag_ready"), 1)
                    for h in range(HEADS):
                        dve.wait_ge(so.sem("row_ready"), h + 1)
                        for c_ in range(NT):
                            mine = score[:, h, c_:c_ + 1]
                            lo, hi = c_ * P, (c_ + 1) * P
                            if c_:
                                link(ts(junk[:, 0:lo], row[:, 0, h, 0:lo], mine, None, ALU.is_le, ALU.add,
                                        accum_out=counts[:, c_, 0:1]))
                            link(ts(junk[:, lo:N], row[:, 0, h, lo:N], mine, None, ALU.is_lt, ALU.add,
                                    accum_out=counts[:, c_, 1:2]))
                            link(stt(junk[:, 0:P], row[:, 0, h, lo:hi], mine, below[:, :], ALU.is_equal, ALU.mult))
                            link(nc.vector.tensor_reduce(counts[:, c_, 2:3], junk[:, 0:P], AX, ALU.add))
                        link(nc.vector.tensor_reduce(rank[:, h, :], counts[:, :, :], AX, ALU.add))
                        for c_ in range(NT):
                            ins = ts(diag[:, h, c_, :], ident[:, :], rank[:, h, c_:c_ + 1], None, ALU.mult)
                        ins.then_inc(so.sem("diag_ready"), 1)
                        for c_ in range(NT):
                            ts(forward[:, h, c_, :], token[:, :], rank[:, h, c_:c_ + 1], None,
                               ALU.is_equal).then_inc(so.sem("forward_ready"), 1)
                    for h in range(HEADS):
                        dve.wait_ge(so.sem("row_ready"), HEADS + h + 1)
                        for c_ in range(NT):
                            ts(backward[:, h, c_, :], row[:, 1, h, :], token_col[:, c_:c_ + 1], None,
                               ALU.is_equal).then_inc(so.sem("backward_ready"), 1)
                    dve.wait_ge(so.sem("decay_exp"), 1)
                    link(ts(decay[:, :, :], decay[:, :, :], -1.0, None, ALU.mult))

                @block.tensor
                def _(pe):
                    pe.wait_ge(so.sem("const"), 3)
                    for n in range(2 * HEADS):
                        pe.wait_ge(so.sem("diag_ready"), n + 1)
                        for c_ in range(NT):
                            ins = nc.tensor.matmul(ps[:, n * N + c_ * P:n * N + (c_ + 1) * P], ones[:, :],
                                                   diag[:, n % HEADS, c_, :], start=True, stop=True)
                        ins.then_inc(so.sem("row_spread"), 1)
            so.clear()

        xn = st.sb("xn", [P, KC, N])
        stats = st.sb("stats", [P, KC, 6 * NH])
        moments = st.sb("moments", [P, KC, 8])
        xf = st.sb("xf", [P, KC, N])
        dbc = st.sb("dbc", [P, NT, HEADS, DBC])
        sp_t = st.sb("sp_t", [P, 6, NT, HEADS])
        rows = st.sb("rows", [P, NT, HEADS, ROWS])
        rows_rest = st.sb("rows_rest", [P, NT, HEADS, ROWS])
        rows3 = st.sb("rows3", [P, NT, HEADS, 3, ROWS], BF16)
        turned = st.sb("turned", [P, N])
        ssm_xt3 = st.sb("ssm_xt3", [P, HEADS * 3 * N // 2])
        ssm = ssm_xt3[:, HEADS * 3 * N // 2 - KC * (N + 2):].rearrange("p (k n) -> p k n", k=KC)
        xt3 = ssm_xt3[:, :].bitcast(BF16).rearrange("p (h a n) -> p h a n", h=HEADS, a=3)
        res = st.sb("res", [P, 2, KC, N])
        gate = st.sb("gate", [P, 2, KC, N])
        rows_p = st.sb("rows_p", [3 * ROWS, 2, HEADS, N], BF16)
        xp = st.sb("xp", [P, 2, HEADS, N])
        dbx = st.sb("dbx", [P, 2, N])
        states = st.sb("states", [P, 2, N])
        seen = st.sb("seen", [P, 2, N])
        acc = st.sb("acc", [P, HEADS, N])
        silu_out, old_x, mixed, rest_y = dbx, acc, seen, dbx[:, 0, :]
        stored = [ctx.enter_context(nc.semaphore(f"l0_stored_{n}")) for n in ("even", "odd")]
        STEPS = HEADS * S

        ORDER = ([("project", m, j) for m in range(3) for j in range(NH)] + [("turn", 0, j) for j in range(NH)]
                 + [("project", 3, j) for j in range(NH)] + [("dbc", 0, 0)] + [("turn", 1, j) for j in range(NH)]
                 + [("project", 4, j) for j in range(NH)] + [("move_x", 0, 0), ("project", 5, 0), ("move_x", 0, 1),
                                                            ("project", 5, 1)]
                 + [("move_rows", h, j) for h in range(HEADS) for j in range(NH)]
                 + [("move_x", 1, j) for j in range(NH)])

        PREPARE_DVE = (2, 3, 4, 6, 7, 8, 9, 10)
        PREPARE_PE = [(n + 1) * 7 // 6 - n * 7 // 6 for n in range(3 * STEPS)]

        def bank(g):
            return (6 + g % 2) * HALF

        def filled(g):
            return sem(f"bank{6 + g % 2}_filled")

        def read(g):
            return sem(f"bank{6 + g % 2}_read")

        def await_filled(eng, *group):
            g = ORDER.index(group)
            eng.wait_ge(filled(g), g // 2 + 1)
            return g

        def run(steps, count):
            for _ in range(count):
                next(steps, None)

        def scan_block(scan_b, prepare_b, norm_b, even):
            scan, prepare, norm = scan_b is not None, prepare_b is not None, norm_b is not None
            mine, other = (0, 1) if even else (1, 0)
            with nc.Block() as block:

                @block.sync
                def _(sp):
                    if norm:
                        if prepare:
                            await_filled(sp, "project", 5, 1)
                        sp.dma_start(xn[:, :, :], image(t["x"], norm_b)).then_inc(sem("x_loaded"), 16)
                    if scan:
                        sp.wait_ge(sem("y_turned"), HEADS * NH)
                        sp.dma_start(old_x[:, :, :], image(t["x"], scan_b)).then_inc(sem("old_x_loaded"), 16)
                        for j in range(NH):
                            sp.wait_ge(sem("new_x"), KC * (j + 1))
                            half = slice(j * HALF, (j + 1) * HALF)
                            sp.dma_start(image(xcur, scan_b)[:, :, half], old_x[:, :, half]).then_inc(stored[mine], 16)
                        if not prepare:
                            sp.wait_ge(stored[mine], 16 * NH)

                @block.gpsimd
                def _(pool):
                    if not scan and not prepare:
                        nc.gpsimd.memset(acc[:, 0, 0:1], 0.0).then_inc(stored[mine], 16 * NH)
                    if prepare:
                        nc.gpsimd.memset(ssm[:, :, 0:1], 0.0).then_inc(sem("border"), 1)
                        nc.gpsimd.memset(ssm[:, :, N + 1:N + 2], 0.0).then_inc(sem("border"), 1)
                    if scan:
                        pool.wait_ge(stored[other], 16 * NH)
                        for i in range(STEPS):
                            h, s = divmod(i, S)
                            pool.wait_ge(sem("seen_ready"), i + 1)
                            if s == 0:
                                ins = nc.gpsimd.tensor_copy(acc[:, h, :], seen[:, i % 2, :])
                            else:
                                pool.wait_ge(sem("summed"), i)
                                ins = nc.gpsimd.tensor_tensor(acc[:, h, :], acc[:, h, :], seen[:, i % 2, :], ALU.add)
                            ins.then_inc(sem("summed"), 1)
                    if norm:
                        norm_stats_pool(nc, pool, st, moments, minus_half)

                @block.scalar
                def _(act):
                    def project(m, j):
                        g = await_filled(act, "project", m, j)
                        part = (ssm[:, m, 1 + j * HALF:1 + (j + 1) * HALF] if m < 2 else
                                (res if m < 4 else gate)[:, other, m % 2, j * HALF:(j + 1) * HALF])
                        nc.scalar.activation(part, ps[:, bank(g):bank(g) + HALF], ACT.Silu,
                                             bias=in_b[:, m:m + 1]).then_inc(read(g), 1)
                        return g

                    def conv_silu(k):
                        act.wait_ge(sem("conv_ready"), k + 1)
                        nc.scalar.activation(xf[:, k, :], xf[:, k, :], ACT.Silu,
                                             bias=dw_b[:, k:k + 1]).then_inc(sem("xf_ready"), 1)

                    def turn(h, j):
                        g = await_filled(act, "turn", h, j)
                        if h:
                            act.wait_ge(sem("xt3_ready"), h)
                            act.wait_ge(sem("conv_ready"), KC)
                        nc.scalar.activation(xt3[:, h, 0, j * HALF:(j + 1) * HALF], ps[:, bank(g):bank(g) + HALF],
                                             ACT.Copy).then_inc(sem("x_high"), 1)
                        nc.scalar.activation(turned[:, j * HALF:(j + 1) * HALF], ps[:, bank(g):bank(g) + HALF],
                                             ACT.Copy).then_inc(read(g), 1)

                    def gate_silu(k):
                        for j in range(NH):
                            g = project(4 + k, j)
                            act.wait_ge(read(g), g // 2 + 1)
                            part = gate[:, other, k, j * HALF:(j + 1) * HALF]
                            nc.scalar.activation(part, part, ACT.Silu).then_inc(sem("gate_ready"), 1)

                    def moved_x(h, j):
                        g = await_filled(act, "move_x", h, j)
                        nc.scalar.activation(xp[:, other, h, j * HALF:(j + 1) * HALF], ps[:, bank(g):bank(g) + HALF],
                                             ACT.Copy).then_inc(read(g), 1)

                    if prepare:
                        for m in range(2):
                            for j in range(NH):
                                project(m, j)
                        conv_silu(0)
                        for j in range(NH):
                            project(2, j)
                        for j in range(NH):
                            turn(0, j)
                        conv_silu(1)
                        for j in range(NH):
                            project(3, j)
                        for j in range(NH):
                            turn(1, j)
                        act.wait_ge(sem("minus_abs"), 1)
                        nc.scalar.activation(sp_t[:, 1, :, :], sp_t[:, 0, :, :], ACT.Exp).then_inc(sem("soft_exp"), 1)
                        gate_silu(0)
                        act.wait_ge(sem("one_plus"), 1)
                        nc.scalar.activation(sp_t[:, 3, :, :], sp_t[:, 2, :, :], ACT.Ln).then_inc(sem("soft_ln"), 1)
                        for j in range(NH):
                            moved_x(0, j)
                            g = project(5, j)
                            act.wait_ge(read(g), g // 2 + 1)
                            part = gate[:, other, 1, j * HALF:(j + 1) * HALF]
                            nc.scalar.activation(part, part, ACT.Silu).then_inc(sem("gate_ready"), 1)
                            if j == 0:
                                act.wait_ge(sem("dt_decay"), 1)
                                nc.scalar.activation(rows[:, :, :, 0:S], rows[:, :, :, 0:S],
                                                     ACT.Exp).then_inc(sem("decay_ready"), 1)
                        for h in range(HEADS):
                            for j in range(NH):
                                g = await_filled(act, "move_rows", h, j)
                                nc.scalar.activation(rows_p[:, other, h, j * HALF:(j + 1) * HALF],
                                                     ps[0:3 * ROWS, bank(g):bank(g) + HALF],
                                                     ACT.Copy).then_inc(read(g), 1)
                        for j in range(NH):
                            moved_x(1, j)
                    if scan:
                        for n in range(HEADS * NH):
                            act.wait_ge(sem("y_turned"), n + 1)
                            h, j = divmod(n, NH)
                            nc.scalar.activation(xt3[:, h, 0, j * HALF:(j + 1) * HALF], ps[:, n * HALF:(n + 1) * HALF],
                                                 ACT.Copy).then_inc(sem("y_high"), 1)
                        for j in range(NH):
                            for m in range(KC):
                                act.wait_ge(sem("out_projected"), j * KC + m + 1)
                                lo = m * N + j * HALF
                                nc.scalar.activation(silu_out[:, m, j * HALF:(j + 1) * HALF], ps[:, lo:lo + HALF], ACT.Silu,
                                                     bias=out_b[:, m:m + 1]).then_inc(sem("out_ready"), 1)

                @block.vector
                def _(dve):
                    link = Chain(dve, sem("dve_chain"))
                    tt, ts, stt = nc.vector.tensor_tensor, nc.vector.tensor_scalar, nc.vector.scalar_tensor_tensor

                    def preparation():
                        dve.wait_ge(sem("border"), 2)
                        for k in range(KC):
                            for j in range(NH):
                                g = ORDER.index(("project", k, j))
                                dve.wait_ge(read(g), g // 2 + 1)
                            link(ts(xf[:, k, :], ssm[:, k, 0:N], dw_w[:, k, 0:1], None, ALU.mult))
                            link(stt(xf[:, k, :], ssm[:, k, 1:N + 1], dw_w[:, k, 1:2], xf[:, k, :], ALU.mult, ALU.add))
                            stt(xf[:, k, :], ssm[:, k, 2:N + 2], dw_w[:, k, 2:3], xf[:, k, :], ALU.mult,
                                ALU.add).then_inc(sem("conv_ready"), 1)
                            yield
                        for h in range(HEADS):
                            g = ORDER.index(("turn", h, NH - 1))
                            for q in (g - 1, g):
                                dve.wait_ge(read(q), q // 2 + 1)
                            dve.wait_ge(sem("conv_ready"), KC)
                            dve.wait_ge(sem("x_high"), NH * (h + 1))
                            link(tt(turned[:, :], turned[:, :], xt3[:, h, 0, :], ALU.subtract))
                            link(nc.vector.tensor_copy(xt3[:, h, 1, :], turned[:, :]))
                            tt(xt3[:, h, 2, :], turned[:, :], xt3[:, h, 1, :], ALU.subtract).then_inc(sem("xt3_ready"), 1)
                            yield
                            if h:
                                continue
                            g = await_filled(dve, "dbc", 0, 0)
                            flat = dbc[:, :, :, :].rearrange("p t h r -> p t (h r)")
                            tt(flat, ps[:, bank(g):bank(g) + NT * HEADS * DBC].rearrange("p (t r) -> p t r", t=NT),
                               dbc_b[:, :].unsqueeze(1).to_broadcast([P, NT, HEADS * DBC]), ALU.add).then_inc(read(g), 1)
                            dve.wait_ge(read(g), g // 2 + 1)
                            raw = dbc[:, :, :, 0]
                            stt(sp_t[:, 0, :, :], raw, -1.0, raw, ALU.mult, ALU.min).then_inc(sem("minus_abs"), 1)
                            yield
                        dve.wait_ge(sem("soft_exp"), 1)
                        ts(sp_t[:, 2, :, :], sp_t[:, 1, :, :], 1.0, None, ALU.add).then_inc(sem("one_plus"), 1)
                        yield
                        dve.wait_ge(sem("soft_ln"), 1)
                        link(ts(sp_t[:, 4, :, :], sp_t[:, 2, :, :], -1.0, None, ALU.add))
                        link(ts(sp_t[:, 5, :, :], sp_t[:, 4, :, :], 0.0, None, ALU.is_equal))
                        link(tt(sp_t[:, 4, :, :], sp_t[:, 4, :, :], sp_t[:, 5, :, :], ALU.add))
                        link(nc.vector.reciprocal(sp_t[:, 4, :, :], sp_t[:, 4, :, :]))
                        link(tt(sp_t[:, 3, :, :], sp_t[:, 3, :, :], sp_t[:, 5, :, :], ALU.add))
                        link(tt(sp_t[:, 3, :, :], sp_t[:, 3, :, :], sp_t[:, 1, :, :], ALU.mult))
                        link(tt(sp_t[:, 3, :, :], sp_t[:, 3, :, :], sp_t[:, 4, :, :], ALU.mult))
                        link(stt(sp_t[:, 0, :, :], raw, 0.0, sp_t[:, 3, :, :], ALU.max, ALU.add))
                        for h in range(HEADS):
                            dt = sp_t[:, 0, :, h].unsqueeze(2).to_broadcast([P, NT, S])
                            a = decay[:, h, :].unsqueeze(1).to_broadcast([P, NT, S])
                            link(tt(rows[:, :, h, 0:S], dt, a, ALU.mult))
                            link(tt(rows[:, :, h, S:2 * S], dt, dbc[:, :, h, 1:1 + S], ALU.mult))
                            link(nc.vector.tensor_copy(rows[:, :, h, 2 * S:3 * S], dbc[:, :, h, 1 + S:1 + 2 * S]))
                        nc.vector.memset(sp_t[:, 4, 0, 0:1], 0.0).then_inc(sem("dt_decay"), 1)
                        yield
                        dve.wait_ge(sem("decay_ready"), 1)
                        split_vector(nc, link, [rows3[:, :, :, i, :] for i in range(3)], rows[:, :, :, :],
                                     rows_rest[:, :, :, :]).then_inc(sem("rows3_ready"), 1)

                    def norm_of_next():
                        dve.wait_ge(sem("x_loaded"), 16)
                        norm_begin(nc, st, link, xn, stats, moments)
                        yield
                        norm_spread(nc, dve, st, link, moments, ps[:, 4 * HALF:5 * HALF])
                        yield
                        norm_end(nc, dve, st, moments, ps[:, 4 * HALF:5 * HALF])
                        for k in range(KC):
                            normalise(nc, xn[:, k, :], xn[:, k, :], moments, k).then_inc(sem("xn_ready"), 1)

                    def skip_term(h):
                        dve.wait_ge(sem("summed"), (h + 1) * S)
                        stt(acc[:, h, :], xp[:, mine, h, :], skip[:, h:h + 1], acc[:, h, :], ALU.mult,
                            ALU.add).then_inc(sem("y_ready"), 1)

                    prep = preparation() if prepare else iter(())
                    norms = norm_of_next() if norm else iter(())
                    if scan:
                        for i in range(STEPS):
                            h, s = divmod(i, S)
                            run(prep, PREPARE_DVE.count(i))
                            if i == S + 2:
                                skip_term(0)
                            dve.wait_ge(sem("db_spread"), i + 1)
                            tt(dbx[:, i % 2, :], ps[:, 2 * HALF:4 * HALF], xp[:, mine, h, :],
                               ALU.mult).then_inc(sem("db_used"), 1)
                            dve.wait_ge(sem("db_used"), i + 1)
                            dve.wait_ge(sem("da_spread"), i + 1)
                            nc.vector.tensor_tensor_scan(states[:, i % 2, :], ps[:, 0:2 * HALF], dbx[:, i % 2, :], 0.0,
                                                         ALU.mult, ALU.add).then_inc(sem("da_used"), 1)
                            dve.wait_ge(sem("da_used"), i + 1)
                            dve.wait_ge(sem("c_spread"), i + 1)
                            if i >= 2:
                                dve.wait_ge(sem("summed"), i - 1)
                            tt(seen[:, i % 2, :], ps[:, 4 * HALF:6 * HALF], states[:, i % 2, :],
                               ALU.mult).then_inc(sem("seen_ready"), 1)
                    run(prep, 99)
                    if scan:
                        for h in range(HEADS):
                            if h:
                                skip_term(h)
                            for j in range(NH):
                                n = h * NH + j
                                dve.wait_ge(sem("y_high"), n + 1)
                                half = slice(j * HALF, (j + 1) * HALF)
                                link(tt(rest_y[:, half], ps[:, n * HALF:(n + 1) * HALF], xt3[:, h, 0, half], ALU.subtract))
                                link(nc.vector.tensor_copy(xt3[:, h, 1, half], rest_y[:, half]))
                                tt(xt3[:, h, 2, half], rest_y[:, half], xt3[:, h, 1, half],
                                   ALU.subtract).then_inc(sem("yt3_ready"), 1)
                                dve.wait_ge(sem("yt3_ready"), n + 1)
                    run(norms, 1)
                    for h in range(HEADS if scan else 0):
                        for j in range(NH):
                            dve.wait_ge(sem("y_moved"), h * NH + j + 1)
                            lo = (4 + 2 * h + j) * HALF
                            half = slice(j * HALF, (j + 1) * HALF)
                            link(tt(mixed[:, h, half], ps[:, lo:lo + HALF], gate[:, mine, h, half], ALU.mult))
                            tt(mixed[:, h, half], mixed[:, h, half], res[:, mine, h, half],
                               ALU.add).then_inc(sem("mixed"), 1)
                            if (h, j) == (1, 0):
                                run(norms, 1)
                    run(norms, 2)
                    if scan:
                        dve.wait_ge(sem("old_x_loaded"), 16)
                        for j in range(NH):
                            half = slice(j * HALF, (j + 1) * HALF)
                            for m in range(KC):
                                dve.wait_ge(sem("out_ready"), j * KC + m + 1)
                                tt(old_x[:, m, half], old_x[:, m, half], silu_out[:, m, half],
                                   ALU.add).then_inc(sem("new_x"), 1)

                @block.tensor
                def _(pe):
                    def group(*name):
                        g = ORDER.index(name)
                        if g >= 2:
                            pe.wait_ge(read(g), g // 2)
                        return g

                    def project(m, j):
                        g = group("project", m, j)
                        for k in range(KC):
                            ins = nc.tensor.matmul(ps[:, bank(g):bank(g) + HALF], in_w[:, k, m * P:(m + 1) * P],
                                                   xn[:, k, j * HALF:(j + 1) * HALF], start=(k == 0), stop=(k == KC - 1))
                            if k == KC - 1:
                                ins.then_inc(filled(g), 1)
                            yield

                    def turn(h, j):
                        pe.wait_ge(sem("xf_ready"), h + 1)
                        g = group("turn", h, j)
                        for c_ in range(NT // NH):
                            lo = (j * (NT // NH) + c_) * P
                            ins = nc.tensor.transpose(ps[:, bank(g) + c_ * P:bank(g) + (c_ + 1) * P],
                                                      xf[:, h, lo:lo + P], ident[:, :])
                        ins.then_inc(filled(g), 1)
                        yield

                    def move_x(h, j):
                        pe.wait_ge(sem("xt3_ready"), h + 1)
                        g = group("move_x", h, j)
                        for c_ in range(NT):
                            for i in range(3):
                                ins = nc.tensor.matmul(ps[:, bank(g):bank(g) + HALF], xt3[:, h, i, c_ * P:(c_ + 1) * P],
                                                       forward[:, h, c_, j * HALF:(j + 1) * HALF],
                                                       start=(c_ == 0 and i == 0), stop=(c_ == NT - 1 and i == 2))
                            if c_ == NT - 1:
                                ins.then_inc(filled(g), 1)
                            if c_ % 2:
                                yield

                    def preparation():
                        for m in range(3):
                            for j in range(NH):
                                yield from project(m, j)
                        for j in range(NH):
                            yield from turn(0, j)
                        for j in range(NH):
                            yield from project(3, j)
                        pe.wait_ge(sem("xf_ready"), KC)
                        g = group("dbc", 0, 0)
                        for c_ in range(NT):
                            for k in range(KC):
                                lo = bank(g) + c_ * HEADS * DBC
                                ins = nc.tensor.matmul(ps[:, lo:lo + HEADS * DBC], xf[:, k, c_ * P:(c_ + 1) * P],
                                                       dbc_w[:, k, :], start=(k == 0), stop=(k == KC - 1))
                            if c_ == NT - 1:
                                ins.then_inc(filled(g), 1)
                            if c_ % 4 == 3:
                                yield
                        for j in range(NH):
                            yield from turn(1, j)
                        for j in range(NH):
                            yield from project(4, j)
                        for j in range(NH):
                            yield from move_x(0, j)
                            yield from project(5, j)
                        pe.wait_ge(sem("rows3_ready"), 1)
                        for h in range(HEADS):
                            for j in range(NH):
                                g = group("move_rows", h, j)
                                for c_ in range(NT):
                                    ins = nc.tensor.matmul(ps[0:3 * ROWS, bank(g):bank(g) + HALF],
                                                           rows3[:, c_, h, :, :].rearrange("p a r -> p (a r)"),
                                                           forward[:, h, c_, j * HALF:(j + 1) * HALF],
                                                           start=(c_ == 0), stop=(c_ == NT - 1))
                                    if c_ == NT - 1:
                                        ins.then_inc(filled(g), 1)
                                    if c_ % 4 == 3:
                                        yield
                        for j in range(NH):
                            yield from move_x(1, j)

                    prep = preparation() if prepare else iter(())
                    if scan:
                        for i in range(STEPS):
                            h, s = divmod(i, S)
                            for n, (q, at, ready, used) in enumerate(((S + s, 2, "db_spread", "db_used"),
                                                                      (s, 0, "da_spread", "da_used"),
                                                                      (2 * S + s, 4, "c_spread", "seen_ready"))):
                                if i:
                                    pe.wait_ge(sem(used), i)
                                for j in range(NH):
                                    lo = (at + j) * HALF
                                    ins = nc.tensor.matmul(ps[:, lo:lo + HALF], sel[:, q, :],
                                                           rows_p[:, mine, h, j * HALF:(j + 1) * HALF],
                                                           start=True, stop=True)
                                ins.then_inc(sem(ready), 1)
                                run(prep, PREPARE_PE[3 * i + n])
                    run(prep, 99)

                    def turn_y(h):
                        pe.wait_ge(sem("y_ready"), h + 1)
                        for c_ in range(NT):
                            lo = h * N + c_ * P
                            ins = nc.tensor.transpose(ps[:, lo:lo + P], acc[:, h, c_ * P:(c_ + 1) * P], ident[:, :])
                            if (c_ + 1) * P % HALF == 0:
                                ins.then_inc(sem("y_turned"), 1)

                    if scan:
                        pe.wait_ge(sem("da_used"), STEPS)
                        turn_y(0)
                        pe.wait_ge(sem("seen_ready"), STEPS)
                        if prepare:
                            for g in (len(ORDER) - 2, len(ORDER) - 1):
                                pe.wait_ge(read(g), g // 2 + 1)
                    for h in range(HEADS):
                        for j in range(NH):
                            if scan:
                                lo = (4 + 2 * h + j) * HALF
                                for c_ in range(NT):
                                    if c_ * P % HALF == 0:
                                        pe.wait_ge(sem("yt3_ready"), h * NH + c_ * P // HALF + 1)
                                    for i in range(3):
                                        ins = nc.tensor.matmul(ps[:, lo:lo + HALF], xt3[:, h, i, c_ * P:(c_ + 1) * P],
                                                               backward[:, h, c_, j * HALF:(j + 1) * HALF],
                                                               start=(c_ == 0 and i == 0), stop=(c_ == NT - 1 and i == 2))
                                ins.then_inc(sem("y_moved"), 1)
                                if (h, j) == (0, 0):
                                    turn_y(1)
                            if norm and (h, j) == (1, 0):
                                if scan:
                                    pe.wait_ge(sem("mixed"), 1)
                                norm_means_tensor(nc, pe, st, moments, average, ps[:, 4 * HALF:5 * HALF])
                    if norm:
                        norm_vars_tensor(nc, pe, st, moments, average, ps[:, 4 * HALF:5 * HALF])
                    if scan:
                        for j in range(NH):
                            pe.wait_ge(sem("mixed"), NH + j + 1)
                            for m in range(KC):
                                for k in range(KC):
                                    lo = m * N + j * HALF
                                    ins = nc.tensor.matmul(ps[:, lo:lo + HALF], out_w[:, k, m * P:(m + 1) * P],
                                                           mixed[:, k, j * HALF:(j + 1) * HALF],
                                                           start=(k == 0), stop=(k == KC - 1))
                                ins.then_inc(sem("out_projected"), 1)
            if scan:
                nc.gpsimd.sem_clear(stored[other])
                if not prepare:
                    nc.gpsimd.sem_clear(stored[mine])
            st.clear()

        scan_block(None, None, 0, False)
        scan_block(None, 0, 1, False)
        with nc.Fori(0, B // 2 - 1) as pair:
            scan_block(pair * 2, pair * 2 + 1, pair * 2 + 2, True)
            scan_block(pair * 2 + 1, pair * 2 + 2, pair * 2 + 3, False)
        scan_block(B - 2, B - 1, None, True)
        scan_block(B - 1, None, None, False)


def split_pair(nc, link, high, low, full):
    link(nc.vector.tensor_copy(high, full))
    return nc.vector.tensor_tensor(low, full, high.bitcast(F32), ALU.subtract)


PRODUCTS = ((0, 0), (0, 1), (1, 0))


def build_expert_layer(nc, t, ps, src, dst):
    with ExitStack() as ctx:
        st = Stage(nc, ctx, "l1")
        sem = st.sem
        w1, w3, w2 = (st.sb(n, [P, 2, KC, E, C], F32R) for n in ("w1", "w3", "w2"))
        gate_w = st.sb("gate_w", [P, KC, E])
        sel = st.sb("sel", [3 * E, E, P], BF16)
        average = st.sb("average", [P, P])
        ident = st.sb("ident", [P, P], BF16)
        minus_half = st.sb("minus_half", [P, 4])
        index = st.sb("index", [P, E])
        with ExitStack() as own:
            staged = own.enter_context(nc.sbuf_tensor("w_staged", [P, 3, KC, E, C], F32))
            loads = [
                (gate_w[:, :, :], t["gate_w"].rearrange("(k p) e -> p k e", p=P)),
                (sel[:, :, :], t["sel_experts"].bitcast(BF16)), (average[:, :], t["average"]),
                (ident[:, :], t["ident_bf16"].bitcast(BF16)), (index[:, :], t["index"].partition_broadcast(P)),
            ]
            weights = ((w1, "w1"), (w3, "w3"), (w2, "w2"))
            pieces = [(i, k) for i in range(3) for k in range(KC)]
            with nc.Block() as block:

                @block.sync
                def _(sp):
                    for i, k in pieces:
                        sp.dma_start(staged[:, i, k], t[weights[i][1]].rearrange("(k p) e f -> p k e f", p=P)[:, k])\
                          .then_inc(sem(f"staged{i}{k}"), 16)
                    for to, of in loads:
                        sp.dma_start(to, of).then_inc(sem("loaded"), 16)
                    sp.wait_ge(sem("loaded"), 16 * len(loads))

                @block.scalar
                def _(act):
                    for i, k in pieces:
                        act.wait_ge(sem(f"staged{i}{k}"), 16)
                        nc.scalar.activation(weights[i][0][:, 0, k], staged[:, i, k], ACT.Copy).then_inc(sem("high_ready"), 1)

                @block.vector
                def _(dve):
                    for n, (i, k) in enumerate(pieces):
                        dve.wait_ge(sem("high_ready"), n + 1)
                        w = weights[i][0]
                        nc.vector.tensor_tensor(w[:, 1, k], staged[:, i, k], w[:, 0, k].bitcast(F32),
                                                ALU.subtract).then_inc(sem("low_ready"), 1)
                    dve.wait_ge(sem("low_ready"), len(pieces))

                @block.gpsimd
                def _(pool):
                    nc.gpsimd.memset(minus_half[:, :], -0.5).then_inc(sem("const"), 1)
                    pool.wait_ge(sem("const"), 1)
            st.clear()

        x = st.sb("x", [P, 2, KC, N])
        xn = st.sb("xn", [P, KC, N])
        pair = st.sb("pair", [P, 2, 2, KC, N], F32R)
        stats = st.sb("stats", [P, KC, 6 * NH])
        moments = st.sb("moments", [P, KC, 8])
        prob = st.sb("prob", [P, NT, E])
        left = st.sb("left", [P, NT, E])
        work = st.sb("work", [P, NT, E])
        first = st.sb("first", [P, NT, E])
        best = st.sb("best", [P, NT, 6])
        comb = st.sb("comb", [P, NT, E])
        comb_rest = st.sb("comb_rest", [P, NT, E])
        comb3 = st.sb("comb3", [P, NT, 3, E], BF16)
        comb_t = st.sb("comb_t", [3 * E, 2, N], BF16)
        weight = st.sb("weight", [P, 2, HALF])
        act1 = st.sb("act1", [P, 2, HALF])
        mixed = st.sb("mixed", [P, HALF])
        mixed2 = st.sb("mixed2", [P, 3, 2, HALF], F32R)

        steps = [(m, j, e, f) for m in range(EXPERT_IMGS) for j in range(NH) for e in range(E) for f in range(KC)]
        per = NH * E * KC
        bank = lambda i: ps[:, i * HALF:(i + 1) * HALF]
        small = bank(7)

        CHOOSE = 7
        AT = {"begin": 8, "means": 10, "spread": 11, "vars": 12, "end": 13, "logits": 15, "shift": 16, "exp": 17,
              "turn0": 26, "copy0": 27, "turn1": 28, "copy1": 29} | {f"choose{i}": 18 + i for i in range(CHOOSE)}

        def parts_at(i, parts):
            m, k = divmod(i, per)
            out = [(p, 0) for p in parts] if i == 0 else []
            if m + 1 < EXPERT_IMGS:
                out += [(p, m + 1) for p in parts if AT[p] == k]
            return out

        with nc.Fori(0, B // EXPERT_IMGS) as turn:
            b0 = turn * EXPERT_IMGS
            with nc.Block() as block:

                @block.sync
                def _(sp):
                    for m in range(EXPERT_IMGS + 1):
                        if m < EXPERT_IMGS:
                            if m >= 2:
                                sp.wait_ge(sem(f"stored{m - 2}"), 16)
                            sp.dma_start(x[:, m % 2], image(src, b0 + m)).then_inc(sem(f"x_loaded{m}"), 16)
                        if m:
                            sp.wait_ge(sem("new_x"), NH * KC * m)
                            sp.dma_start(image(dst, b0 + m - 1), x[:, (m - 1) % 2]).then_inc(sem(f"stored{m - 1}"), 16)
                    for m in range(max(0, EXPERT_IMGS - 2), EXPERT_IMGS):
                        sp.wait_ge(sem(f"stored{m}"), 16)

                @block.gpsimd
                def _(pool):
                    for m in range(EXPERT_IMGS):
                        norm_stats_pool(nc, pool, st, moments, minus_half, m)

                @block.scalar
                def _(act):
                    def router(part, m):
                        if part == "exp":
                            act.wait_ge(sem("shifted"), m + 1)
                            nc.scalar.activation(prob[:, :, :], prob[:, :, :], ACT.Exp).then_inc(sem("exped"), 1)
                        else:
                            h = int(part[-1])
                            act.wait_ge(sem("comb_turned"), 2 * m + h + 1)
                            nc.scalar.activation(comb_t[:, m % 2, h * HALF:(h + 1) * HALF], small[0:3 * E, :],
                                                 ACT.Copy).then_inc(sem("comb_t_ready"), 1)

                    for i, (m, j, e, f) in enumerate(steps):
                        for p in parts_at(i, ("exp", "copy0", "copy1")):
                            router(*p)
                        if f == 0:
                            act.wait_ge(sem("weight_spread"), i // KC + 1)
                            if i >= 2 * KC:
                                act.wait_ge(sem("mixed_ready"), i - KC)
                            nc.scalar.activation(weight[:, (i // KC) % 2, :], bank(4), ACT.Copy).then_inc(sem("weight_ready"), 1)
                        act.wait_ge(sem("up_ready"), i + 1)
                        if i >= 2:
                            act.wait_ge(sem("mixed_ready"), i - 1)
                        nc.scalar.activation(act1[:, i % 2, :], bank(i % 2), ACT.Gelu).then_inc(sem("gelu_ready"), 1)

                @block.vector
                def _(dve):
                    link = Chain(dve, sem("dve_chain"))
                    tt, ts, stt = nc.vector.tensor_tensor, nc.vector.tensor_scalar, nc.vector.scalar_tensor_tensor

                    def spread(v):
                        return v.unsqueeze(2).to_broadcast([P, NT, E])

                    def choose(part, m):
                        idx = index[:, :].unsqueeze(1).to_broadcast([P, NT, E])
                        if part == 0:
                            dve.wait_ge(sem("exped"), m + 1)
                            link(nc.vector.tensor_reduce(best[:, :, 1], prob[:, :, :], AX, ALU.add))
                            link(nc.vector.reciprocal(best[:, :, 1], best[:, :, 1]))
                            link(tt(prob[:, :, :], prob[:, :, :], spread(best[:, :, 1]), ALU.mult))
                            link(nc.vector.tensor_copy(left[:, :, :], prob[:, :, :]))
                            link(nc.vector.memset(comb[:, :, :], 0.0))
                        elif part in (1, 3):
                            r = part // 2
                            link(nc.vector.tensor_reduce(best[:, :, 2 + r], left[:, :, :], AX, ALU.max))
                            link(tt(work[:, :, :], left[:, :, :], spread(best[:, :, 2 + r]), ALU.not_equal))
                            link(stt(work[:, :, :], work[:, :, :], float(E), idx, ALU.mult, ALU.add))
                            link(nc.vector.tensor_reduce(best[:, :, 4], work[:, :, :], AX, ALU.min))
                        elif part in (2, 4):
                            link(tt(first[:, :, :], idx, spread(best[:, :, 4]), ALU.is_equal))
                            link(stt(left[:, :, :], first[:, :, :], -2.0, left[:, :, :], ALU.mult, ALU.add))
                            link(tt(first[:, :, :], first[:, :, :], prob[:, :, :], ALU.mult))
                            link(tt(comb[:, :, :], comb[:, :, :], first[:, :, :], ALU.add))
                        elif part == 5:
                            link(tt(best[:, :, 5], best[:, :, 2], best[:, :, 3], ALU.add))
                            link(nc.vector.reciprocal(best[:, :, 5], best[:, :, 5]))
                            link(tt(comb[:, :, :], comb[:, :, :], spread(best[:, :, 5]), ALU.mult))
                        else:
                            split_vector(nc, link, [comb3[:, :, i, :] for i in range(3)], comb[:, :, :],
                                         comb_rest[:, :, :]).then_inc(sem("comb3_ready"), 1)

                    def router(part, m):
                        if part == "begin":
                            dve.wait_ge(sem(f"x_loaded{m}"), 16)
                            norm_begin(nc, st, link, x[:, m % 2], stats, moments)
                        elif part == "spread":
                            norm_spread(nc, dve, st, link, moments, small, m)
                        elif part == "end":
                            norm_end(nc, dve, st, moments, small, m)
                            for k in range(KC):
                                normalise(nc, xn[:, k, :], x[:, m % 2, k, :], moments, k).then_inc(sem("xn_ready"), 1)
                            dve.wait_ge(sem("xn_ready"), KC * (m + 1))
                            split_pair(nc, link, pair[:, m % 2, 0], pair[:, m % 2, 1], xn[:, :, :]).then_inc(sem("pair_ready"), 1)
                        elif part == "shift":
                            dve.wait_ge(sem("logits_ready"), m + 1)
                            logits = small[:, 64:64 + NT * E].rearrange("p (t e) -> p t e", t=NT)
                            link(nc.vector.tensor_reduce(best[:, :, 0], logits, AX, ALU.max))
                            tt(prob[:, :, :], logits, spread(best[:, :, 0]), ALU.subtract).then_inc(sem("shifted"), 1)
                        else:
                            choose(int(part[-1]), m)

                    choices = [f"choose{i}" for i in range(CHOOSE)]

                    def new_x(k):
                        m, j, _, _ = steps[k]
                        dve.wait_ge(sem("down_done"), k + 1)
                        for c in range(KC):
                            part = x[:, m % 2, c, j * HALF:(j + 1) * HALF]
                            nc.vector.tensor_tensor(part, bank(5 + c), part, ALU.add).then_inc(sem("new_x"), 1)

                    for i, (m, j, e, f) in enumerate(steps):
                        for p in parts_at(i, ("begin", "spread", "end", "shift", *choices)):
                            router(*p)
                        dve.wait_ge(sem("gelu_ready"), i + 1)
                        link(tt(act1[:, i % 2, :], bank(2 + i % 2), act1[:, i % 2, :], ALU.mult))
                        dve.wait_ge(sem("weight_ready"), i // KC + 1)
                        tt(mixed[:, :], act1[:, i % 2, :], weight[:, (i // KC) % 2, :], ALU.mult).then_inc(sem("mixed_ready"), 1)
                        dve.wait_ge(sem("mixed_ready"), i + 1)
                        if i >= 3:
                            dve.wait_ge(sem("down_done"), i - 2)
                        split_pair(nc, link, mixed2[:, i % 3, 0, :], mixed2[:, i % 3, 1, :], mixed[:, :])\
                            .then_inc(sem("split_ready"), 1)
                        dve.wait_ge(sem("split_ready"), i + 1)
                        k = i - 2
                        if k >= 0 and (k + 1) % (E * KC) == 0:
                            new_x(k)
                    new_x(len(steps) - 1)

                @block.tensor
                def _(pe):
                    def router(part, m):
                        if part == "means":
                            norm_means_tensor(nc, pe, st, moments, average, small, m)
                        elif part == "vars":
                            norm_vars_tensor(nc, pe, st, moments, average, small, m)
                        elif part == "logits":
                            pe.wait_ge(sem("xn_ready"), KC * (m + 1))
                            for c_ in range(NT):
                                for k in range(KC):
                                    lo = 64 + c_ * E
                                    ins = nc.tensor.matmul(small[:, lo:lo + E], xn[:, k, c_ * P:(c_ + 1) * P],
                                                           gate_w[:, k, :], start=(k == 0), stop=(k == KC - 1))
                            ins.then_inc(sem("logits_ready"), 1)
                        else:
                            h = int(part[-1])
                            pe.wait_ge(sem("comb3_ready"), m + 1)
                            if h:
                                pe.wait_ge(sem("comb_t_ready"), 2 * m + 1)
                            for c_ in range(NT // 2):
                                ins = nc.tensor.matmul(small[0:3 * E, c_ * P:(c_ + 1) * P],
                                                       comb3[:, h * NT // 2 + c_, :, :].rearrange("p a e -> p (a e)"),
                                                       ident[:, :], start=True, stop=True)
                            ins.then_inc(sem("comb_turned"), 1)

                    def up(i):
                        m, j, e, f = steps[i]
                        if i % per == 0:
                            pe.wait_ge(sem("pair_ready"), m + 1)
                        if f == 0:
                            pe.wait_ge(sem("comb_t_ready"), 2 * m + 2)
                            if i:
                                pe.wait_ge(sem("weight_ready"), i // KC)
                            nc.tensor.matmul(bank(4), sel[:, e, :], comb_t[:, m % 2, j * HALF:(j + 1) * HALF],
                                             start=True, stop=True).then_inc(sem("weight_spread"), 1)
                        if i >= 2:
                            pe.wait_ge(sem("mixed_ready"), i - 1)
                        for b_, w in ((0, w1), (2, w3)):
                            for k in range(KC):
                                for r, (a, c) in enumerate(PRODUCTS):
                                    ins = nc.tensor.matmul(bank(b_ + i % 2), w[:, a, k, e, f * P:(f + 1) * P],
                                                           pair[:, m % 2, c, k, j * HALF:(j + 1) * HALF],
                                                           start=(k == 0 and r == 0), stop=(k == KC - 1 and r == 2))
                        ins.then_inc(sem("up_ready"), 1)

                    def down(i):
                        m, j, e, f = steps[i]
                        pe.wait_ge(sem("split_ready"), i + 1)
                        if e == 0 and f == 0 and i:
                            pe.wait_ge(sem("new_x"), KC * (i // (E * KC)))
                        for c in range(KC):
                            for r, (a, d) in enumerate(PRODUCTS):
                                ins = nc.tensor.matmul(bank(5 + c), w2[:, a, f, e, c * P:(c + 1) * P], mixed2[:, i % 3, d, :],
                                                       start=(e == 0 and f == 0 and r == 0),
                                                       stop=(e == E - 1 and f == KC - 1 and r == 2))
                        ins.then_inc(sem("down_done"), 1)

                    for i in range(len(steps)):
                        for p in parts_at(i, ("means", "vars", "logits", "turn0", "turn1")):
                            router(*p)
                        up(i)
                        if i >= 2:
                            down(i - 2)
                    down(len(steps) - 2)
                    down(len(steps) - 1)
            st.clear()


class Coordinates:

    def __init__(self, st, parts):
        self.pos = st.sb("pos", [parts, N])
        self.parts2 = st.sb("parts2", [parts, 2, 2, N], F32R)

    def vector(self, nc, link, i, off, bias, grid):
        stt, ts = nc.vector.scalar_tensor_tensor, nc.vector.tensor_scalar
        high, low = (self.parts2[:, i % 2, j, :] for j in range(2))
        link(stt(self.pos[:, :], off, bias, grid, ALU.add, ALU.add))
        link(ts(self.pos[:, :], self.pos[:, :], 0.0, float(SIDE - 1), ALU.max, ALU.min))
        link(nc.vector.tensor_copy(high, self.pos[:, :]))
        return nc.vector.tensor_tensor(low, self.pos[:, :], high.bitcast(F32), ALU.subtract)

    def stored(self, q, i):
        return self.parts2[q * BLK:(q + 1) * BLK, i % 2, :, :].bitcast(F32)


def padded_rows(pad, j, tap):
    dy, dx = divmod(tap, 3)
    rows = HALF // SIDE
    return pad[:, j * rows + dy:j * rows + dy + rows, dx:dx + SIDE]


def build_offsets_1(nc, t, ps, xcur, dense, coords):
    with ExitStack() as ctx:
        st = Stage(nc, ctx, "o1")
        sem = st.sem
        ow = st.sb("ow", [P, 2, KC, 9, 2, C], F32R)
        ob = st.sb("ob", [P, 2 * KC])
        grid = st.sb("grid", [P, 2, N])
        average = st.sb("average", [P, P])
        minus_half = st.sb("minus_half", [P, 4])
        pad = st.sb("pad", [P, IMGS, 2, KC, PAD, PAD], F32R)
        with ExitStack() as own:
            staged = own.enter_context(nc.sbuf_tensor("ow_staged", [P, KC, 9, 2, C], F32))
            ow_src = t["ow1"].rearrange("(k p) a y c -> p k a y c", p=P)
            pieces = [(k, slice(lo, lo + 3)) for k in range(KC) for lo in range(0, 9, 3)]
            loads = [
                (ob[:, :], t["ob1"]),
                (grid[:, 0, :], t["row_of"].partition_broadcast(P)), (grid[:, 1, :], t["col_of"].partition_broadcast(P)),
                (average[:, :], t["average"]),
            ]
            with nc.Block() as block:

                @block.sync
                def _(sp):
                    for i, (k, taps) in enumerate(pieces):
                        sp.dma_start(staged[:, k, taps], ow_src[:, k, taps]).then_inc(sem(f"piece_loaded{i}"), 16)
                    for dst, src in loads:
                        sp.dma_start(dst, src).then_inc(sem("loaded"), 16)
                    sp.wait_ge(sem("loaded"), 16 * len(loads))

                @block.scalar
                def _(act):
                    for i, (k, taps) in enumerate(pieces):
                        act.wait_ge(sem(f"piece_loaded{i}"), 16)
                        nc.scalar.activation(ow[:, 0, k, taps], staged[:, k, taps], ACT.Copy).then_inc(sem("high_ready"), 1)

                @block.vector
                def _(dve):
                    for i, (k, taps) in enumerate(pieces):
                        dve.wait_ge(sem("high_ready"), i + 1)
                        nc.vector.tensor_tensor(ow[:, 1, k, taps], staged[:, k, taps], ow[:, 0, k, taps].bitcast(F32),
                                                ALU.subtract).then_inc(sem("low_ready"), 1)
                    dve.wait_ge(sem("low_ready"), len(pieces))

                @block.gpsimd
                def _(pool):
                    nc.gpsimd.memset(minus_half[:, :], -0.5).then_inc(sem("const"), 1)
                    nc.gpsimd.memset(pad[:, :, :, :, :, :].bitcast(F32), 0.0).then_inc(sem("const"), 1)
                    pool.wait_ge(sem("const"), 2)
            st.clear()

        x = st.sb("x", [P, 2, KC, N])
        stats = st.sb("stats", [P, KC, 6 * NH])
        moments = st.sb("moments", [P, KC, 8])
        co = Coordinates(st, P)
        kinds = [(m, k, y) for m in range(IMGS) for k in range(KC) for y in range(2)]
        with nc.Fori(0, B // IMGS) as turn:
            b0 = turn * IMGS
            with nc.Block() as block:

                @block.sync
                def _(sp):
                    for m in range(2):
                        sp.dma_start(x[:, m], image(xcur, b0 + m)).then_inc(sem(f"x_loaded{m}"), 16)
                    for i, (m, k, y) in enumerate(kinds):
                        if k == 0 and y == 0:
                            sp.wait_ge(sem("split_ready"), KC * (m + 1))
                            sp.dma_start(dense[bass.ds((b0 + m) * C, C), :].rearrange("(k p) n -> p k n", p=P),
                                         x[:, m % 2]).then_inc(sem(f"stored{m}"), 16)
                            if m + 2 < IMGS:
                                sp.wait_ge(sem(f"stored{m}"), 16)
                                sp.dma_start(x[:, m % 2], image(xcur, b0 + m + 2)).then_inc(sem(f"x_loaded{m + 2}"), 16)
                        sp.wait_ge(sem("coords_ready"), i + 1)
                        for q in range(P // BLK):
                            blk = (b0 + m) * (C // BLK) + k * (P // BLK) + q
                            sp.dma_start(coords[bass.ds(blk, 1), y, :, :, :].rearrange("a s p n -> (a p) s n"),
                                         co.stored(q, i)).then_inc(sem(f"coords_stored{i}"), 16)
                    for i in range(len(kinds)):
                        sp.wait_ge(sem(f"coords_stored{i}"), 16 * (P // BLK))
                    for m in range(IMGS):
                        sp.wait_ge(sem(f"stored{m}"), 16)

                @block.gpsimd
                def _(pool):
                    for m in range(IMGS):
                        norm_stats_pool(nc, pool, st, moments, minus_half, m)

                @block.vector
                def _(dve):
                    link = Chain(dve, sem("dve_chain"))

                    def norm(m):
                        dve.wait_ge(sem(f"x_loaded{m}"), 16)
                        xm = x[:, m % 2]
                        norm_stats_vector(nc, dve, st, link, xm, stats, moments, ps[:, 7 * HALF:8 * HALF], m)
                        for k in range(KC):
                            link(normalise(nc, xm[:, k, :], xm[:, k, :], moments, k))
                            inner = [pad[:, m, i, k, 1:SIDE + 1, 1:SIDE + 1] for i in range(2)]
                            split_pair(nc, link, inner[0], inner[1], xm[:, k, :].rearrange("p (y w) -> p y w", w=SIDE))\
                                .then_inc(sem("split_ready"), 1)

                    norm(0)
                    for i, (m, k, y) in enumerate(kinds):
                        dve.wait_ge(sem("offsets_ready"), i + 1)
                        if i >= 2:
                            dve.wait_ge(sem(f"coords_stored{i - 2}"), 16 * (P // BLK))
                        lo = (i % 2) * N
                        col = 2 * k + y
                        co.vector(nc, link, i, ps[:, lo:lo + N], ob[:, col:col + 1], grid[:, y, :])\
                          .then_inc(sem("coords_ready"), 1)
                        dve.wait_ge(sem("coords_ready"), i + 1)
                        if k == 0 and y == 0 and m + 1 < IMGS:
                            norm(m + 1)

                @block.tensor
                def _(pe):
                    norm_stats_tensor(nc, pe, st, moments, average, ps[:, 7 * HALF:8 * HALF], 0)
                    for i, (m, k, y) in enumerate(kinds):
                        if i >= 2:
                            pe.wait_ge(sem("coords_ready"), i - 1)
                        for j in range(NH):
                            if k == 1 and y == 0 and m + 1 < IMGS:
                                (norm_means_tensor, norm_vars_tensor)[j](nc, pe, st, moments, average,
                                                                         ps[:, 7 * HALF:8 * HALF], m + 1)
                            lo = (i % 2) * N + j * HALF
                            for n in range(KC * 9):
                                kk, tap = divmod(n, 9)
                                if k == 0 and y == 0 and j == 0 and tap == 0:
                                    pe.wait_ge(sem("split_ready"), KC * m + kk + 1)
                                for r, (a, c) in enumerate(PRODUCTS):
                                    ins = nc.tensor.matmul(ps[:, lo:lo + HALF], ow[:, a, kk, tap, y, k * P:(k + 1) * P],
                                                           padded_rows(pad[:, m, c, kk], j, tap), start=(n == 0 and r == 0),
                                                           stop=(n == KC * 9 - 1 and r == 2))
                        ins.then_inc(sem("offsets_ready"), 1)
            st.clear()


def build_gather(nc, ps, consts, dense, coords, gathered, blocks, tag):
    with ExitStack() as ctx:
        st = Stage(nc, ctx, tag)
        sem = st.sem
        spread, fold, index, img = (consts[name] for name in ("spread", "fold", "index", "img"))
        coord = st.sb("coord", [P, SETS, UNITS, N], F32R)
        WB, PB = 4, 8
        wts = st.sb("wts", [P, WB, 2, HALF])
        prod = st.sb("prod", [P, PB, HALF])
        res = st.sb("res", [P, 2, HALF])
        steps = [(s, j, g, u) for s in range(SETS) for j in range(NH) for g in range(NG) for u in range(UNITS)]
        n = len(steps)
        per = NG * UNITS
        with nc.Fori(0, blocks // (SETS * UNITS)) as turn:
            n0 = turn * (SETS * UNITS)
            with nc.Block() as block:

                @block.sync
                def _(sp):
                    def load_coord(s, units, halves, signal):
                        px = slice(halves[0] * HALF, (halves[-1] + 1) * HALF)
                        sp.dma_start(coord[:, s, units[0]:units[-1] + 1, px].bitcast(F32),
                                     coords[bass.ds(n0 + s * UNITS + units[0], len(units)), :, :, :, px]
                                     .rearrange("a y s p n -> (y s p) a n")).then_inc(sem(signal), 16)

                    for u in range(UNITS):
                        load_coord(0, [u], [0], f"first_coord_loaded{u}")
                    for s in range(SETS):
                        if s:
                            load_coord(s, range(UNITS), range(NH), f"coord_loaded{s}")
                        src = dense[bass.ds((n0 + s * UNITS) * BLK, UNITS * BLK), :]\
                            .rearrange("(g c) (i j) -> c i g j", c=4, j=SIDE)
                        for c in range(4):
                            sp.dma_start(img[c * SIDE:(c + 1) * SIDE, s, :, c * SIDE:(c + 1) * SIDE],
                                         src[c]).then_inc(sem(f"img_loaded{s}"), 16)
                        if s == 0:
                            load_coord(0, range(UNITS), [1], "coord_loaded0")
                    for r in range(SETS * NH):
                        s, j = divmod(r, NH)
                        sp.wait_ge(sem("res_ready"), r + 1)
                        sp.dma_start(gathered[bass.ds((n0 + s * UNITS) * BLK, P), j * HALF:(j + 1) * HALF],
                                     res[:, r % 2, :]).then_inc(sem(f"stored{r}"), 16)
                    for r in range(SETS * NH):
                        sp.wait_ge(sem(f"stored{r}"), 16)

                @block.scalar
                def _(act):
                    def evacuate(r):
                        act.wait_ge(sem("folded"), NG * (r + 1))
                        if r >= 2:
                            act.wait_ge(sem(f"stored{r - 2}"), 16)
                        nc.scalar.activation(res[:, r % 2, :], ps[:, (6 + r % 2) * HALF:(7 + r % 2) * HALF],
                                             ACT.Copy).then_inc(sem("res_ready"), 1)

                    for i in range(n):
                        act.wait_ge(sem("spread_ready"), i + 1)
                        if i >= WB:
                            act.wait_ge(sem("weighted"), i - WB + 1)
                        lo = 2 * (i % 2) * HALF
                        nc.scalar.activation(wts[:, i % WB, :, :].rearrange("p y n -> p (y n)"), ps[:, lo:lo + 2 * HALF],
                                             ACT.Abs, bias=index[:, 0:1]).then_inc(sem("distance_ready"), 1)
                        if i % per == 8 and i > per:
                            evacuate(i // per - 1)
                    evacuate(SETS * NH - 1)

                @block.vector
                def _(dve):
                    for i in range(n + 1):
                        if i < n:
                            dve.wait_ge(sem("distance_ready"), i + 1)
                            nc.vector.tensor_scalar(wts[:, i % WB, :, :], wts[:, i % WB, :, :], 1.0, -1.0, ALU.min,
                                                    ALU.add).then_inc(sem("weights_ready"), 1)
                        if i:
                            k = i - 1
                            dve.wait_ge(sem("weights_ready"), i)
                            dve.wait_ge(sem("rows_summed"), k + 1)
                            if k >= PB:
                                dve.wait_ge(sem("folded"), (k - PB) // UNITS + 1)
                            nc.vector.tensor_tensor(prod[:, k % PB, :], ps[:, (4 + k % 2) * HALF:(5 + k % 2) * HALF],
                                                    wts[:, k % WB, 1, :], ALU.mult).then_inc(sem("weighted"), 1)

                @block.tensor
                def _(pe):
                    def spread_step(i):
                        s, j, g, u = steps[i]
                        if i < UNITS:
                            pe.wait_ge(sem(f"first_coord_loaded{u}"), 16)
                        elif i == per or (s and i % (per * NH) == 0):
                            pe.wait_ge(sem(f"coord_loaded{s}"), 16)
                        if i >= 2:
                            pe.wait_ge(sem("distance_ready"), i - 1)
                        for y in range(2):
                            lo = (2 * (i % 2) + y) * HALF
                            ins = nc.tensor.matmul(ps[:, lo:lo + HALF], spread[:, y, g, :],
                                                   coord[:, s, u, j * HALF:(j + 1) * HALF],
                                                   start=True, stop=True)
                        ins.then_inc(sem("spread_ready"), 1)

                    def rows_step(i):
                        s, j, g, u = steps[i]
                        if i % (per * NH) == 0:
                            pe.wait_ge(sem(f"img_loaded{s}"), 64)
                        pe.wait_ge(sem("weights_ready"), i + 1)
                        if i >= 2:
                            pe.wait_ge(sem("weighted"), i - 1)
                        lo = (4 + i % 2) * HALF
                        nc.tensor.matmul(ps[:, lo:lo + HALF], img[:, s, u * NG + g, :], wts[:, i % WB, 0, :], start=True,
                                         stop=True).then_inc(sem("rows_summed"), 1)

                    def fold_steps(q):
                        r, g = divmod(q, NG)
                        pe.wait_ge(sem("weighted"), UNITS * (q + 1))
                        if g == 0 and r >= 2:
                            pe.wait_ge(sem("res_ready"), r - 1)
                        lo = (6 + r % 2) * HALF
                        for u in range(UNITS):
                            ins = nc.tensor.matmul(ps[u * BLK:(u + 1) * BLK, lo:lo + HALF], fold[:, g, :],
                                                   prod[:, (UNITS * q + u) % PB, :], start=(g == 0), stop=(g == NG - 1))
                        ins.then_inc(sem("folded"), 1)

                    spread_step(0)
                    spread_step(1)
                    for i in range(n):
                        if i + 2 < n:
                            spread_step(i + 2)
                        rows_step(i)
                        if i % UNITS == 1 and i > UNITS:
                            fold_steps(i // UNITS - 1)
                    fold_steps(n // UNITS - 1)
            st.clear()


def batch_norm_setup(nc, dve, link, sem, cols, out, count):
    link(nc.vector.tensor_scalar(out[:, 2], cols[:, 3], BN_EPS, None, ALU.add))
    nc.vector.tensor_scalar(out[:, 2], out[:, 2], 1.0, None, ALU.mult).then_inc(sem("bn_var"), 1)
    dve.wait_ge(sem("bn_root"), count)
    link(nc.vector.tensor_tensor(out[:, 0], cols[:, 0], out[:, 3], ALU.mult))
    link(nc.vector.tensor_tensor(out[:, 1], cols[:, 2], out[:, 0], ALU.mult))
    link(nc.vector.tensor_tensor(out[:, 1], cols[:, 1], out[:, 1], ALU.subtract))


def stacked_taps():
    return [(dx, 0, P) for dx in range(3)] + [(dx, 2, CM) for dx in range(3)]


def stacked_conv(nc, operands, out, concurrent):
    for i, (dx, dy, rows) in enumerate(stacked_taps()):
        for j in range(NH):
            if rows == P or concurrent:
                base, lift = 0, 0
            else:
                base, lift = j * CM, j
            y0 = j * (HALF // SIDE) + dy - lift
            for r, (weights, stack) in enumerate(operands):
                ins = nc.tensor.matmul(out[j], weights[base:base + rows, i, :],
                                       stack[base:base + rows, y0:y0 + HALF // SIDE, dx:dx + SIDE],
                                       start=(i == 0 and r == 0), stop=(i == 5 and r == len(operands) - 1),
                                       skip_group_check=True)
    return ins


def load_constants(nc, st, t):
    sem = st.sem
    c = {
        "spread": st.sb("spread", [P, 2, NG, P], F32R), "fold": st.sb("fold", [P, NG, BLK]),
        "index": st.sb("index", [P, 1]), "img": st.sb("img", [P, SETS, UNITS * NG, P]),
        "w2": st.sb("w2", [P, KC, CM]), "w3": st.sb("w3", [P, 6, CM]), "w4": st.sb("w4", [CM, C]),
        "grid": st.sb("grid", [P, N]), "wide": st.sb("wide", [P, KC, C]), "average": st.sb("average", [P, P]),
        "minus_half": st.sb("minus_half", [P, 4]), "bn4": st.sb("bn4", [P, 4, KC]),
    }
    for n in (2, 3):
        c[f"ow{n}"] = st.sb(f"ow{n}", [P, 2, 6, P], F32R)
        c[f"ob{n}"] = st.sb(f"ob{n}", [P, 1])
        c[f"bn{n}"] = st.sb(f"bn{n}", [P, 4, 1])
    norms = (2, 3, 4)
    with ExitStack() as own:
        spread_f = own.enter_context(nc.sbuf_tensor("spread_f", [P, 2, NG, P], F32))
        ow_f = {n: own.enter_context(nc.sbuf_tensor(f"ow_f{n}", [P, 6, P], F32)) for n in (2, 3)}
        cols = {n: own.enter_context(nc.sbuf_tensor(f"bn_cols{n}", [P, 4, c[f"bn{n}"].shape[2]], F32)) for n in norms}
        loads = [
            (spread_f[:, :, :, :], t["sel_spread"]), (cols[2][0:CM, :, 0], t["bn1"]), (cols[2][CM:P, :, 0], t["bn1"]),
            (cols[3][0:CM, :, 0], t["bn2"]), (cols[3][CM:P, :, 0], t["bn2"]), (cols[4][:, :, :], t["bn3"]),
            (c["fold"][:, :, :], t["sel_fold"]), (c["index"][:, :], t["minus_index"]),
            (c["w2"][:, :, :], t["w_2"].rearrange("(k p) c -> p k c", p=P)), (c["w3"][:, :, :], t["w_3"]),
            (c["w4"][:, :], t["w_4"]), (ow_f[2][:, :, :], t["ow2"]), (ow_f[3][:, :, :], t["ow3"]),
            (c["ob2"][:, :], t["ob2"]), (c["ob3"][:, :], t["ob3"]), (c["average"][:, :], t["average"]),
            (c["grid"][0:CM, :], t["row_of"].partition_broadcast(CM)),
            (c["grid"][CM:P, :], t["col_of"].partition_broadcast(CM)),
            (c["wide"][:, :, :], t["wide"].rearrange("(k p) o -> p k o", p=P)),
        ]
        with nc.Block() as block:

            @block.sync
            def _(sp):
                for dst, src in loads:
                    sp.dma_start(dst, src).then_inc(sem("loaded"), 16)

            @block.gpsimd
            def _(pool):
                nc.gpsimd.memset(c["minus_half"][:, :], -0.5).then_inc(sem("const"), 1)
                nc.gpsimd.memset(c["img"][:, 0:SETS // 2, :, :], 0.0).then_inc(sem("img_zero"), 1)
                pool.wait_ge(sem("const"), 1)
                for i, n in enumerate(norms):
                    pool.wait_ge(sem("bn_var"), i + 1)
                    bn = c[f"bn{n}"]
                    nc.gpsimd.tensor_tensor(bn[:, 3], bn[:, 2], c["minus_half"][:, 0:bn.shape[2]],
                                            ALU.pow).then_inc(sem("bn_root"), 1)
                pool.wait_ge(sem("img_zero"), 2)

            @block.vector
            def _(dve):
                link = Chain(dve, sem("dve_chain"))
                nc.vector.memset(c["img"][:, SETS // 2:SETS, :, :], 0.0).then_inc(sem("img_zero"), 1)
                dve.wait_ge(sem("loaded"), 16 * len(loads))
                link(nc.vector.tensor_copy(c["spread"][:, :, :, :], spread_f[:, :, :, :]))
                for n in (2, 3):
                    link(split_pair(nc, link, c[f"ow{n}"][:, 0], c[f"ow{n}"][:, 1], ow_f[n][:, :, :]))
                for i, n in enumerate(norms):
                    batch_norm_setup(nc, dve, link, sem, cols[n], c[f"bn{n}"], i + 1)
        st.clear()
    return c


def build_middle(nc, ps, consts, gathered, dense, coords, n):
    with ExitStack() as ctx:
        st = Stage(nc, ctx, f"o{n}")
        sem = st.sem
        w, ow, ob, bn = (consts[f"{name}{n}"] for name in ("w", "ow", "ob", "bn"))
        grid = consts["grid"]
        x = st.sb("x", [P, PASS, KC, N] if n == 2 else [P, PASS, PAD, PAD])
        stack = st.sb("stack", [P, PASS, PAD, PAD])
        pair = st.sb("pair", [P, 2, 2, PAD, PAD], F32R)
        co = Coordinates(st, P)

        def zero_border(buf):
            parts = (buf[:, :, :, 0], buf[:, :, :, PAD - 1], buf[0:CM, :, 0, 1:PAD - 1], buf[:, :, PAD - 1, 1:PAD - 1],
                     buf[CM:P, :, PAD - 2, 1:PAD - 1])
            for part in parts:
                nc.vector.memset(part, 0.0).then_inc(sem("border"), 1)

        rows = HALF // SIDE
        with nc.Fori(0, B // PASS) as turn:
            b0 = turn * PASS
            with nc.Block() as block:

                @block.sync
                def _(sp):
                    for m in range(PASS):
                        b = b0 + m
                        if n == 2:
                            sp.dma_start(x[:, m], gathered[bass.ds(b * C, C), :].rearrange("(k p) n -> p k n", p=P))\
                              .then_inc(sem(f"x_loaded{m}"), 16)
                        else:
                            src = gathered[bass.ds(b * CM, CM), :].rearrange("p (y w) -> p y w", w=SIDE)
                            for r in range(2):
                                sp.dma_start(x[r * CM:(r + 1) * CM, m, 1 - r:SIDE + 1 - r, 1:SIDE + 1], src)\
                                  .then_inc(sem(f"x_loaded{m}"), 16)
                    for m in range(PASS):
                        b = b0 + m
                        sp.wait_ge(sem("h_ready"), 4 * (m + 1))
                        sp.dma_start(dense[bass.ds(b * CM, CM), :].rearrange("p (y w) -> p y w", w=SIDE),
                                     stack[0:CM, m, 1:SIDE + 1, 1:SIDE + 1]).then_inc(sem("stored"), 16)
                        sp.wait_ge(sem("coords_ready"), m + 1)
                        for q in range(P // BLK):
                            y, half = divmod(q, 2)
                            sp.dma_start(coords[bass.ds(b * 2 + half, 1), y, :, :, :].rearrange("a s p n -> (a p) s n"),
                                         co.stored(q, m)).then_inc(sem(f"coords_stored{m}"), 16)
                    for m in range(PASS):
                        sp.wait_ge(sem(f"coords_stored{m}"), 16 * (P // BLK))
                    sp.wait_ge(sem("stored"), 16 * PASS)

                @block.scalar
                def _(act):
                    for m in range(PASS):
                        act.wait_ge(sem("conv_ready"), m + 1)
                        lo = (m % 2) * HALF
                        for j in range(NH):
                            for r in range(2):
                                part = slice(j * CM, (j + 1) * CM)
                                y0 = j * rows + 1 - r
                                nc.scalar.activation(stack[r * CM:(r + 1) * CM, m, y0:y0 + rows, 1:SIDE + 1],
                                                     ps[part, lo:lo + HALF].rearrange("p (y w) -> p y w", w=SIDE),
                                                     ACT.Identity, bias=bn[part, 1, :],
                                                     scale=bn[part, 0, :]).then_inc(sem("h_ready"), 1)

                @block.vector
                def _(dve):
                    link = Chain(dve, sem("dve_chain"))
                    for buf in (stack, x) if n == 3 else (stack,):
                        zero_border(buf)

                    def split(m):
                        dve.wait_ge(sem("h_ready"), 4 * (m + 1))
                        if m >= 2:
                            dve.wait_ge(sem("offsets_ready"), m - 1)
                        else:
                            dve.wait_ge(sem("border"), 5 * (n - 1))
                        split_pair(nc, link, pair[:, m % 2, 0], pair[:, m % 2, 1], stack[:, m]).then_inc(sem("pair_ready"), 1)

                    split(0)
                    for m in range(PASS):
                        if m + 1 < PASS:
                            split(m + 1)
                        dve.wait_ge(sem("offsets_ready"), m + 1)
                        if m >= 2:
                            dve.wait_ge(sem(f"coords_stored{m - 2}"), 16 * (P // BLK))
                        lo = (4 + 2 * (m % 2)) * HALF
                        co.vector(nc, link, m, ps[:, lo:lo + N], ob[:, 0:1], grid[:, :]).then_inc(sem("coords_ready"), 1)
                        dve.wait_ge(sem("coords_ready"), m + 1)

                @block.tensor
                def _(pe):
                    def conv(m):
                        pe.wait_ge(sem(f"x_loaded{m}"), 16 if n == 2 else 32)
                        if m >= 2:
                            pe.wait_ge(sem("h_ready"), 4 * (m - 1))
                        lo = (m % 2) * HALF
                        halves = [ps[j * CM:(j + 1) * CM, lo:lo + HALF] for j in range(NH)]
                        if n == 2:
                            for k in range(KC):
                                for j in range(NH):
                                    ins = nc.tensor.matmul(halves[j], w[:, k, :], x[:, m, k, j * HALF:(j + 1) * HALF],
                                                           start=(k == 0), stop=(k == KC - 1), skip_group_check=True)
                        else:
                            ins = stacked_conv(nc, [(w, x[:, m])], halves, True)
                        ins.then_inc(sem("conv_ready"), 1)

                    def offsets(m):
                        pe.wait_ge(sem("pair_ready"), m + 1)
                        if m >= 2:
                            pe.wait_ge(sem("coords_ready"), m - 1)
                        lo = (4 + 2 * (m % 2)) * HALF
                        halves = [ps[:, lo + j * HALF:lo + (j + 1) * HALF] for j in range(NH)]
                        operands = [(ow[:, a], pair[:, m % 2, c]) for a, c in PRODUCTS]
                        stacked_conv(nc, operands, halves, False).then_inc(sem("offsets_ready"), 1)

                    pe.wait_ge(sem("border"), 5 * (n - 1))
                    conv(0)
                    for m in range(PASS):
                        if m + 1 < PASS:
                            conv(m + 1)
                        offsets(m)
            st.clear()


def build_last(nc, ps, consts, xcur, gathered, out):
    with ExitStack() as ctx:
        st = Stage(nc, ctx, "l3")
        sem = st.sem
        w3, wide, bn, average, minus_half = (consts[name] for name in ("w4", "wide", "bn4", "average", "minus_half"))
        h = st.sb("h", [CM, LAST_IMGS, N])
        r = st.sb("r", [P, LAST_IMGS, KC, N])
        x = st.sb("x", [P, LAST_IMGS, KC, N])
        xn = st.sb("xn", [P, 2, KC, N])
        stats = st.sb("stats", [P, KC, 6 * NH])
        moments = st.sb("moments", [P, KC, 8])
        norm_ps = ps[:, 7 * HALF:8 * HALF]
        with nc.Fori(0, B // LAST_IMGS) as turn:
            b0 = turn * LAST_IMGS
            with nc.Block() as block:

                @block.sync
                def _(sp):
                    for i in range(LAST_IMGS):
                        sp.dma_start(h[:, i, :], gathered[bass.ds((b0 + i) * CM, CM), :]).then_inc(sem(f"h_loaded{i}"), 16)
                        sp.dma_start(x[:, i], image(xcur, b0 + i)).then_inc(sem(f"x_loaded{i}"), 16)
                    for i in range(LAST_IMGS):
                        sp.wait_ge(sem("new_x"), KC * (i + 1))
                        sp.dma_start(image(out, b0 + i), x[:, i]).then_inc(sem("stored"), 16)
                    sp.wait_ge(sem("stored"), 16 * LAST_IMGS)

                @block.gpsimd
                def _(pool):
                    for i in range(LAST_IMGS):
                        norm_stats_pool(nc, pool, st, moments, minus_half, i)

                @block.scalar
                def _(act):
                    for i in range(LAST_IMGS):
                        for m in range(KC):
                            act.wait_ge(sem("wide_ready"), KC * i + m + 1)
                            nc.scalar.activation(r[:, i, m, :], ps[:, 0:N], ACT.Relu, bias=bn[:, 1, m:m + 1],
                                                 scale=bn[:, 0, m:m + 1]).then_inc(sem("relu_ready"), 1)

                @block.vector
                def _(dve):
                    link = Chain(dve, sem("dve_chain"))
                    tt = nc.vector.tensor_tensor

                    def add_relu(i):
                        dve.wait_ge(sem(f"x_loaded{i}"), 16)
                        for m in range(KC):
                            dve.wait_ge(sem("relu_ready"), KC * i + m + 1)
                            link(tt(x[:, i, m, :], x[:, i, m, :], r[:, i, m, :], ALU.add))

                    def end(i):
                        norm_end(nc, dve, st, moments, norm_ps, i)
                        for k in range(KC):
                            normalise(nc, xn[:, i % 2, k, :], x[:, i, k, :], moments, k).then_inc(sem("xn_ready"), 1)
                        dve.wait_ge(sem("xn_ready"), KC * (i + 1))

                    def add_last(i, m):
                        dve.wait_ge(sem("last_ready"), KC * i + m + 1)
                        tt(x[:, i, m, :], ps[:, (m + 1) * N:(m + 2) * N], x[:, i, m, :], ALU.add).then_inc(sem("new_x"), 1)

                    add_relu(0)
                    norm_begin(nc, st, link, x[:, 0], stats, moments)
                    norm_spread(nc, dve, st, link, moments, norm_ps)
                    end(0)
                    add_relu(1)
                    for i in range(LAST_IMGS):
                        if i + 1 < LAST_IMGS:
                            norm_begin(nc, st, link, x[:, i + 1], stats, moments)
                            norm_spread(nc, dve, st, link, moments, norm_ps, i + 1)
                        add_last(i, 0)
                        if i + 1 < LAST_IMGS:
                            end(i + 1)
                        add_last(i, 1)
                        if i + 2 < LAST_IMGS:
                            add_relu(i + 2)

                @block.tensor
                def _(pe):
                    def widen(i, m):
                        pe.wait_ge(sem(f"h_loaded{i}"), 16)
                        if i + m:
                            pe.wait_ge(sem("relu_ready"), KC * i + m)
                        for j in range(NH):
                            ins = nc.tensor.matmul(ps[:, j * HALF:(j + 1) * HALF], w3[:, m * P:(m + 1) * P],
                                                   h[:, i, j * HALF:(j + 1) * HALF], start=True, stop=True)
                        ins.then_inc(sem("wide_ready"), 1)

                    def last(i, m):
                        if i:
                            pe.wait_ge(sem("new_x"), KC * (i - 1) + m + 1)
                        for j in range(NH):
                            for k in range(KC):
                                lo = (m + 1) * N + j * HALF
                                ins = nc.tensor.matmul(ps[:, lo:lo + HALF], wide[:, k, m * P:(m + 1) * P],
                                                       xn[:, i % 2, k, j * HALF:(j + 1) * HALF],
                                                       start=(k == 0), stop=(k == KC - 1))
                        ins.then_inc(sem("last_ready"), 1)

                    for m in range(KC):
                        widen(0, m)
                    norm_means_tensor(nc, pe, st, moments, average, norm_ps)
                    norm_vars_tensor(nc, pe, st, moments, average, norm_ps)
                    for m in range(KC):
                        widen(1, m)
                    for i in range(LAST_IMGS):
                        pe.wait_ge(sem("xn_ready"), KC * (i + 1))
                        last(i, 0)
                        if i + 1 < LAST_IMGS:
                            norm_means_tensor(nc, pe, st, moments, average, norm_ps, i + 1)
                        last(i, 1)
                        if i + 1 < LAST_IMGS:
                            norm_vars_tensor(nc, pe, st, moments, average, norm_ps, i + 1)
                        if i + 2 < LAST_IMGS:
                            for m in range(KC):
                                widen(i + 2, m)
            st.clear()


def kernel_program(nc, t, out):
    with ExitStack() as ctx:
        def dram(name, shape, dt=F32):
            return nc.dram_tensor(name, shape, dt, kind="Internal").ap()

        ps = ctx.enter_context(nc.psum_tensor("ps", [P, 8 * HALF], F32))
        xcur = dram("xcur", (B, C, N))
        dense = dram("dense", (B * C, N))
        gathered = dram("gathered", (B * C, N))
        coords = dram("coords", (B * C // BLK, 2, 2, BLK, N))
        build_scan_layer(nc, t, ps, xcur)
        build_expert_layer(nc, t, ps, xcur, xcur)
        build_offsets_1(nc, t, ps, xcur, dense, coords)
        with ExitStack() as kept:
            consts = load_constants(nc, Stage(nc, kept, "l2"), t)
            build_gather(nc, ps, consts, dense, coords, gathered, B * C // BLK, "g1")
            build_middle(nc, ps, consts, gathered, dense, coords, 2)
            build_gather(nc, ps, consts, dense, coords, gathered, B * CM // BLK, "g2")
            build_middle(nc, ps, consts, gathered, dense, coords, 3)
            build_gather(nc, ps, consts, dense, coords, gathered, B * CM // BLK, "g3")
            build_last(nc, ps, consts, xcur, gathered, out)


def constants():
    import numpy as np

    def ones_bf16(where):
        return where.astype(np.uint16) * np.uint16(0x3F80)

    tok = np.arange(N)
    lin = np.linspace(-1.0, 1.0, SIDE, dtype=np.float32)
    col = lambda v: np.ascontiguousarray(v.reshape(NT, P).T.astype(np.float32))
    gx, gy = lin[tok % SIDE], lin[tok // SIDE]
    p = np.arange(P)
    sel_rows = np.zeros((3 * ROWS, ROWS, P), np.float32)
    for q in range(ROWS):
        sel_rows[q::ROWS, q, :] = 1
    sel_experts = np.zeros((3 * E, E, P), np.float32)
    for e in range(E):
        sel_experts[e::E, e, :] = 1
    spread = np.zeros((P, 2, NG, P), np.float32)
    fold = np.zeros((P, NG, BLK), np.float32)
    for g in range(NG):
        for q in p:
            for y in range(2):
                spread[y * 2 * BLK + 4 * g + q // SIDE:(y + 1) * 2 * BLK:BLK, y, g, q] = 1
            fold[q, g, 4 * g + q // SIDE] = 1
    return {
        "sel_experts": ones_bf16(sel_experts), "ident_bf16": ones_bf16(np.eye(P)),
        "index": np.arange(E, dtype=np.float32), "minus_index": -(p % SIDE).astype(np.float32).reshape(P, 1),
        "row_of": (tok // SIDE).astype(np.float32), "col_of": (tok % SIDE).astype(np.float32),
        "sel_spread": spread, "sel_fold": fold,
        "grid_token": tok.astype(np.float32),
        "col_x": col(gx), "col_y": col(gy), "col_token": col(tok),
        "below": (p[None, :] < p[:, None]).astype(np.float32),
        "average": (p[None, :] // 8 == p[:, None] // 8).astype(np.float32) / 8,
        "ident": np.eye(P, dtype=np.float32),
        "sel_rows": ones_bf16(sel_rows),
    }


def kernel(**inputs):
    import numpy as np
    import concourse.bacc as bacc
    from concourse import mybir as _mybir
    from concourse.bass_utils import run_bass_kernel_spmd as _run

    nc = bacc.Bacc("TRN2", target_bir_lowering=False, num_devices=1)
    a = {k: np.asarray(v) for k, v in inputs.items()}
    sent = {
        "x": a["x"].reshape(B, C, N),
        "in_w": a["L0_conv_in_proj_w"].T, "out_w": a["L0_conv_out_proj_w"].T, "dbc_w": a["L0_conv_dbc_w"].T,
    }
    for name, key in (("in_b", "L0_conv_in_proj_b"), ("out_b", "L0_conv_out_proj_b"), ("dw_b", "L0_conv_dw_b")):
        sent[name] = a[key].reshape(-1, P).T
    for name in ("dw_w", "dbc_b", "A_log", "Dparam", "mobius"):
        sent[f"L0_conv_{name}"] = a[f"L0_conv_{name}"]

    def stacked(w):
        w = w.reshape(CM, 3, 3, -1)
        return np.concatenate([np.concatenate([w[:, 0], w[:, 1]], 0), np.concatenate([w[:, 2], w[:, 2]], 0)], 1)

    for name in ("w1", "w2", "w3"):
        sent[name] = a[f"L1_conv_{name}"].transpose(2, 0, 1)
    sent["gate_w"] = a["L1_conv_gate_w"].T
    for n, cin in ((1, C), (2, CM), (3, CM)):
        v = a[f"L2_conv_ow{n}"].reshape(cin, 2, cin, 9).transpose(2, 3, 1, 0)
        o = a[f"L2_conv_ob{n}"].reshape(cin, 2)
        sent[f"ow{n}"] = v if n == 1 else stacked(v.reshape(cin, 9, 2 * cin))
        sent[f"ob{n}"] = o.reshape(KC, P, 2).transpose(1, 0, 2).reshape(P, 2 * KC) if n == 1 else o.T.reshape(P, 1)
    sent["w_2"] = a["L2_conv_w1"].reshape(CM, C).T
    sent["w_3"] = stacked(a["L2_conv_w2"].reshape(CM, CM, 9).transpose(1, 2, 0))
    sent["w_4"] = a["L2_conv_w3"].reshape(C, CM).T
    for n in (1, 2, 3):
        v = np.stack([a[f"L2_conv_{k}{n}"] for k in "gbmv"], 1)
        sent[f"bn{n}"] = v if n < 3 else v.reshape(KC, P, 4).transpose(1, 2, 0)
    lw = a["L3_conv_weights"]
    wide = np.zeros((C, C), lw.dtype)
    o, u = np.arange(C)[:, None], np.arange(lw.shape[1])[None, :]
    wide[(o * 32 + u) % C, np.broadcast_to(o, lw.shape)] = lw
    sent["wide"] = wide
    sent.update(constants())
    arrays, t = {}, {}
    for name, v in sent.items():
        v = np.ascontiguousarray(v)
        arrays[f"in_{name}"] = v
        t[name] = nc.dram_tensor(f"in_{name}", v.shape, _mybir.dt.from_np(v.dtype), kind="ExternalInput").ap()
    out = nc.dram_tensor("out_0", (B, C, N), F32, kind="ExternalOutput").ap()
    kernel_program(nc, t, out)
    r = _run(nc, [arrays], core_ids=[0])
    return np.asarray(r.results[0]["out_0"]).reshape(B, C, SIDE, SIDE)
```
